# Optimizing a Trainium2 kernel written in Bass

```python
import numpy as np
import jax
import jax.numpy as jnp

def _softmax(x, axis=-1):
    return jax.nn.softmax(x, axis=axis)

def _gelu(x):
    return jax.nn.gelu(x, approximate=True)

def _silu(x):
    return jax.nn.silu(x)

def _sigmoid(x):
    return jax.nn.sigmoid(x)

def _layernorm(x, axis=-1, eps=1e-05):
    m = jnp.mean(x, axis=axis, keepdims=True)
    v = jnp.var(x, axis=axis, keepdims=True)
    return (x - m) / jnp.sqrt(v + eps)

def _scatter_add(tgt, idx, src, axis=0):
    return tgt.at[idx].add(src)

def _segment_sum(src, seg, n):
    return jax.ops.segment_sum(src, seg, n)
kernel_name = 'mk_adj_preln_d4_adj_r2_8ca995'

def setup_inputs(seed: int=0):
    np.random.seed(seed)
    _w = jnp.asarray

    def _rec_inputs():
        import jax
        import jax.numpy as jnp
        _gk = jax.random.key(seed)
        x = -0.000929 + 1 * jax.random.normal(jax.random.fold_in(_gk, 1), (3327, 256), jnp.float32)
        _a = jax.random.bernoulli(jax.random.fold_in(_gk, 2), 0.00480914, (3327, 3327))
        _a = jnp.logical_or(_a, jnp.swapaxes(_a, -1, -2))
        _a = jnp.logical_or(_a, jnp.eye(3327, dtype=bool))
        adj = _a.astype(jnp.int32)
        return (x, adj)
    x, adj = _rec_inputs()

    def _L0_gnn_setup():
        import jax, jax.numpy as jnp
        import numpy as np
        N_NODES = 1024
        IN_FEATURES = 256
        OUT_FEATURES = 256
        N_HEADS = 8
        N_HIDDEN = OUT_FEATURES // N_HEADS
        NEG_SLOPE = 0.2
        key = jax.random.key(seed)
        k_h, k_adj, k_w, k_a = jax.random.split(key, 4)
        h = jax.random.normal(k_h, (N_NODES, IN_FEATURES), dtype=jnp.float32)
        adj_mat = jax.random.randint(k_adj, (N_NODES, N_NODES), 0, 2, dtype=jnp.int32)
        bound = 1.0 / np.sqrt(IN_FEATURES)
        W_lin = jax.random.uniform(k_w, (N_HEADS * N_HIDDEN, IN_FEATURES), jnp.float32, -bound, bound)
        bound_a = 1.0 / np.sqrt(2 * N_HIDDEN)
        attn_w = jax.random.uniform(k_a, (2 * N_HIDDEN,), jnp.float32, -bound_a, bound_a)
        return {'h': h, 'adj_mat': adj_mat, 'W_lin': W_lin, 'attn_w': attn_w}
    _L0_gnn_all = _L0_gnn_setup()
    _L0_gnn_in = {k: v for k, v in _L0_gnn_all.items() if k in ('W_lin', 'attn_w')}
    del _L0_gnn_all

    def _L1_gnn_setup():
        import jax, jax.numpy as jnp
        import numpy as np
        EPS = 1e-08
        key = jax.random.key(seed)
        k1, k2, k3 = jax.random.split(key, 3)
        N, IN_DIM, OUT_DIM = (4096, 256, 256)
        h = jax.random.normal(k1, (N, IN_DIM), dtype=jnp.float32)
        adj = jax.random.randint(k2, (N, N), 0, 2, dtype=jnp.int32)
        W = jax.random.normal(k3, (OUT_DIM, IN_DIM), dtype=jnp.float32) * (1.0 / np.sqrt(IN_DIM))
        return {'h': h, 'adj': adj, 'W': W}
    _L1_gnn_all = _L1_gnn_setup()
    _L1_gnn_in = {k: v for k, v in _L1_gnn_all.items() if k in ('W',)}
    del _L1_gnn_all

    def _L2_gnn_setup():
        import jax, jax.numpy as jnp
        import numpy as np
        N = 2048
        IN_FEAT = 256
        EMBED = 256
        HEADS = 8
        HEAD_DIM = EMBED // HEADS
        SCALING = HEAD_DIM ** (-0.5)
        key = jax.random.key(seed)
        ks = jax.random.split(key, 7)
        x = jax.random.normal(ks[0], (N, IN_FEAT), dtype=jnp.float32)
        adj = jax.random.randint(ks[1], (N, N), 0, 2, dtype=jnp.int32)
        s = 0.04
        WQ = jax.random.normal(ks[2], (EMBED, IN_FEAT), dtype=jnp.float32) * s
        WK = jax.random.normal(ks[3], (EMBED, IN_FEAT), dtype=jnp.float32) * s
        WV = jax.random.normal(ks[4], (EMBED, IN_FEAT), dtype=jnp.float32) * s
        we = jax.random.normal(ks[5], (1, HEAD_DIM), dtype=jnp.float32) * 0.1
        be = jnp.zeros((1,), dtype=jnp.float32)
        return {'x': x, 'adj': adj, 'WQ': WQ, 'WK': WK, 'WV': WV, 'we': we, 'be': be}
    _L2_gnn_all = _L2_gnn_setup()
    _L2_gnn_in = {k: v for k, v in _L2_gnn_all.items() if k in ('WQ', 'WK', 'WV', 'we', 'be')}
    del _L2_gnn_all

    def _L3_gnn_setup():
        import jax, jax.numpy as jnp
        import numpy as np
        N, D_IN, D_OUT = (4096, 256, 256)
        key = jax.random.key(seed)
        ks = jax.random.split(key, 8)
        scale_in = 1.0 / np.sqrt(D_IN)
        scale_cat = 1.0 / np.sqrt(2 * D_OUT)
        return {'x': jax.random.normal(ks[0], (N, D_IN), dtype=jnp.float32), 'adj': jax.random.randint(ks[1], (N, N), 0, 2, dtype=jnp.int32), 'W_self': jax.random.uniform(ks[2], (D_IN, D_OUT), jnp.float32, -scale_in, scale_in), 'b_self': jax.random.uniform(ks[3], (D_OUT,), jnp.float32, -scale_in, scale_in), 'W_nb': jax.random.uniform(ks[4], (D_IN, D_OUT), jnp.float32, -scale_in, scale_in), 'b_nb': jax.random.uniform(ks[5], (D_OUT,), jnp.float32, -scale_in, scale_in), 'W_comb': jax.random.uniform(ks[6], (2 * D_OUT, D_OUT), jnp.float32, -scale_cat, scale_cat), 'b_comb': jax.random.uniform(ks[7], (D_OUT,), jnp.float32, -scale_cat, scale_cat)}
    _L3_gnn_all = _L3_gnn_setup()
    _L3_gnn_in = {k: v for k, v in _L3_gnn_all.items() if k in ('W_self', 'b_self', 'W_nb', 'b_nb', 'W_comb', 'b_comb')}
    del _L3_gnn_all
    return {'x': x, 'adj': adj, 'L0_gnn_W_lin': _L0_gnn_in['W_lin'], 'L0_gnn_attn_w': _L0_gnn_in['attn_w'], 'L1_gnn_W': _L1_gnn_in['W'], 'L2_gnn_WQ': _L2_gnn_in['WQ'], 'L2_gnn_WK': _L2_gnn_in['WK'], 'L2_gnn_WV': _L2_gnn_in['WV'], 'L2_gnn_we': _L2_gnn_in['we'], 'L2_gnn_be': _L2_gnn_in['be'], 'L3_gnn_W_self': _L3_gnn_in['W_self'], 'L3_gnn_b_self': _L3_gnn_in['b_self'], 'L3_gnn_W_nb': _L3_gnn_in['W_nb'], 'L3_gnn_b_nb': _L3_gnn_in['b_nb'], 'L3_gnn_W_comb': _L3_gnn_in['W_comb'], 'L3_gnn_b_comb': _L3_gnn_in['b_comb']}

def reference(x, adj, L0_gnn_W_lin, L0_gnn_attn_w, L1_gnn_W, L2_gnn_WQ, L2_gnn_WK, L2_gnn_WV, L2_gnn_we, L2_gnn_be, L3_gnn_W_self, L3_gnn_b_self, L3_gnn_W_nb, L3_gnn_b_nb, L3_gnn_W_comb, L3_gnn_b_comb):
    import jax
    import jax.numpy as jnp

    def _L0_gnn_ref(h, adj_mat, W_lin, attn_w):
        import jax, jax.numpy as jnp
        import numpy as np
        N_NODES = 1024
        IN_FEATURES = 256
        OUT_FEATURES = 256
        N_HEADS = 8
        N_HIDDEN = OUT_FEATURES // N_HEADS
        NEG_SLOPE = 0.2
        n = h.shape[0]
        g = (h @ W_lin.T).reshape(n, N_HEADS, N_HIDDEN)
        a_l, a_r = (attn_w[:N_HIDDEN], attn_w[N_HIDDEN:])
        el = jnp.einsum('nhd,d->nh', g, a_l)
        er = jnp.einsum('nhd,d->nh', g, a_r)
        e = el[:, None, :] + er[None, :, :]
        e = jnp.where(e >= 0, e, NEG_SLOPE * e)
        mask = (adj_mat == 0)[:, :, None]
        e = jnp.where(mask, -jnp.inf, e)
        a = jax.nn.softmax(e, axis=1)
        attn_res = jnp.einsum('ijh,jhf->ihf', a, g)
        return attn_res.reshape(n, N_HEADS * N_HIDDEN)

    def _L1_gnn_ref(h, adj, W):
        import jax, jax.numpy as jnp
        import numpy as np
        EPS = 1e-08
        Wh = h @ W.T
        N = Wh.shape[0]
        norms = jnp.linalg.norm(Wh, axis=1, keepdims=True)
        sim = Wh @ Wh.T / (norms * norms.T + EPS)
        mask = (adj > 0) | jnp.eye(N, dtype=bool)
        sim_masked = jnp.where(mask, sim, -jnp.inf)
        alpha = jax.nn.softmax(sim_masked, axis=1)
        return alpha @ Wh

    def _L2_gnn_ref(x, adj, WQ, WK, WV, we, be):
        import jax, jax.numpy as jnp
        import numpy as np
        N = 2048
        IN_FEAT = 256
        EMBED = 256
        HEADS = 8
        HEAD_DIM = EMBED // HEADS
        SCALING = HEAD_DIM ** (-0.5)
        n = x.shape[0]
        Q = (x @ WQ.T).reshape(n, HEADS, HEAD_DIM).transpose(1, 0, 2)
        K = (x @ WK.T).reshape(n, HEADS, HEAD_DIM).transpose(1, 0, 2)
        V = (x @ WV.T).reshape(n, HEADS, HEAD_DIM).transpose(1, 0, 2)
        energy = Q @ we.T + be
        attn = jnp.einsum('hqd,hkd->hqk', Q, K) * SCALING + energy
        attn = attn + jnp.where(adj > 0, 0.0, -jnp.inf)
        attn = jax.nn.softmax(attn, axis=-1)
        hard = (attn == jnp.max(attn, axis=-1, keepdims=True)).astype(jnp.float32) / HEADS
        out = jnp.einsum('hqk,hkd->hqd', hard, V)
        return out.transpose(1, 0, 2).reshape(n, EMBED)

    def _L3_gnn_ref(x, adj, W_self, b_self, W_nb, b_nb, W_comb, b_comb):
        import jax, jax.numpy as jnp
        import numpy as np
        N, D_IN, D_OUT = (4096, 256, 256)
        mask = (adj > 0).astype(x.dtype)
        deg = jnp.sum(mask, axis=1, keepdims=True)
        agg = mask @ x / jnp.maximum(deg, 1.0)
        self_f = x @ W_self + b_self
        nb_f = agg @ W_nb + b_nb
        combined = jnp.concatenate([self_f, nb_f], axis=-1)
        out = combined @ W_comb + b_comb
        return jax.nn.relu(out)
    h = jnp.maximum(_layernorm(x, axis=-1), 0.0)
    x = x + _L0_gnn_ref(h, adj, L0_gnn_W_lin, L0_gnn_attn_w)
    h = jnp.maximum(_layernorm(x, axis=-1), 0.0)
    x = x + _L1_gnn_ref(h, adj, L1_gnn_W)
    h = jnp.maximum(_layernorm(x, axis=-1), 0.0)
    x = x + _L2_gnn_ref(h, adj, L2_gnn_WQ, L2_gnn_WK, L2_gnn_WV, L2_gnn_we, L2_gnn_be)
    h = jnp.maximum(_layernorm(x, axis=-1), 0.0)
    x = x + _L3_gnn_ref(h, adj, L3_gnn_W_self, L3_gnn_b_self, L3_gnn_W_nb, L3_gnn_b_nb, L3_gnn_W_comb, L3_gnn_b_comb)
    return x

_drawn_inputs = setup_inputs


def setup_inputs(seed=0):
    import zlib

    import numpy as np

    out = dict(_drawn_inputs(seed))
    spreads = {}
    factors = {'L0_gnn_attn_w': 6.247, 'L3_gnn_b_self': 7.14, 'L3_gnn_b_nb': 6.13, 'L3_gnn_b_comb': 3.664}
    for name, (base, spread) in spreads.items():
        noise = np.random.default_rng([zlib.crc32(name.encode()), seed]).standard_normal(out[name].shape)
        drawn = base * np.exp(spread * noise) if base else spread * noise
        out[name] = jnp.asarray(drawn.astype(out[name].dtype))
    for name, factor in factors.items():
        out[name] = (out[name] * factor).astype(out[name].dtype)
    return out
```

```python
from contextlib import ExitStack

import concourse.bass as bass
from concourse import mybir

F32 = mybir.dt.float32
F16 = mybir.dt.float16
BF16 = mybir.dt.bfloat16
FP8 = mybir.dt.float8e4
I32 = mybir.dt.int32
U16 = mybir.dt.uint16
U8 = mybir.dt.uint8
ALU = mybir.AluOpType
ACT = mybir.ActivationFunctionType
AX = mybir.AxisListType

N = 3327
P = 128
NT = -(-N // P)
NP = NT * P
LAST = N - (NT - 1) * P
D = 256
KC = D // P
HEADS = 8
HD = D // HEADS
LN_EPS = 1e-5
SLOPE = 0.2
NORM_EPS = 1e-8
HSC = 256.0
WSC = 1024.0
PSC = HSC * WSC
FP8_ONE = 0x38
CH = 512
CHUNKS = [(c, min(CH, NP - c)) for c in range(0, NP, CH)]


def hi_lo_products(pairs):
    return [(kc, a, b) for kc in range(pairs) for a, b in ((0, 0), (0, 1), (1, 0))]


class Kernel:

    def __init__(self, nc):
        self.nc = nc
        self.layer_sems = []
        self.s_settled = nc.alloc_semaphore(name="s_settled")

    def sem(self, name):
        self.layer_sems.append(self.nc.alloc_semaphore(name=name))
        return self.layer_sems[-1]

    def end_layer(self):
        self.nc.all_engine_barrier()
        self.nc.clear_and_free_semaphores(self.layer_sems)
        self.nc.all_engine_barrier()
        self.layer_sems = []

    def settle(self, eng):
        eng.sem_inc(self.s_settled, 1)

    def sb(self, ctx, name, shape, dt):
        return ctx.enter_context(self.nc.sbuf_tensor(name, shape, dt))

    def ps(self, ctx, name, shape, dt=F32):
        return ctx.enter_context(self.nc.psum_tensor(name, shape, dt))

    def dram(self, name, shape, dt):
        return self.nc.dram_tensor(name, shape, dt, kind="Internal").ap()


def setup_constants(k, x_dram):
    nc = k.nc
    s_x, s_zero, s_ones, s_id = (k.sem(n) for n in ("s_x", "s_x_zero", "s_const_ones", "s_identity"))
    with ExitStack() as c:
        ones = k.sb(c, "ones_pp", [P, P], F32)
        corner = k.sb(c, "corner_f", [P, P], F32)
        block = c.enter_context(nc.Block())

        @block.sync
        def _(sp):
            sp.dma_start(k.X[:, 0:NT - 1, :], x_dram[0:(NT - 1) * P, :].rearrange("(t p) d -> p t d", p=P)).then_inc(s_x, 16)
            sp.wait_ge(s_zero, 1)
            sp.dma_start(k.X[0:LAST, NT - 1, :], x_dram[(NT - 1) * P:N, :]).then_inc(s_x, 16)
            sp.wait_ge(s_x, 32)

        @block.vector
        def _(dve):
            nc.vector.memset(k.X[:, NT - 1, :], 0.0).then_inc(s_zero, 1)
            nc.vector.memset(ones[:], 1.0).then_inc(s_ones, 1)
            dve.wait_ge(s_id, 2)
            nc.vector.tensor_copy(k.ident16[:], k.ident[:])
            nc.vector.tensor_copy(k.corner16[:], corner[:])

        @block.gpsimd
        def _(pool):
            pool.wait_ge(s_ones, 1)
            nc.gpsimd.affine_select(out=k.ident[:], in_=ones[:], compare_op=ALU.is_equal, fill=0.0, base=0,
                                    pattern=[[-1, P]], channel_multiplier=1).then_inc(s_id, 1)
            nc.gpsimd.affine_select(out=corner[:], in_=ones[:], compare_op=ALU.is_equal, fill=0.0, base=-2 * (P - 1),
                                    pattern=[[1, P]], channel_multiplier=1).then_inc(s_id, 1)


def transpose_adjacency(k, adj_dram):
    nc = k.nc
    s_rows = [k.sem(f"s_adj_rows{s}") for s in range(2)]
    s_used, s_corner, s_tr, s_evac, s_pad = (
        k.sem(n) for n in ("s_adj_used", "s_corner", "s_adj_tr", "s_adj_evac", "s_adj_pad"))
    STEPS = NT // 2 - 1
    with ExitStack() as c:
        rows = k.sb(c, "adj_rows", [P, 2, NP], I32)
        a16 = k.sb(c, "adj16", [P, 2, NP], BF16)
        tr = k.ps(c, "adj_tr", [P, 2, 4 * 1024], BF16)
        block = c.enter_context(nc.Block())

        def rows_of(t):
            return adj_dram[bass.ds(t * P, P), :]

        @block.sync
        def _(sp):
            sp.wait_ge(s_pad, 1)
            sp.dma_start(rows[:, 0, 0:N], adj_dram[0:P, :]).then_inc(s_rows[0], 16)
            sp.dma_start(rows[:, 1, 0:N], adj_dram[P:2 * P, :]).then_inc(s_rows[1], 16)
            with sp.Fori(0, STEPS - 1) as i:
                for s in range(2):
                    sp.wait_ge(s_used, 2 * i + s + 1)
                    sp.dma_start(rows[:, s, 0:N], adj_dram[bass.ds(i * (2 * P) + (s + 2) * P, P), :]).then_inc(s_rows[s], 16)
            sp.wait_ge(s_used, NT - 3)
            sp.dma_start(rows[:, 0, 0:N], adj_dram[(NT - 2) * P:(NT - 1) * P, :]).then_inc(s_rows[0], 16)
            sp.wait_ge(s_pad, 2)
            sp.dma_start(rows[0:LAST, 1, 0:N], adj_dram[(NT - 1) * P:N, :]).then_inc(s_rows[1], 16)

        @block.gpsimd
        def _(pool):
            nc.gpsimd.memset(rows[:, :, N:NP], 0).then_inc(s_pad, 1)
            pool.wait_ge(s_used, NT - 2)
            nc.gpsimd.memset(rows[96:P, 1, :], 0).then_inc(s_pad, 1)

        @block.scalar
        def _(act):
            def convert(t, s, step):
                act.wait_ge(s_rows[s], 16 * (step + 1))
                act.wait_ge(s_tr, t + 1)
                nc.scalar.activation(a16[:, s, :], rows[:, s, :], ACT.Copy,
                                     accum_out=k.deg[:, bass.ds(t, 1)]).then_inc(s_used, 1)

            act.wait_ge(s_pad, 1)
            with act.Fori(0, STEPS) as i:
                for s in range(2):
                    convert(2 * i + s, s, i)
            convert(NT - 2, 0, STEPS)
            act.wait_ge(s_pad, 2)
            convert(NT - 1, 1, STEPS)

        @block.tensor
        def _(pe):
            pe.sem_inc(s_tr, 2)

            def transpose(t, s):
                if not isinstance(t, int) or t < NT - 1:
                    pe.wait_ge(s_used, t + 1)
                else:
                    pe.wait_ge(s_corner, 1)
                pe.wait_ge(s_evac, t + 1)
                for jt in range(NT):
                    last = nc.tensor.transpose(tr[:, s, jt * P:(jt + 1) * P], a16[:, s, jt * P:(jt + 1) * P], k.ident16[:])
                last.then_inc(s_tr, 1)

            with pe.Fori(0, STEPS) as i:
                for s in range(2):
                    transpose(2 * i + s, s)
            transpose(NT - 2, 0)
            transpose(NT - 1, 1)

        @block.vector
        def _(dve):
            dve.sem_inc(s_evac, 2)

            def evacuate(t, s):
                dve.wait_ge(s_tr, t + 3)
                nc.vector.tensor_scalar(k.adjT[:, bass.ds(t, 1), :, :].rearrange("p t j i -> p (t j i)").bitcast(U8),
                                        tr[:, s, 0:NP], float(FP8_ONE), None, ALU.mult).then_inc(s_evac, 1)

            with dve.Fori(0, STEPS) as i:
                for s in range(2):
                    evacuate(2 * i + s, s)
            dve.wait_ge(s_used, NT)
            nc.vector.tensor_tensor(a16[:, 1, NP - P:NP], a16[:, 1, NP - P:NP], k.corner16[:], ALU.add).then_inc(s_corner, 1)
            evacuate(NT - 2, 0)
            evacuate(NT - 1, 1)


def normalise(k, tag, hT, weights, h_nat=None):
    nc = k.nc
    s_w, s_stat, s_sq, s_sm, s_h, s_tr, s_hi, s_lo = (
        k.sem(f"s_{tag}_{n}") for n in ("w", "stat", "sqrt", "small", "h", "tr", "hi", "lo"))
    slots = [(g, kc) for g in range(-(-NT // 4)) for kc in range(KC)]
    NB = 4
    with ExitStack() as c:
        H = k.sb(c, f"{tag}_h", [P, NT, D], F32)
        stats = k.sb(c, f"{tag}_stats", [P, NT, 6], F32)
        mv = k.sb(c, f"{tag}_mv", [P, NT, 2], F32)
        sm = k.sb(c, f"{tag}_sm", [P, 6, NT], F32)
        ve, rt, rs, t1, t2, nb = (sm[:, i, :] for i in range(6))
        raw = k.sb(c, f"{tag}_wraw", [P, max(1, len(weights)), 2, D], F32)
        pt = k.ps(c, f"{tag}_pt", [P, NB, CH])
        block = c.enter_context(nc.Block())
        nw = len(weights)

        @block.sync
        def _(sp):
            for i, (w, _) in enumerate(weights):
                sp.dma_start(raw[:, i, :, :], w.rearrange("(k p) c -> p k c", p=P)).then_inc(s_w, 16)

        @block.vector
        def _(dve):
            for t in range(NT):
                nc.vector.bn_stats(stats[:, t, :], k.X[:, t, :]).then_inc(s_stat, 1)
            for t in range(NT):
                dve.wait_ge(s_stat, t + 1)
                last = nc.vector.bn_aggr(mv[:, t, :], stats[:, t, :])
            last.then_inc(s_sm, 1)
            dve.wait_ge(s_sm, 1)
            nc.vector.tensor_scalar(ve, mv[:, :, 1], LN_EPS, None, ALU.add).then_inc(s_sm, 1)
            dve.wait_ge(s_sq, 1)
            nc.vector.reciprocal(rs, rt).then_inc(s_sm, 1)
            dve.wait_ge(s_sm, 3)
            nc.vector.tensor_tensor(t1, rs, rs, ALU.mult).then_inc(s_sm, 1)
            dve.wait_ge(s_sm, 4)
            nc.vector.tensor_tensor(t2, t1, ve, ALU.mult).then_inc(s_sm, 1)
            dve.wait_ge(s_sm, 5)
            nc.vector.tensor_scalar(t1, t2, -0.5, 1.5, ALU.mult, ALU.add).then_inc(s_sm, 1)
            dve.wait_ge(s_sm, 6)
            nc.vector.tensor_tensor(rt, t1, rs, ALU.mult).then_inc(s_sm, 1)
            dve.wait_ge(s_sm, 7)
            nc.vector.scalar_tensor_tensor(nb, mv[:, :, 0], -1.0, rt, ALU.mult, ALU.mult).then_inc(s_sm, 1)
            for i in range(nw):
                dve.wait_ge(s_hi, i + 1)
                wt = weights[i][1]
                nc.vector.scalar_tensor_tensor(wt(1), pt[:, i % NB, :].rearrange("p (k n) -> p k n", k=KC), WSC, wt(0),
                                               ALU.mult, ALU.subtract).then_inc(s_lo, 1)
            for j, (g, kc) in enumerate(slots):
                n0, n1 = g * CH, min(NP, (g + 1) * CH)
                dve.wait_ge(s_hi, nw + j + 1)
                nc.vector.scalar_tensor_tensor(hT[:, 1, kc, n0:n1], pt[:, (nw + j) % NB, 0:n1 - n0], HSC, hT[:, 0, kc, n0:n1],
                                               ALU.mult, ALU.subtract).then_inc(s_lo, 1)
            if h_nat is not None:
                dve.wait_ge(s_hi, nw + len(slots) + 1)
                nc.vector.scalar_tensor_tensor(h_nat[:, 1, :, :].rearrange("p t d -> p (t d)"), H[:].rearrange("p t d -> p (t d)"),
                                               HSC, h_nat[:, 0, :, :].rearrange("p t d -> p (t d)"), ALU.mult, ALU.subtract)

        @block.scalar
        def _(act):
            act.wait_ge(s_sm, 2)
            nc.scalar.activation(rt, ve, ACT.Sqrt).then_inc(s_sq, 1)
            for i in range(nw):
                act.wait_ge(s_tr, i + 1)
                nc.scalar.activation(weights[i][1](0), pt[:, i % NB, :].rearrange("p (k n) -> p k n", k=KC), ACT.Copy,
                                     scale=WSC).then_inc(s_hi, 1)
            act.wait_ge(s_sm, 8)

            def relu(t):
                nc.scalar.activation(H[:, t, :], k.X[:, t, :], ACT.Relu, scale=rt[:, t:t + 1], bias=nb[:, t:t + 1]).then_inc(s_h, 1)

            def high(j):
                g, kc = slots[j]
                n0, n1 = g * CH, min(NP, (g + 1) * CH)
                act.wait_ge(s_tr, nw + j + 1)
                nc.scalar.activation(hT[:, 0, kc, n0:n1], pt[:, (nw + j) % NB, 0:n1 - n0], ACT.Copy, scale=HSC).then_inc(s_hi, 1)

            for t in range(4):
                relu(t)
            for g in range(-(-NT // 4)):
                for t in range(4 * g + 4, min(4 * g + 8, NT)):
                    relu(t)
                high(2 * g)
                high(2 * g + 1)
            if h_nat is not None:
                act.wait_ge(s_h, NT)
                nc.scalar.activation(h_nat[:, 0, :, :].rearrange("p t d -> p (t d)"), H[:].rearrange("p t d -> p (t d)"),
                                     ACT.Copy, scale=HSC).then_inc(s_hi, 1)

        @block.tensor
        def _(pe):
            for i in range(nw):
                pe.wait_ge(s_w, 16 * nw)
                if i >= NB:
                    pe.wait_ge(s_lo, i - NB + 1)
                for kc in range(KC):
                    for kn in range(2):
                        last = nc.tensor.transpose(pt[:, i % NB, kc * D + kn * P:kc * D + (kn + 1) * P],
                                                   raw[:, i, kn, kc * P:(kc + 1) * P], k.ident[:])
                last.then_inc(s_tr, 1)
            for j, (g, kc) in enumerate(slots):
                tiles = range(4 * g, min(4 * g + 4, NT))
                pe.wait_ge(s_h, tiles[-1] + 1)
                if nw + j >= NB:
                    pe.wait_ge(s_lo, nw + j - NB + 1)
                for t in tiles:
                    last = nc.tensor.transpose(pt[:, (nw + j) % NB, (t % 4) * P:(t % 4 + 1) * P],
                                               H[:, t, kc * P:(kc + 1) * P], k.ident[:])
                last.then_inc(s_tr, 1)



G1 = HD + 1
VSC = 2048.0
STEP = 2.0 ** 60


def gat_project(k, hT, w, attn_w, el_dram, GE):
    nc = k.nc
    s_z, s_aw, s_wa, s_wahi, s_walo, s_g, s_ge, s_elp, s_elt = (
        k.sem(f"s_g0_{n}") for n in ("z", "aw", "wa", "wahi", "walo", "g", "ge", "elp", "elt"))
    s_out = [k.sem(f"s_g0_elout{i}") for i in range(2)]
    NB = 4
    prods = hi_lo_products(KC)
    with ExitStack() as c:
        raw = k.sb(c, "g0_wraw", [P, 2, D], F32)
        ad = k.sb(c, "g0_ad", [P, 2, 2 * HEADS], F32)
        elT = k.sb(c, "g0_elT", [HEADS, 2, CH], F32)
        pg = k.ps(c, "g0_pg", [P, NB, CH])
        pel = k.ps(c, "g0_pel", [HEADS, 2, CH])
        block = c.enter_context(nc.Block())

        @block.sync
        def _(sp):
            sp.wait_ge(s_z, 1)
            for h in range(HEADS):
                q, kn = h % 4, h // 4
                for side in range(2):
                    sp.dma_start(ad[HD * q:HD * q + HD, kn, side * HEADS + h:side * HEADS + h + 1],
                                 attn_w[side * HD:(side + 1) * HD].rearrange("(p o) -> p o", o=1)).then_inc(s_aw, 16)
            sp.dma_start(raw[:], k.w_lin.rearrange("(k p) c -> p k c", p=P)).then_inc(s_aw, 16)
            for m, (c0, cn) in enumerate(CHUNKS):
                sp.wait_ge(s_elt, m + 1)
                sp.dma_start(el_dram[:, c0:c0 + cn], elT[:, m % 2, 0:cn]).then_inc(s_out[m % 2], 16)
            for i in range(2):
                sp.wait_ge(s_out[i], 16 * len(range(i, len(CHUNKS), 2)))

        @block.vector
        def _(dve):
            nc.vector.memset(ad[:], 0.0).then_inc(s_z, 1)
            dve.wait_ge(s_wahi, 1)
            nc.vector.scalar_tensor_tensor(w[:, 1, :, D:D + 16], pg[:, 0, 0:32].rearrange("p (k n) -> p k n", k=KC), WSC,
                                           w[:, 0, :, D:D + 16], ALU.mult, ALU.subtract).then_inc(s_walo, 1)

        @block.tensor
        def _(pe):
            pe.wait_ge(s_aw, 17 * 16)
            for kc in range(KC):
                for kn in range(2):
                    last = nc.tensor.matmul(pg[:, 0, kc * 16:kc * 16 + 16], raw[:, kn, kc * P:(kc + 1) * P], ad[:, kn, :],
                                            start=(kn == 0), stop=(kn == 1))
            last.then_inc(s_wa, 1)
            pe.wait_ge(s_walo, 1)
            for t in range(NT):
                if t >= NB:
                    pe.wait_ge(s_ge, t - NB + 1)
                for n, (kc, a, b) in enumerate(prods):
                    last = nc.tensor.matmul(pg[:, t % NB, 0:D + 16], hT[:, a, kc, t * P:(t + 1) * P], w[:, b, kc, :],
                                            start=(n == 0), stop=(n == len(prods) - 1))
                last.then_inc(s_g, 1)
            for m, (c0, cn) in enumerate(CHUNKS):
                if m >= 2:
                    pe.wait_ge(s_elt, m - 1)
                for n, (kc, a, b) in enumerate(prods):
                    last = nc.tensor.matmul(pel[:, m % 2, 0:cn], w[:, a, kc, D:D + HEADS], hT[:, b, kc, c0:c0 + cn],
                                            start=(n == 0), stop=(n == len(prods) - 1))
                last.then_inc(s_elp, 1)

        @block.scalar
        def _(act):
            act.wait_ge(s_wa, 1)
            nc.scalar.activation(w[:, 0, :, D:D + 16], pg[:, 0, 0:32].rearrange("p (k n) -> p k n", k=KC), ACT.Copy,
                                 scale=WSC).then_inc(s_wahi, 1)
            for t in range(NT):
                act.wait_ge(s_g, t + 1)
                nc.scalar.activation(GE[:, t, :], pg[:, t % NB, 0:D + 16], ACT.Copy, scale=1.0 / PSC).then_inc(s_ge, 1)
            for m, (c0, cn) in enumerate(CHUNKS):
                act.wait_ge(s_elp, m + 1)
                if m >= 2:
                    act.wait_ge(s_out[m % 2], 16 * (m // 2))
                nc.scalar.activation(elT[:, m % 2, 0:cn], pel[:, m % 2, 0:cn], ACT.Copy, scale=1.0 / PSC).then_inc(s_elt, 1)


def gat_factors(k, adjT_dram, xv_dram, XA, HC, GE, spare):
    nc = k.nc
    s_red, s_rmax, s_fac, s_exp, s_f, s_xh, s_xl = (
        k.sem(f"s_x0_{n}") for n in ("red", "rmax", "fac", "exp", "f", "xh", "xl"))
    s_out = [k.sem(f"s_x0_out{i}") for i in range(2)]
    SL = NT * 2 * G1
    F = spare[:, 0:2 * SL].bitcast(F32).rearrange("p (s t d) -> p s t d", s=2, d=G1)
    X1 = spare[:, 2 * SL:4 * SL].rearrange("p (s t a d) -> p s t a d", s=2, a=2, d=G1)
    steps = [(f, h) for f in (1, 0) for h in range(HEADS)]
    er, el = GE[:, :, D + HEADS:D + 2 * HEADS], GE[:, :, D:D + HEADS]
    with ExitStack() as c:
        rm = k.sb(c, "x0_rm", [P, 2, HEADS], F32)
        vf = k.sb(c, "x0_vf", [P, 2, NT, HEADS], F32)
        dd = k.sb(c, "x0_dd", [P, 4, NT, HEADS], F32)
        block = c.enter_context(nc.Block())

        def split_out(n):
            f, h = steps[n]
            return X1[:, n % 2] if f else XA[:, h]

        @block.sync
        def _(sp):
            for n, (f, h) in enumerate(steps):
                sp.wait_ge(s_xl, n + 1)
                sp.dma_start(xv_dram[f, h], split_out(n).rearrange("p t a d -> p (t a d)")).then_inc(s_out[n % 2], 16)
            sp.dma_start(adjT_dram.rearrange("t p n -> p t n"), k.adjT[:].rearrange("p t j i -> p t (j i)")).then_inc(k.s_adjT_out, 16)
            for i in range(2):
                sp.wait_ge(s_out[i], 16 * len(steps) // 2)

        @block.scalar
        def _(act):
            act.wait_ge(s_fac, 1)
            nc.scalar.activation(vf[:, 1], dd[:, 0], ACT.Exp).then_inc(s_exp, 1)
            nc.scalar.activation(vf[:, 0], dd[:, 0], ACT.Exp, scale=SLOPE).then_inc(s_exp, 1)
            act.wait_ge(s_fac, 6)
            nc.scalar.activation(HC[:, :, 2, :].rearrange("p h t -> p t h"), dd[:, 1], ACT.Exp)
            nc.scalar.activation(HC[:, :, 3, :].rearrange("p h t -> p t h"), dd[:, 2], ACT.Exp)
            for n, (f, h) in enumerate(steps):
                act.wait_ge(s_f, 2 * (n + 1))
                if f and n >= 2:
                    act.wait_ge(s_out[n % 2], 16 * (n // 2))
                nc.scalar.activation(split_out(n)[:, :, 0, :], F[:, n % 2], ACT.Copy).then_inc(s_xh, 1)

        @block.gpsimd
        def _(pool):
            pool.wait_ge(s_red, 1)
            nc.gpsimd.partition_all_reduce(rm[:, 1, :], rm[:, 0, :], P, bass.bass_isa.ReduceOp.max).then_inc(s_rmax, 1)

        @block.vector
        def _(dve):
            nc.vector.tensor_reduce(rm[:, 0, :], er.rearrange("p t h -> p h t"), AX.X, ALU.max).then_inc(s_red, 1)
            nc.vector.tensor_scalar(HC[:, :, 0, :].rearrange("p h t -> p t h"), er, -1.0, None, ALU.mult)
            nc.vector.tensor_scalar(HC[:, :, 1, :].rearrange("p h t -> p t h"), er, STEP, None, ALU.mult)
            dve.wait_ge(s_rmax, 1)
            R = rm[:, 1, :].unsqueeze(1).to_broadcast([P, NT, HEADS])
            nc.vector.tensor_tensor(dd[:, 0], er, R, ALU.subtract).then_inc(s_fac, 1)
            nc.vector.tensor_tensor(dd[:, 1], el, R, ALU.add).then_inc(s_fac, 1)
            dve.wait_ge(s_fac, 2)
            nc.vector.tensor_scalar(dd[:, 2], dd[:, 1], SLOPE, None, ALU.mult).then_inc(s_fac, 1)
            dve.wait_ge(s_fac, 3)
            nc.vector.tensor_tensor(dd[:, 3], dd[:, 1], dd[:, 2], ALU.max).then_inc(s_fac, 1)
            dve.wait_ge(s_fac, 4)
            nc.vector.tensor_tensor(dd[:, 1], dd[:, 1], dd[:, 3], ALU.subtract).then_inc(s_fac, 1)
            nc.vector.tensor_tensor(dd[:, 2], dd[:, 2], dd[:, 3], ALU.subtract).then_inc(s_fac, 1)
            dve.wait_ge(s_exp, 2)
            nc.vector.tensor_scalar(vf[:], vf[:], VSC, None, ALU.mult).then_inc(s_fac, 1)
            dve.wait_ge(s_fac, 7)
            for n, (f, h) in enumerate(steps):
                if n >= 2:
                    dve.wait_ge(s_xl, n - 1)
                v = vf[:, f, :, h]
                nc.vector.tensor_tensor(F[:, n % 2, :, 0:HD], GE[:, :, h * HD:(h + 1) * HD],
                                        v.unsqueeze(2).to_broadcast([P, NT, HD]), ALU.mult).then_inc(s_f, 1)
                nc.vector.tensor_copy(F[:, n % 2, :, HD], v).then_inc(s_f, 1)
                if n >= 1:
                    dve.wait_ge(s_xh, n)
                    nc.vector.tensor_tensor(split_out(n - 1)[:, :, 1, :], F[:, (n - 1) % 2], split_out(n - 1)[:, :, 0, :],
                                            ALU.subtract).then_inc(s_xl, 1)
            n = len(steps) - 1
            dve.wait_ge(s_xh, n + 1)
            nc.vector.tensor_tensor(split_out(n)[:, :, 1, :], F[:, n % 2], split_out(n)[:, :, 0, :], ALU.subtract).then_inc(s_xl, 1)


def gat_all_edges(k, XA, SA):
    nc = k.nc
    s_in = [k.sem(f"s_a0_in{i}") for i in range(2)]
    s_mm, s_cp, s_add = (k.sem(f"s_a0_{n}") for n in ("mm", "cp", "add"))
    W = HEADS * G1
    with ExitStack() as c:
        ring = k.sb(c, "a0_ring", [P, 2, NT, P], FP8)
        hi = k.sb(c, "a0_hi", [P, 2, W], F32)
        pa = k.ps(c, "a0_pa", [P, 2, 2, CH])
        block = c.enter_context(nc.Block())

        @block.sync
        def _(sp):
            with sp.Fori(0, NT // 2) as i:
                for s in range(2):
                    sp.wait_ge(s_mm, 2 * i + s + 1)
                    sp.dma_start(ring[:, s].rearrange("p j i -> p (j i)").bitcast(U8),
                                 k.adjT[:, bass.ds(2 * i + s, 1)].rearrange("p t j i -> p (t j i)").bitcast(U8)).then_inc(s_in[s], 16)

        @block.tensor
        def _(pe):
            pe.sem_inc(s_mm, 2)
            with pe.Fori(0, NT // 2) as i:
                for s in range(2):
                    pe.wait_ge(s_add, 2 * i + s + 1)
                    pe.wait_ge(s_in[s], 16 * (i + 1))
                    k.settle(pe)
                    for jt in range(NT):
                        for part in range(2):
                            last = nc.tensor.matmul(pa[:, s, part, 0:W], ring[:, s, jt, :], XA[:, :, jt, part, :],
                                                    start=(jt == 0), stop=(jt == NT - 1))
                    last.then_inc(s_mm, 1)

        @block.scalar
        def _(act):
            with act.Fori(0, NT // 2) as i:
                for s in range(2):
                    act.wait_ge(s_mm, 2 * i + s + 3)
                    act.wait_ge(s_add, 2 * i + s + 1)
                    nc.scalar.activation(hi[:, s, :], pa[:, s, 0, 0:W], ACT.Copy).then_inc(s_cp, 1)

        @block.vector
        def _(dve):
            dve.sem_inc(s_add, 2)
            with dve.Fori(0, NT // 2) as i:
                for s in range(2):
                    dve.wait_ge(s_cp, 2 * i + s + 1)
                    nc.vector.tensor_tensor(SA[:, :, bass.ds(2 * i + s, 1), :].rearrange("p h t d -> p h (t d)"),
                                            pa[:, s, 1, 0:W].rearrange("p (h d) -> p h d", d=G1),
                                            hi[:, s, :].rearrange("p (h d) -> p h d", d=G1), ALU.add).then_inc(s_add, 1)


GROUPS = [(0, 9), (9, 9), (18, 8)]
RING = 4
ON_ACT = [jt % 8 not in (2, 5, 7) for jt in range(NT)]
COPY_AT, COMBINE_AT = 4, 9


def over_heads(eng, head):
    head(0, 0, False)
    with eng.Fori(0, HEADS // 2 - 1) as i:
        head(2 * i + 1, 1, True)
        head(2 * i + 2, 0, True)
    head(HEADS - 1, 1, True)


def gat_selected_edges(k, group, el_dram, xv_dram, SA, HC, spare):
    nc = k.nc
    g0, gn = GROUPS[group]
    cols = gn * P
    tag = f"b{group}"
    s_mm, s_sel, s_ca, s_cd, s_y, s_t, s_use = (k.sem(f"s_{tag}_{n}") for n in ("mm", "sel", "ca", "cd", "y", "t", "use"))
    s_in = [k.sem(f"s_{tag}_in{i}") for i in range(2)]
    NA, ND = sum(ON_ACT), NT - sum(ON_ACT)
    TS = 6
    W = 4 * G1
    before = lambda jt: sum(1 for x in range(jt) if ON_ACT[x] == ON_ACT[jt])
    slot = lambda p, jt: (p * NT + jt) % RING
    with ExitStack() as c:
        xb = k.sb(c, f"{tag}_x", [P, 2, 2, NT, 2 * G1], F16)
        elr = k.sb(c, f"{tag}_el", [P, 2, cols], F32)
        hc = k.sb(c, f"{tag}_hc", [P, 2, 4, NT], F32)
        C = k.sb(c, f"{tag}_C", [P, RING, cols], FP8)
        B = k.sb(c, f"{tag}_B", [P, RING, cols], FP8)
        Y = spare[:, 0:2 * 2 * gn * W].bitcast(F32).rearrange("p (s t f d) -> p s t f d", s=2, f=4, d=G1)
        S = k.sb(c, f"{tag}_S", [P, gn, 2, G1], F32)
        T = k.sb(c, f"{tag}_T", [P, gn, G1], F32)
        rd = k.sb(c, f"{tag}_rd", [P, gn], F32)
        pb = k.ps(c, f"{tag}_pb", [P, 2, 3, CH])
        block = c.enter_context(nc.Block())

        @block.sync
        def _(sp):
            sp.wait_ge(k.s_adjT_out, 16)
            with sp.Fori(0, HEADS // 2) as i:
                for p in range(2):
                    h = 2 * i + p
                    sp.wait_ge(s_use, h + 1)
                    for f in range(2):
                        sp.dma_start(xb[:, p, f].rearrange("p t n -> p (t n)"),
                                     xv_dram[f, bass.ds(h, 1)].rearrange("h p n -> p (h n)")).then_inc(s_in[p], 16)
                    sp.dma_start(elr[:, p, :], el_dram[bass.ds(h, 1), g0 * P:g0 * P + cols].to_broadcast([P, cols])).then_inc(s_in[p], 16)
                    sp.dma_start(hc[:, p].rearrange("p f t -> p (f t)"),
                                 HC[:, bass.ds(h, 1)].rearrange("p h f t -> p (h f t)")).then_inc(s_in[p], 16)

        @block.scalar
        def _(act):
            def copy_sums(h, p):
                act.wait_ge(s_mm, (h + 1) * NT + RING)
                act.wait_ge(s_t, TS * h + 1)
                for b in range(-(-gn // 3)):
                    n = min(3, gn - 3 * b)
                    last = nc.scalar.activation(Y[:, p, 3 * b:3 * b + n].rearrange("p t f d -> p (t f d)"),
                                                pb[:, p, b, 0:n * W], ACT.Copy)
                last.then_inc(s_y, 1)

            def head(h, p, previous):
                act.wait_ge(s_in[p], 32 * (h - p) + 64)
                for jt in range(NT):
                    if jt == COPY_AT and previous:
                        copy_sums(h - 1, 1 - p)
                    if ON_ACT[jt]:
                        act.wait_ge(s_sel, h * NT + jt + 1)
                        k.settle(act)
                        nc.scalar.activation(C[:, slot(p, jt), :], elr[:, p, :], ACT.Sigmoid, bias=hc[:, p, 1, jt:jt + 1],
                                             scale=STEP, saturate=False).then_inc(s_ca, 1)

            act.sem_inc(s_y, 2)
            over_heads(act, head)
            copy_sums(HEADS - 1, 1)

        @block.vector
        def _(dve):
            def combine(h, p):
                v = TS * h + 2 * TS
                u, u1 = (hc[:, p, f, g0:g0 + gn].unsqueeze(2).to_broadcast([P, gn, G1]) for f in (2, 3))
                dve.wait_ge(s_y, h + 3)
                for f in range(2):
                    last = nc.vector.tensor_tensor(S[:, :, f, :], Y[:, p, :, 2 * f, :], Y[:, p, :, 2 * f + 1, :], ALU.add)
                last.then_inc(s_t, 1)
                dve.wait_ge(s_t, v + 1)
                nc.vector.tensor_tensor(T[:], SA[:, bass.ds(h, 1), g0:g0 + gn, :].rearrange("p h t d -> p (h t) d"),
                                        S[:, :, 0, :], ALU.subtract)
                nc.vector.tensor_tensor(S[:, :, 1, :], S[:, :, 1, :], u, ALU.mult).then_inc(s_t, 1)
                dve.wait_ge(s_t, v + 2)
                nc.vector.tensor_tensor(T[:], T[:], u1, ALU.mult).then_inc(s_t, 1)
                dve.wait_ge(s_t, v + 3)
                nc.vector.tensor_tensor(S[:, :, 0, :], T[:], S[:, :, 1, :], ALU.add).then_inc(s_t, 1)
                dve.wait_ge(s_t, v + 4)
                nc.vector.reciprocal(rd[:], S[:, :, 0, HD]).then_inc(s_t, 1)
                dve.wait_ge(s_t, v + 5)
                nc.vector.tensor_tensor(T[:, :, 0:HD], S[:, :, 0, 0:HD], rd[:].unsqueeze(2).to_broadcast([P, gn, HD]),
                                        ALU.mult).then_inc(s_t, 1)
                dve.wait_ge(s_t, v + 6)
                xs = k.X[:, g0:g0 + gn, bass.ds(h * HD, HD)]
                nc.vector.tensor_tensor(xs, xs, T[:, :, 0:HD], ALU.add).then_inc(s_use, 1)

            def head(h, p, previous):
                dve.wait_ge(s_in[p], 32 * (h - p) + 64)
                for jt in range(NT):
                    if jt == COMBINE_AT and previous:
                        combine(h - 1, 1 - p)
                    sl = slot(p, jt)
                    if not ON_ACT[jt]:
                        dve.wait_ge(s_sel, h * NT + jt + 1)
                        nc.vector.tensor_scalar(C[:, sl, :].bitcast(U8), elr[:, p, :], hc[:, p, 0, jt:jt + 1], float(FP8_ONE),
                                                ALU.is_gt, ALU.mult).then_inc(s_cd, 1)
                        dve.wait_ge(s_cd, h * ND + before(jt) + 1)
                    else:
                        dve.wait_ge(s_ca, h * NA + before(jt) + 1)
                    dve.wait_ge(s_mm, h * NT + jt + 1)
                    nc.vector.tensor_tensor(B[:, sl, :].bitcast(I32).rearrange("p (t w) -> p t w", t=gn),
                                            C[:, sl, :].bitcast(I32).rearrange("p (t w) -> p t w", t=gn),
                                            k.adjT[:, g0:g0 + gn, jt, :].bitcast(I32), ALU.bitwise_and).then_inc(s_sel, 1)

            dve.sem_inc(s_use, 2)
            dve.sem_inc(s_t, 2 * TS)
            dve.sem_inc(s_sel, RING)
            over_heads(dve, head)
            combine(HEADS - 1, 1)

        @block.tensor
        def _(pe):
            pe.sem_inc(s_mm, RING)
            with pe.Fori(0, HEADS // 2) as i:
                for p in range(2):
                    h = 2 * i + p
                    pe.wait_ge(s_in[p], 64 * i + 64)
                    pe.wait_ge(s_y, h + 1)
                    for jt in range(NT):
                        pe.wait_ge(s_sel, h * NT + jt + 1 + RING)
                        k.settle(pe)
                        for t in range(gn):
                            b, r = t // 3, t % 3
                            last = nc.tensor.matmul(pb[:, p, b, r * W:(r + 1) * W], B[:, slot(p, jt), t * P:(t + 1) * P],
                                                    xb[:, p, :, jt, :], start=(jt == 0 and r == 0), stop=(jt == NT - 1),
                                                    skip_group_check=True)
                        last.then_inc(s_mm, 1)


def layer0(k, ap, adjT_dram):
    nc = k.nc
    el_dram = k.dram("el_dram", (HEADS, NP), F32)
    xv_dram = k.dram("xv_dram", (2, HEADS, P, NT * 2 * G1), F16)
    k.w_lin = ap["L0_gnn_W_lin"]
    with ExitStack() as c:
        HC = k.sb(c, "HC", [P, HEADS, 4, NT], F32)
        XA_flat = k.sb(c, "XA", [P, HEADS * NT * 2 * G1], F16)
        XA = XA_flat[:].rearrange("p (h t a d) -> p h t a d", h=HEADS, t=NT, a=2)
        with ExitStack() as c1:
            w = k.sb(c1, "w_gat", [P, 2, KC, D + 16], F16)
            hT = k.sb(c1, "hT0", [P, 2 * KC * NP], F16)
            hTv = hT[:].rearrange("p (a k n) -> p a k n", a=2, k=KC)
            normalise(k, "n0", hTv, [(ap["L0_gnn_W_lin"], lambda part: w[:, part, :, 0:D])])
            with ExitStack() as c2:
                GE = k.sb(c2, "GE", [P, NT, D + 16], F32)
                gat_project(k, hTv, w, ap["L0_gnn_attn_w"], el_dram, GE)
                gat_factors(k, adjT_dram, xv_dram, XA, HC, GE, hT[:])
        SA = k.sb(c, "SA", [P, HEADS, NT, G1], F32)
        gat_all_edges(k, XA, SA)
        for group in range(len(GROUPS)):
            gat_selected_edges(k, group, el_dram, xv_dram, SA, HC, XA_flat[:])



R_MIN = 1e-13
WHSC = 64.0
NSC = 4096.0
ESHIFT = 5.5
CT = 2
CW = CT * P
NC = NT // CT


def prior_use(idx, ring, per):
    return idx - ring + 1 + per if idx >= ring else max(j for j in range(per) if j % ring == idx) + 1


def over_chunks(eng, chunk):
    with eng.Fori(0, NC // 2) as i:
        chunk(2 * i, 0, False)
        chunk(2 * i + 1, 1, False)
    chunk(NC - 1, 0, True)


def step_ahead(c, q, jp, d, last):
    if jp + d < NC:
        return c, q, jp + d
    return None if last else (c + 1, 1 - q, jp + d - NC)


def cosine_project(k, hT, w, WnT, WHhi, WHlo, rcol, r_dram):
    nc = k.nc
    s_w, s_hi, s_lo, s_sm, s_sq, s_rt, s_rT, s_out, s_row, s_T, s_tp, s_th, s_tl = (
        k.sem(f"s_p1_{n}") for n in ("w", "hi", "lo", "sm", "sq", "rt", "rT", "out", "row", "T", "tp", "th", "tl"))
    prods = hi_lo_products(KC)
    slots = [(m, c0, cn) for c0, cn in CHUNKS for m in range(KC)]
    NB = 3
    with ExitStack() as c:
        n2 = k.sb(c, "p1_n2", [P, NT], F32)
        junk = k.sb(c, "p1_junk", [P, 2, D], F32)
        sm = k.sb(c, "p1_sm", [P, 4, NT], F32)
        rT = k.sb(c, "p1_rT", [NT, P], F32)
        rrow = k.sb(c, "p1_rrow", [P, 2, CH], F32)
        T = k.sb(c, "p1_T", [P, 2, CH], F32)
        pw = k.ps(c, "p1_pw", [P, NB, CH])
        pt = k.ps(c, "p1_pt", [P, NB, CH])
        pr = k.ps(c, "p1_pr", [P, CH])
        block = c.enter_context(nc.Block())
        s_rr = [k.sem(f"s_p1_rr{i}") for i in range(2)]

        @block.sync
        def _(sp):
            sp.wait_ge(s_rT, 1)
            sp.dma_start(r_dram.rearrange("(t p) -> t p", p=P), rT[:]).then_inc(s_out, 16)
            sp.wait_ge(s_out, 16)
            for m, (c0, cn) in enumerate(CHUNKS):
                if m >= 2:
                    sp.wait_ge(s_T, 2 * (m - 1))
                sp.dma_start(rrow[:, m % 2, 0:cn], r_dram[c0:c0 + cn].unsqueeze(0).to_broadcast([P, cn])).then_inc(s_rr[m % 2], 16)

        @block.tensor
        def _(pe):
            for t in range(NT):
                if t >= NB:
                    pe.wait_ge(s_lo, t - NB + 1)
                    pe.wait_ge(s_sq, t - NB + 1)
                for n, (kc, a, b) in enumerate(prods):
                    last = nc.tensor.matmul(pw[:, t % NB, 0:D], hT[:, a, kc, t * P:(t + 1) * P], w[:, b, kc, :],
                                            start=(n == 0), stop=(n == len(prods) - 1))
                last.then_inc(s_w, 1)
            for j, (m, c0, cn) in enumerate(slots):
                if j == 2:
                    pe.wait_ge(s_sm, 8)
                    nc.tensor.transpose(pr[0:NT, 0:P], rcol[:, 0, :], k.ident[:]).then_inc(s_rt, 1)
                if j >= NB:
                    pe.wait_ge(s_T, j - NB + 1)
                for n, (kc, a, b) in enumerate(prods):
                    last = nc.tensor.matmul(pt[:, j % NB, 0:cn], w[:, a, kc, m * P:(m + 1) * P], hT[:, b, kc, c0:c0 + cn],
                                            start=(n == 0), stop=(n == len(prods) - 1))
                last.then_inc(s_tp, 1)

        @block.scalar
        def _(act):
            for t in range(NT):
                act.wait_ge(s_w, t + 1)
                nc.scalar.activation(WHhi[:, t, 0:D], pw[:, t % NB, 0:D], ACT.Copy, scale=WHSC / PSC).then_inc(s_hi, 1)
                if t >= 2:
                    act.wait_ge(s_sq, t - 1)
                nc.scalar.activation(junk[:, t % 2, :], pw[:, t % NB, 0:D], ACT.Square, scale=1.0 / PSC,
                                     accum_out=n2[:, t:t + 1]).then_inc(s_sq, 1)
            act.wait_ge(s_sm, 1)
            nc.scalar.activation(sm[:, 1, :], sm[:, 0, :], ACT.Sqrt).then_inc(s_sm, 1)
            act.wait_ge(s_rt, 1)
            nc.scalar.activation(rT[:], pr[0:NT, 0:P], ACT.Copy).then_inc(s_rT, 1)
            for j, (m, c0, cn) in enumerate(slots):
                act.wait_ge(s_T, j + 1)
                nc.scalar.activation(WnT[:, 0, m, c0:c0 + cn], T[:, j % 2, 0:cn], ACT.Copy).then_inc(s_th, 1)

        @block.vector
        def _(dve):
            nc.vector.memset(WHhi[:, :, D], WHSC)
            for t in range(NT):
                dve.wait_ge(s_sq, t + 1)
                nc.vector.scalar_tensor_tensor(WHlo[:, t, :], pw[:, t % NB, 0:D], WHSC / PSC, WHhi[:, t, 0:D],
                                               ALU.mult, ALU.subtract).then_inc(s_lo, 1)
            dve.wait_ge(s_sq, NT)
            nc.vector.tensor_scalar(sm[:, 0, :], n2[:], R_MIN * R_MIN, None, ALU.max).then_inc(s_sm, 1)
            dve.wait_ge(s_sm, 2)
            nc.vector.reciprocal(sm[:, 2, :], sm[:, 1, :]).then_inc(s_sm, 1)
            dve.wait_ge(s_sm, 3)
            nc.vector.tensor_tensor(sm[:, 3, :], sm[:, 2, :], sm[:, 0, :], ALU.mult).then_inc(s_sm, 1)
            dve.wait_ge(s_sm, 4)
            nc.vector.tensor_tensor(sm[:, 3, :], sm[:, 3, :], sm[:, 2, :], ALU.mult).then_inc(s_sm, 1)
            dve.wait_ge(s_sm, 5)
            nc.vector.tensor_scalar(sm[:, 3, :], sm[:, 3, :], -0.5, 1.5, ALU.mult, ALU.add).then_inc(s_sm, 1)
            dve.wait_ge(s_sm, 6)
            nc.vector.tensor_tensor(rcol[:, 0, :], sm[:, 3, :], sm[:, 2, :], ALU.mult).then_inc(s_sm, 1)
            dve.wait_ge(s_sm, 7)
            nc.vector.tensor_scalar(rcol[:, 1, :], rcol[:, 0, :], NORM_EPS, None, ALU.mult).then_inc(s_sm, 1)
            nc.vector.tensor_scalar(k.ident8[:].bitcast(U8), k.ident[:], float(FP8_ONE), None, ALU.mult)
            for j, (m, c0, cn) in enumerate(slots):
                dve.wait_ge(s_tp, j + 1)
                dve.wait_ge(s_rr[(j // 2) % 2], 16 * (j // 4 + 1))
                if j >= 2:
                    dve.wait_ge(s_tl, j - 1)
                nc.vector.scalar_tensor_tensor(T[:, j % 2, 0:cn], pt[:, j % NB, 0:cn], NSC / PSC, rrow[:, (j // 2) % 2, 0:cn],
                                               ALU.mult, ALU.mult).then_inc(s_T, 1)
                dve.wait_ge(s_th, j + 1)
                nc.vector.tensor_tensor(WnT[:, 1, m, c0:c0 + cn], T[:, j % 2, 0:cn], WnT[:, 0, m, c0:c0 + cn],
                                        ALU.subtract).then_inc(s_tl, 1)


def cosine_attend(k, WnT, WHhi, WHlo, rcol, r_dram, adjT_dram):
    nc = k.nc
    s_q, s_ln, s_cf, s_dot, s_t, s_e, s_em, s_hi, s_lo, s_mm, s_rd, s_x, s_own = (
        k.sem(f"s_c1_{n}") for n in ("q", "ln", "cf", "dot", "t", "e", "em", "hi", "lo", "mm", "rd", "x", "own"))
    s_in = [k.sem(f"s_c1_in{i}") for i in range(2)]
    prods = hi_lo_products(KC)
    RD, RC, RT, RE, RS = 4, 3, 2, 2, 3
    W = 2 * CW
    with ExitStack() as c:
        Q = k.sb(c, "c1_Q", [P, 2, NC, W], F32)
        CF = k.sb(c, "c1_CF", [P, RC, W], F32)
        T = k.sb(c, "c1_T", [P, RT, W], F32)
        E = k.sb(c, "c1_E", [P, RE, W], F32)
        EM = k.sb(c, "c1_EM", [P, 2, W], F32)
        rr = k.sb(c, "c1_rr", [P, 2, CW], F32)
        EH = k.sb(c, "c1_EH", [P, RS, W], F16)
        EL = k.sb(c, "c1_EL", [P, RS, W], F16)
        mv = k.sb(c, "c1_mv", [P, 2, 2, KC, CW], F16)
        ad = k.sb(c, "c1_ad", [P, 2, CT, NT, P], FP8)
        rden = k.sb(c, "c1_rden", [P, 2, CT], F32)
        shift = k.sb(c, "c1_shift", [P, 1], F32)
        pd = k.ps(c, "c1_pd", [P, RD, CH])
        pa = k.ps(c, "c1_pa", [P, 2, CT, CH])
        s_c = k.sem("s_c1_shift")
        block = c.enter_context(nc.Block())

        @block.sync
        def _(sp):
            def chunk(c, q, last):
                sp.wait_ge(s_x, c + 1)
                sp.dma_start(mv[:, q].rearrange("p a k n -> p (a k) n"),
                             WnT[:, :, :, bass.ds(c * CW, CW)].rearrange("p a k n -> p (a k) n")).then_inc(s_in[q], 16)
                sp.dma_start(rr[:, q, :], r_dram[bass.ds(c * CW, CW)].unsqueeze(0).to_broadcast([P, CW])).then_inc(s_in[q], 16)
                sp.dma_start(ad[:, q].rearrange("p t j i -> p t (j i)").bitcast(U8),
                             adjT_dram[bass.ds(c * CT, CT)].rearrange("t p n -> p t n").bitcast(U8)).then_inc(s_in[q], 16)

            over_chunks(sp, chunk)

        def arrived(eng, c, q):
            eng.wait_ge(s_in[q], 24 * (c - q) + 48)

        @block.gpsimd
        def _(pool):
            nc.gpsimd.memset(shift[:], ESHIFT).then_inc(s_c, 1)

            def chunk(c, q, last):
                arrived(pool, c, q)
                pool.wait_ge(s_cf, (c + 1) * NC)
                k.settle(pool)
                for jp in range(NC):
                    for j in range(2):
                        ins = nc.gpsimd.tensor_scalar(Q[:, q, jp, j * CW:(j + 1) * CW], rr[:, q, :],
                                                      rcol[:, 1, 2 * jp + j:2 * jp + j + 1], 1.0, ALU.mult, ALU.add)
                ins.then_inc(s_q, 1)

            over_chunks(pool, chunk)

        @block.scalar
        def _(act):
            act.sem_inc(s_cf, 2 * NC)
            act.wait_ge(s_c, 1)

            def factor(c, q, jp):
                if jp == 0:
                    act.wait_ge(s_q, c + 1)
                    nc.scalar.activation(Q[:, q], Q[:, q], ACT.Ln).then_inc(s_ln, 1)
                    act.wait_ge(s_ln, c + 1)
                act.wait_ge(s_t, c * NC + prior_use(jp, RC, NC))
                nc.scalar.activation(CF[:, jp % RC, :], Q[:, q, jp, :], ACT.Exp, scale=-1.0).then_inc(s_cf, 1)

            def weight(c, q, jp):
                act.wait_ge(s_t, c * NC + jp + 1 + NC)
                act.wait_ge(s_em, c * NC + prior_use(jp, RE, NC))
                nc.scalar.activation(E[:, jp % RE, :], T[:, jp % RT, :], ACT.Exp, scale=1.0 / (NSC * NSC),
                                     bias=shift[:, 0:1]).then_inc(s_e, 1)

            def chunk(c, q, last):
                for jp in range(NC):
                    for d, what in ((2, factor), (1, weight)):
                        at_ = step_ahead(c, q, jp, d, last)
                        if at_:
                            what(*at_)

            factor(0, 0, 0)
            factor(0, 0, 1)
            weight(0, 0, 0)
            over_chunks(act, chunk)

        @block.vector
        def _(dve):
            dve.sem_inc(s_t, NC)
            dve.sem_inc(s_em, NC)
            dve.sem_inc(s_x, 2)

            def sim(c, q, jp):
                dve.wait_ge(s_cf, (c + 2) * NC + jp + 1)
                dve.wait_ge(s_dot, c * NC + jp + 1)
                dve.wait_ge(s_e, c * NC + prior_use(jp, RT, NC))
                nc.vector.tensor_tensor(T[:, jp % RT, :], pd[:, jp % RD, :], CF[:, jp % RC, :], ALU.mult).then_inc(s_t, 1)

            def split(c, q, jp):
                dve.wait_ge(s_e, c * NC + jp + 1 + NC)
                dve.wait_ge(s_lo, c * NC + prior_use(jp, 2, NC))
                k.settle(dve)
                for j in range(2):
                    ins = nc.vector.tensor_tensor(EM[:, jp % 2, j * CW:(j + 1) * CW].rearrange("p (t i) -> p t i", t=CT),
                                                  E[:, jp % RE, j * CW:(j + 1) * CW].rearrange("p (t i) -> p t i", t=CT),
                                                  ad[:, q, :, 2 * jp + j, :], ALU.mult)
                ins.then_inc(s_em, 1)
                dve.wait_ge(s_em, c * NC + jp + 1 + NC)
                dve.wait_ge(s_mm, c * NC + prior_use(jp, RS, NC))
                nc.vector.tensor_copy(EH[:, jp % RS, :], EM[:, jp % 2, :]).then_inc(s_hi, 1)
                dve.wait_ge(s_hi, c * NC + jp + 1)
                nc.vector.tensor_tensor(EL[:, jp % RS, :], EM[:, jp % 2, :], EH[:, jp % RS, :], ALU.subtract).then_inc(s_lo, 1)

            def finish(c, q):
                dve.wait_ge(s_mm, (c + 1) * NC + NC)
                nc.vector.reciprocal(rden[:, q, :], pa[:, q, :, D]).then_inc(s_rd, 1)
                dve.wait_ge(s_rd, c + 1)
                for t in range(CT):
                    xs = k.X[:, bass.ds(c * CT + t, 1), :].rearrange("p t d -> p (t d)")
                    ins = nc.vector.scalar_tensor_tensor(xs, pa[:, q, t, 0:D], rden[:, q, t:t + 1], xs, ALU.mult, ALU.add)
                ins.then_inc(s_x, 1)

            def chunk(c, q, last, first=False):
                arrived(dve, c, q)
                for t in range(CT):
                    own = ad[:, q, t, bass.ds(c * CT + t, 1), :].rearrange("p t i -> p (t i)").bitcast(I32)
                    ins = nc.vector.tensor_tensor(own, own, k.ident8[:].bitcast(I32), ALU.bitwise_or)
                ins.then_inc(s_own, 1)
                dve.wait_ge(s_own, c + 1)
                for jp in range(NC):
                    if jp == 3 and not first:
                        finish(c - 1, 1 - q)
                    ahead = step_ahead(c, q, jp, 1, last)
                    if ahead:
                        sim(*ahead)
                    split(c, q, jp)

            dve.sem_inc(s_lo, NC)
            sim(0, 0, 0)
            chunk(0, 0, False, True)
            with dve.Fori(0, NC // 2 - 1) as i:
                chunk(2 * i + 1, 1, False)
                chunk(2 * i + 2, 0, False)
            chunk(NC - 2, 1, False)
            chunk(NC - 1, 0, True)
            finish(NC - 1, 0)

        @block.tensor
        def _(pe):
            pe.sem_inc(s_mm, NC)
            pe.sem_inc(s_e, NC)

            def dots(c, q, jp):
                if jp == 0:
                    arrived(pe, c, q)
                pe.wait_ge(s_t, c * NC + prior_use(jp, RD, NC))
                for j in range(2):
                    jt = 2 * jp + j
                    for n, (kc, a, b) in enumerate(prods):
                        last = nc.tensor.matmul(pd[:, jp % RD, j * CW:(j + 1) * CW], WnT[:, a, kc, jt * P:(jt + 1) * P],
                                                mv[:, q, b, kc, :], start=(n == 0), stop=(n == len(prods) - 1))
                last.then_inc(s_dot, 1)

            def sums(c, q, jp):
                if jp == 0:
                    pe.wait_ge(s_x, c + 1)
                pe.wait_ge(s_lo, c * NC + jp + 1 + NC)
                for j in range(2):
                    jt = 2 * jp + j
                    for t in range(CT):
                        col = j * CW + t * P
                        first, final = jt == 0, jt == NT - 1
                        hi, lo = EH[:, jp % RS, col:col + P], EL[:, jp % RS, col:col + P]
                        nc.tensor.matmul(pa[:, q, t, 0:D + 1], hi, WHhi[:, jt, :], start=first, stop=False, skip_group_check=True)
                        nc.tensor.matmul(pa[:, q, t, 0:D], hi, WHlo[:, jt, :], start=False, stop=False, skip_group_check=True)
                        last = nc.tensor.matmul(pa[:, q, t, 0:D + 1], lo, WHhi[:, jt, :], start=False, stop=final, skip_group_check=True)
                last.then_inc(s_mm, 1)

            def chunk(c, q, last):
                for jp in range(NC):
                    ahead = step_ahead(c, q, jp, 3, last)
                    if ahead:
                        dots(*ahead)
                    sums(c, q, jp)

            for jp in range(3):
                dots(0, 0, jp)
            over_chunks(pe, chunk)


def layer1(k, ap, adjT_dram):
    with ExitStack() as c:
        r_dram = k.dram("r_dram", (NP,), F32)
        w = k.sb(c, "w_cos", [P, 2, KC, D], F16)
        rcol = k.sb(c, "rcol", [P, 2, NT], F32)
        k.ident8 = k.sb(c, "ident8", [P, P], FP8)
        hT = k.sb(c, "hT1", [P, 2 * KC * NP], F16)
        hTv = hT[:].rearrange("p (a k n) -> p a k n", a=2, k=KC)
        normalise(k, "n1", hTv, [(ap["L1_gnn_W"], lambda part: w[:, part, :, :])])
        WnT = k.sb(c, "WnT", [P, 2, KC, NP], F16)
        WHhi = k.sb(c, "WHhi", [P, NT, D + 1], F16)
        WHlo = k.sb(c, "WHlo", [P, NT, D], F16)
        cosine_project(k, hTv, w, WnT, WHhi, WHlo, rcol, r_dram)
        cosine_attend(k, WnT, WHhi, WHlo, rcol, r_dram, adjT_dram)



KROWS = 3 * HD + 2
QKSC = 1024.0
SHARP = 2.0 ** 20
MASK = 2.0 ** 60
SCH = 4
SW = NP // SCH
SB = SW // 2
NB2 = NP // (2 * P)
TA = 8
RESULT_AT = 2


def hard_project(k, ap, hT, w, QT, KT, KS, Vhl, q_dram):
    nc = k.nc
    s_in, s_v, s_vh, s_vl, s_p, s_T, s_hi, s_lo, s_we, s_be, s_st = (
        k.sem(f"s_p2_{n}") for n in ("in", "v", "vh", "vl", "p", "T", "hi", "lo", "we", "be", "st"))
    prods = hi_lo_products(KC)
    NB = 3
    slots = [(s, m, c0, cn) for s in range(2) for m in range(KC) for c0, cn in CHUNKS]
    with ExitStack() as c:
        T = k.sb(c, "p2_T", [P, 2, CH], F32)
        we = k.sb(c, "p2_we", [P, 2], F32)
        be = k.sb(c, "p2_be", [KROWS, 4], F32)
        beh = k.sb(c, "p2_beh", [KROWS, 1], F16)
        pv = k.ps(c, "p2_pv", [P, NB, CH])
        pt = k.ps(c, "p2_pt", [P, NB, CH])
        block = c.enter_context(nc.Block())
        B0 = 3 * HD

        @block.sync
        def _(sp):
            for q in range(P // HD):
                sp.dma_start(we[q * HD:(q + 1) * HD, 0:1], ap["L2_gnn_we"].rearrange("o d -> d o")).then_inc(s_in, 16)
            sp.dma_start(be[B0:KROWS, 0:1], ap["L2_gnn_be"].unsqueeze(0).to_broadcast([2, 1])).then_inc(s_in, 16)
            for s, src in ((0, KT), (1, QT)):
                for m in range(KC):
                    sp.wait_ge(s_lo, len(CHUNKS) * (s * KC + m + 1))
                    for q in range(4):
                        for r in range(3):
                            part = (0, 0, 1)[r] if s == 0 else (0, 1, 0)[r]
                            rows = slice(r * HD, (r + 1) * HD)
                            dst = KS[rows, 4 * m + q, :] if s == 0 else q_dram[rows, 4 * m + q, :]
                            sp.dma_start(dst, src[q * HD:(q + 1) * HD, part, m, :]).then_inc(s_st, 16)
            sp.wait_ge(s_st, 16 * 2 * HEADS * 3)

        @block.gpsimd
        def _(pool):
            pool.wait_ge(s_be, 4)
            nc.gpsimd.tensor_copy(KS[B0:KROWS].rearrange("p h n -> p (h n)"), be[B0:KROWS, 3:4].to_broadcast([2, HEADS * NP]))

        @block.vector
        def _(dve):
            dve.wait_ge(s_in, 16 * (P // HD + 1))
            nc.vector.tensor_scalar(we[:, 1:2], we[:, 0:1], QKSC, None, ALU.mult).then_inc(s_we, 1)
            nc.vector.tensor_scalar(be[B0:KROWS, 1:2], be[B0:KROWS, 0:1], QKSC, None, ALU.mult).then_inc(s_be, 1)
            dve.wait_ge(s_be, 1)
            nc.vector.tensor_copy(beh[B0:KROWS], be[B0:KROWS, 1:2]).then_inc(s_be, 1)
            dve.wait_ge(s_be, 2)
            nc.vector.tensor_tensor(be[B0:KROWS, 2:3], beh[B0:KROWS], k.ident[B0:KROWS, B0 + 1:B0 + 2], ALU.mult).then_inc(s_be, 1)
            dve.wait_ge(s_be, 3)
            nc.vector.tensor_tensor(be[B0:KROWS, 3:4], be[B0:KROWS, 1:2], be[B0:KROWS, 2:3], ALU.subtract).then_inc(s_be, 1)
            dve.wait_ge(s_we, 1)
            for j, (s, m, c0, cn) in enumerate(slots):
                dve.wait_ge(s_p, j + 1)
                if j >= 2:
                    dve.wait_ge(s_lo, j - 1)
                if s == 0:
                    nc.vector.tensor_scalar(T[:, j % 2, 0:cn], pt[:, j % NB, 0:cn], HD ** -0.5 * QKSC / PSC, we[:, 1:2],
                                            ALU.mult, ALU.add).then_inc(s_T, 1)
                else:
                    nc.vector.tensor_scalar(T[:, j % 2, 0:cn], pt[:, j % NB, 0:cn], QKSC / PSC, None, ALU.mult).then_inc(s_T, 1)
                dst = (KT, QT)[s]
                dve.wait_ge(s_hi, j + 1)
                nc.vector.tensor_tensor(dst[:, 1, m, c0:c0 + cn], T[:, j % 2, 0:cn], dst[:, 0, m, c0:c0 + cn],
                                        ALU.subtract).then_inc(s_lo, 1)
            for t in range(NT):
                b, e = t // 2, t % 2
                dve.wait_ge(s_vh, t + 1)
                nc.vector.scalar_tensor_tensor(Vhl[:, b, e, :, HD:2 * HD], pv[:, t % NB, 0:D].rearrange("p (h d) -> p h d", d=HD),
                                               QKSC / HEADS / PSC, Vhl[:, b, e, :, 0:HD], ALU.mult, ALU.subtract).then_inc(s_vl, 1)

        @block.scalar
        def _(act):
            for j, (s, m, c0, cn) in enumerate(slots):
                act.wait_ge(s_T, j + 1)
                nc.scalar.activation((KT, QT)[s][:, 0, m, c0:c0 + cn], T[:, j % 2, 0:cn], ACT.Copy).then_inc(s_hi, 1)
            for t in range(NT):
                act.wait_ge(s_v, t + 1)
                nc.scalar.activation(Vhl[:, t // 2, t % 2, :, 0:HD], pv[:, t % NB, 0:D].rearrange("p (h d) -> p h d", d=HD),
                                     ACT.Copy, scale=QKSC / HEADS / PSC).then_inc(s_vh, 1)

        @block.tensor
        def _(pe):
            for j, (s, m, c0, cn) in enumerate(slots):
                if j >= NB:
                    pe.wait_ge(s_T, j - NB + 1)
                for n, (kc, a, b) in enumerate(prods):
                    last = nc.tensor.matmul(pt[:, j % NB, 0:cn], w[:, 1 - s, a, kc, m * P:(m + 1) * P], hT[:, b, kc, c0:c0 + cn],
                                            start=(n == 0), stop=(n == len(prods) - 1))
                last.then_inc(s_p, 1)
            for t in range(NT):
                blk, e = t // 2, t % 2
                if t >= NB:
                    pe.wait_ge(s_vl, t - NB + 1)
                for n, (kc, a, b) in enumerate(prods):
                    nodes = hT[:, a, kc, blk * 2 * P:(blk + 1) * 2 * P].rearrange("p (n e) -> p n e", e=2)[:, :, e]
                    last = nc.tensor.matmul(pv[:, t % NB, 0:D], nodes, w[:, 2, b, kc, :], start=(n == 0), stop=(n == len(prods) - 1))
                last.then_inc(s_v, 1)


def over_tiles(eng, tile):
    with eng.Fori(0, NT // 2 - 1) as i:
        tile(2 * i, 0, False)
        tile(2 * i + 1, 1, False)
    tile(NT - 2, 0, False)
    tile(NT - 1, 1, True)


def head_ahead(i, q, h, d, last):
    if h + d < HEADS:
        return i, q, h + d
    return None if last else (i + 1, 1 - q, h + d - HEADS)


def hard_attend(k, adj_dram, KS, Vhl, q_dram):
    nc = k.nc
    s_pad, s_nb, s_sc, s_tt, s_mx, s_h, s_trA, s_trB, s_evA, s_evB, s_av, s_x, s_r = (
        k.sem(f"s_h2_{n}") for n in ("pad", "nb", "sc", "tt", "mx", "h", "trA", "trB", "evA", "evB", "av", "x", "r"))
    s_rows = [k.sem(f"s_h2_rows{i}") for i in range(2)]
    s_q = [k.sem(f"s_h2_q{i}") for i in range(2)]
    with ExitStack() as c:
        rows = k.sb(c, "h2_rows", [P, 2, NP], I32)
        off = k.sb(c, "h2_off", [P, 2, NP], F32)
        S = k.sb(c, "h2_S", [P, 2, NP], F32)
        H = k.sb(c, "h2_H", [P, 2 * NP], FP8)
        HT = k.sb(c, "h2_HT", [P, 2 * NP], FP8)
        QS = k.sb(c, "h2_QS", [KROWS, 2, HEADS, P], F16)
        mx = k.sb(c, "h2_mx", [P, 2, SCH], F32)
        nmx = k.sb(c, "h2_nmx", [P, 2], F32)
        ps = k.ps(c, "h2_ps", [P, 2, 2, CH])
        pT = k.ps(c, "h2_pT", [P, 2, 1024], BF16)
        po = k.ps(c, "h2_po", [P, 2, CH])
        block = c.enter_context(nc.Block())
        g_of = lambda i, h: i * HEADS + h

        @block.sync
        def _(sp):
            def load(i, s):
                sp.wait_ge(s_nb, i + 1)
                k.settle(sp)
                sp.dma_start(rows[:, s, 0:N], adj_dram[bass.ds(i * P, P), :]).then_inc(s_rows[s], 16)
                load_q(i, s)

            def load_q(i, s):
                sp.wait_ge(s_x, i + 1)
                k.settle(sp)
                sp.dma_start(QS[0:3 * HD, s], q_dram[:, :, bass.ds(i * P, P)]).then_inc(s_q[s], 16)

            sp.wait_ge(s_pad, 2)
            with sp.Fori(0, NT // 2 - 1) as i:
                load(2 * i, 0)
                load(2 * i + 1, 1)
            load(NT - 2, 0)
            sp.wait_ge(s_pad, 3)
            sp.dma_start(rows[0:LAST, 1, 0:N], adj_dram[(NT - 1) * P:N, :]).then_inc(s_rows[1], 16)
            load_q(NT - 1, 1)

        @block.gpsimd
        def _(pool):
            nc.gpsimd.memset(QS[3 * HD:KROWS], QKSC).then_inc(s_pad, 1)
            pool.wait_ge(s_pad, 1)
            nc.gpsimd.memset(rows[:, :, N:NP], 0).then_inc(s_pad, 1)
            pool.sem_inc(s_nb, 2)

            def offsets(i, s):
                pool.wait_ge(s_rows[s], 8 * (i - s) + 16)
                pool.wait_ge(s_x, i + 1)
                k.settle(pool)
                nc.gpsimd.tensor_scalar(off[:, s, :], rows[:, s, :], -1.0, MASK, ALU.add, ALU.mult).then_inc(s_nb, 1)

            pool.wait_ge(s_pad, 2)
            with pool.Fori(0, NT // 2 - 1) as i:
                offsets(2 * i, 0)
                offsets(2 * i + 1, 1)
            pool.wait_ge(s_nb, NT)
            nc.gpsimd.memset(rows[96:P, 1, :], 0).then_inc(s_pad, 1)
            pool.wait_ge(s_pad, 3)
            offsets(NT - 2, 0)
            offsets(NT - 1, 1)

        @block.tensor
        def _(pe):
            pe.sem_inc(s_trA, 2)
            pe.sem_inc(s_trB, 2)
            pe.sem_inc(s_av, 2)

            def scores(i, q, h, chunks):
                for ch in chunks:
                    if h == 0 and ch == 0:
                        pe.wait_ge(s_q[q], 8 * (i - q) + 16)
                    pe.wait_ge(s_tt, g_of(i, h) * SCH + ch + 1)
                    for b in range(2):
                        c0 = ch * SW + b * SB
                        last = nc.tensor.matmul(ps[:, ch % 2, b, 0:SB], QS[:, q, h, :], KS[:, h, c0:c0 + SB], start=True, stop=True)
                    last.then_inc(s_sc, 1)

            def transposes(i, q, h):
                g = g_of(i, h)
                pe.wait_ge(s_h, g + 3)
                for part, (b0, b1), free, done in ((0, (0, TA), s_evA, s_trA), (1, (TA, NB2), s_evB, s_trB)):
                    pe.wait_ge(free, g + 1)
                    for b in range(b0, b1):
                        src = H[:, (h % 2) * NP + b * 2 * P:(h % 2) * NP + (b + 1) * 2 * P].bitcast(BF16)
                        last = nc.tensor.transpose(pT[:, part, (b - b0) * P:(b - b0 + 1) * P], src, k.ident16[:])
                    last.then_inc(done, 1)

            def sums(i, q, h):
                g = g_of(i, h)
                if h == 0:
                    pe.wait_ge(s_x, i + 1)
                pe.wait_ge(s_evA, g + 2)
                pe.wait_ge(s_evB, g + 2)
                k.settle(pe)
                wt = HT[:, (h % 2) * NP:(h % 2 + 1) * NP].rearrange("p (b i e) -> p b i e", b=NB2, e=2)
                for b in range(NB2):
                    for e in range(2):
                        last = nc.tensor.matmul(po[:, q, h * 2 * HD:(h + 1) * 2 * HD], wt[:, b, :, e], Vhl[:, b, e, h, :],
                                                start=(b == 0 and e == 0), stop=(b == NB2 - 1 and e == 1), skip_group_check=True)
                last.then_inc(s_av, 1)

            def steps(i, q, h, last, own=True):
                s3, s4, t2 = (head_ahead(i, q, h, d, last) for d in (3, 4, 2))
                if s3:
                    scores(*s3, range(1, 2))
                sums(i, q, h)
                if s3:
                    scores(*s3, range(2, SCH))
                if s4:
                    scores(*s4, range(1))
                if t2:
                    transposes(*t2)

            scores(0, 0, 0, range(SCH))
            scores(0, 0, 1, range(SCH))
            scores(0, 0, 2, range(1))
            transposes(0, 0, 0)
            scores(0, 0, 2, range(1, SCH))
            scores(0, 0, 3, range(1))
            transposes(0, 0, 1)
            over_tiles(pe, lambda i, q, last: [steps(i, q, h, last) for h in range(HEADS)])

        @block.scalar
        def _(act):
            act.sem_inc(s_h, 2)
            act.sem_inc(s_evA, 1)

            def weights(i, q, h):
                g = g_of(i, h)
                act.wait_ge(s_mx, g + 1)
                act.wait_ge(s_trB, g + 1)
                k.settle(act)
                nc.scalar.activation(H[:, (h % 2) * NP:(h % 2 + 1) * NP], S[:, h % 2, :], ACT.Exp, bias=nmx[:, h % 2:h % 2 + 1],
                                     scale=1.0, saturate=False).then_inc(s_h, 1)

            def evacuate(i, q, h):
                g = g_of(i, h)
                act.wait_ge(s_trA, g + 3)
                act.wait_ge(s_av, g + 1)
                dst = HT[:, (h % 2) * NP:(h % 2) * NP + TA * 2 * P]
                nc.scalar.activation(dst.bitcast(U16), pT[:, 0, :].bitcast(U16), ACT.Copy).then_inc(s_evA, 1)

            def steps(i, q, h, last):
                s1 = head_ahead(i, q, h, 1, last)
                if s1:
                    weights(*s1)
                evacuate(i, q, h)

            weights(0, 0, 0)
            over_tiles(act, lambda i, q, last: [steps(i, q, h, last) for h in range(HEADS)])

        @block.vector
        def _(dve):
            dve.sem_inc(s_tt, 2)
            dve.sem_inc(s_evB, 1)
            dve.sem_inc(s_x, 2)

            def maxima(i, q, h, chunks):
                g = g_of(i, h)
                for ch in chunks:
                    if h == 0 and ch == 0:
                        dve.wait_ge(s_nb, i + 3)
                    if ch == 0:
                        dve.wait_ge(s_h, g + 1)
                    dve.wait_ge(s_sc, g * SCH + ch + 1)
                    k.settle(dve)
                    two = lambda x: x.rearrange("p (b n) -> p b n", b=2)
                    nc.vector.tensor_tensor_reduce(out=two(S[:, h % 2, ch * SW:(ch + 1) * SW]), in0=ps[:, ch % 2, :, 0:SB],
                                                   in1=two(off[:, q, ch * SW:(ch + 1) * SW]), scale=SHARP, scalar=-3e38,
                                                   op0=ALU.add, op1=ALU.max, accum_out=mx[:, h % 2, ch:ch + 1]).then_inc(s_tt, 1)
                if chunks[-1] == SCH - 1:
                    dve.wait_ge(s_tt, (g + 1) * SCH + 2)
                    nc.vector.tensor_reduce(nmx[:, h % 2:h % 2 + 1], mx[:, h % 2, :], AX.X, ALU.max, negate=True).then_inc(s_mx, 1)

            def evacuate(i, q, h):
                g = g_of(i, h)
                dve.wait_ge(s_trB, g + 3)
                dve.wait_ge(s_av, g + 1)
                dst = HT[:, (h % 2) * NP + TA * 2 * P:(h % 2 + 1) * NP]
                nc.vector.tensor_scalar(dst.bitcast(I32), pT[:, 1, 0:(NB2 - TA) * P].bitcast(I32), 0, None,
                                        ALU.bitwise_or).then_inc(s_evB, 1)

            def result(i, q):
                dve.wait_ge(s_av, i * HEADS + HEADS + 2)
                xs = k.X[:, bass.ds(i, 1), :].rearrange("p t (h d) -> p (t h) d", d=HD)
                both = po[:, q, :].rearrange("p (h a d) -> p h a d", a=2, d=HD)
                nc.vector.scalar_tensor_tensor(xs, both[:, :, 0, :], 1.0 / QKSC, xs, ALU.mult, ALU.add).then_inc(s_r, 1)
                dve.wait_ge(s_r, i + 1)
                nc.vector.scalar_tensor_tensor(xs, both[:, :, 1, :], 1.0 / QKSC, xs, ALU.mult, ALU.add).then_inc(s_x, 1)

            def steps(i, q, h, last, first=False):
                s1, s2 = (head_ahead(i, q, h, d, last) for d in (1, 2))
                if s1:
                    maxima(*s1, range(1, SCH))
                if s2:
                    maxima(*s2, range(1))
                evacuate(i, q, h)
                if h == RESULT_AT and not first:
                    result(i - 1, 1 - q)

            maxima(0, 0, 0, range(SCH))
            maxima(0, 0, 1, range(1))
            for h in range(HEADS):
                steps(0, 0, h, False, True)
            with dve.Fori(0, NT // 2 - 1) as i:
                for h in range(HEADS):
                    steps(2 * i + 1, 1, h, False)
                for h in range(HEADS):
                    steps(2 * i + 2, 0, h, False)
            for h in range(HEADS):
                steps(NT - 1, 1, h, True)
            result(NT - 1, 1)


def layer2(k, ap):
    with ExitStack() as c:
        q_dram = k.dram("q_dram", (3 * HD, HEADS, NP), F16)
        KS = k.sb(c, "KS", [KROWS, HEADS, NP], F16)
        Vhl = k.sb(c, "Vhl", [P, NB2, 2, HEADS, 2 * HD], F16)
        with ExitStack() as c1:
            w = k.sb(c1, "w_hard", [P, 3, 2, KC, D], F16)
            hT = k.sb(c1, "hT2", [P, 2, KC, NP], F16)
            part_of = lambda i: lambda part: w[:, i, part, :, :]
            normalise(k, "n2", hT, [(ap[f"L2_gnn_W{n}"], part_of(i)) for i, n in enumerate("QKV")])
            QT = k.sb(c1, "QT", [P, 2, KC, NP], F16)
            KT = k.sb(c1, "KT", [P, 2, KC, NP], F16)
            hard_project(k, ap, hT, w, QT, KT, KS, Vhl, q_dram)
        hard_attend(k, ap["adj"], KS, Vhl, q_dram)




def mean_weights(k, ap, m, bias, ideg_dram):
    nc = k.nc
    s_in, s_tr, s_cp, s_bb, s_mm, s_hi, s_deg, s_rT, s_out, s_b = (
        k.sem(f"s_w3_{n}") for n in ("in", "tr", "cp", "bb", "mm", "hi", "deg", "rT", "out", "b"))
    with ExitStack() as c:
        raw = k.sb(c, "w3_raw", [P, 2, KC, D], F32)
        wt = k.sb(c, "w3_t", [P, 2, KC, D], F32)
        comb = k.sb(c, "w3_comb", [P, 2, KC, D], F32)
        bcol = k.sb(c, "w3_bcol", [P, 2, KC], F32)
        bb = k.sb(c, "w3_bb", [P, 2, KC, P], F32)
        bc = k.sb(c, "w3_bc", [P, D], F32)
        dg = k.sb(c, "w3_deg", [P, 2, NT], F32)
        dT = k.sb(c, "w3_degT", [NT, P], F32)
        pt = k.ps(c, "w3_pt", [P, 2, CH])
        pm = k.ps(c, "w3_pm", [P, 2, CH])
        pb = k.ps(c, "w3_pb", [P, CH])
        pd = k.ps(c, "w3_pd", [P, CH])
        block = c.enter_context(nc.Block())
        srcs = [(ap["L3_gnn_W_self"], ap["L3_gnn_b_self"]), (ap["L3_gnn_W_nb"], ap["L3_gnn_b_nb"])]
        LOADS = 2 * (1 + KC) + 2

        @block.sync
        def _(sp):
            for s, (w, b) in enumerate(srcs):
                sp.dma_start(raw[:, s], w.rearrange("(k p) c -> p k c", p=P)).then_inc(s_in, 16)
                for kc in range(KC):
                    sp.dma_start(bcol[:, s, kc:kc + 1], b[kc * P:(kc + 1) * P].rearrange("(p o) -> p o", o=1)).then_inc(s_in, 16)
            sp.dma_start(comb[:].rearrange("p s k c -> p (s k) c"),
                         ap["L3_gnn_W_comb"].rearrange("(k p) c -> p k c", p=P)).then_inc(s_in, 16)
            sp.dma_start(bc[:], ap["L3_gnn_b_comb"].unsqueeze(0).to_broadcast([P, D])).then_inc(s_in, 16)
            sp.wait_ge(s_rT, 1)
            sp.dma_start(ideg_dram.rearrange("(t p) -> t p", p=P), dT[:]).then_inc(s_out, 16)
            sp.wait_ge(s_out, 16)

        @block.vector
        def _(dve):
            nc.vector.tensor_scalar(dg[:, 0, :], k.deg[:], 1.0, None, ALU.max).then_inc(s_deg, 1)
            dve.wait_ge(s_deg, 1)
            nc.vector.reciprocal(dg[:, 1, :], dg[:, 0, :]).then_inc(s_deg, 1)
            dve.wait_ge(s_in, 16 * LOADS)
            nc.vector.tensor_copy(bb[:], bcol[:].unsqueeze(3).to_broadcast([P, 2, KC, P])).then_inc(s_bb, 1)
            for s in range(2):
                dve.wait_ge(s_hi, s + 1)
                nc.vector.scalar_tensor_tensor(m[:, 1, s], pm[:, s, :].rearrange("p (k n) -> p k n", k=KC), WSC, m[:, 0, s],
                                               ALU.mult, ALU.subtract)
            dve.wait_ge(s_b, 1)
            nc.vector.tensor_tensor(bias[:], pb[:, 0:D], bc[:], ALU.add)

        @block.tensor
        def _(pe):
            pe.wait_ge(s_deg, 2)
            nc.tensor.transpose(pd[0:NT, 0:P], dg[:, 1, :], k.ident[:]).then_inc(s_tr, 1)
            pe.wait_ge(s_in, 16 * LOADS)
            for s in range(2):
                for kc in range(KC):
                    for kn in range(KC):
                        last = nc.tensor.transpose(pt[:, s, kc * D + kn * P:kc * D + (kn + 1) * P],
                                                   raw[:, s, kn, kc * P:(kc + 1) * P], k.ident[:])
                last.then_inc(s_tr, 1)
            for s in range(2):
                pe.wait_ge(s_cp, s + 1)
                for kn in range(KC):
                    for kc in range(KC):
                        last = nc.tensor.matmul(pm[:, s, kn * D:(kn + 1) * D], wt[:, s, kc, kn * P:(kn + 1) * P], comb[:, s, kc, :],
                                                start=(kc == 0), stop=(kc == KC - 1))
                last.then_inc(s_mm, 1)
            pe.wait_ge(s_bb, 1)
            for n, (s, kc) in enumerate([(s, kc) for s in range(2) for kc in range(KC)]):
                last = nc.tensor.matmul(pb[:, 0:D], bb[:, s, kc, :], comb[:, s, kc, :], start=(n == 0), stop=(n == 2 * KC - 1))
            last.then_inc(s_b, 1)

        @block.scalar
        def _(act):
            act.wait_ge(s_tr, 1)
            nc.scalar.activation(dT[:], pd[0:NT, 0:P], ACT.Copy).then_inc(s_rT, 1)
            for s in range(2):
                act.wait_ge(s_tr, s + 2)
                nc.scalar.activation(wt[:, s].rearrange("p k n -> p (k n)"), pt[:, s, :], ACT.Copy).then_inc(s_cp, 1)
            for s in range(2):
                act.wait_ge(s_mm, s + 1)
                nc.scalar.activation(m[:, 0, s], pm[:, s, :].rearrange("p (k n) -> p k n", k=KC), ACT.Copy, scale=WSC).then_inc(s_hi, 1)


def mean_aggregate(k, hT, Hn, m, bias, ideg_dram, adjT_dram, out_dram):
    nc = k.nc
    s_agg, s_T, s_hi, s_lo, s_mm, s_t, s_x, s_ideg, s_st = (
        k.sem(f"s_m3_{n}") for n in ("agg", "T", "hi", "lo", "mm", "t", "x", "ideg", "st"))
    s_in = [k.sem(f"s_m3_in{i}") for i in range(2)]
    prods = hi_lo_products(KC)
    with ExitStack() as c:
        ad = k.sb(c, "m3_ad", [P, 2, CT, NT, P], FP8)
        idr = k.sb(c, "m3_ideg", [P, NP], F32)
        T = k.sb(c, "m3_T", [P, 2, KC, CW], F32)
        aT = k.sb(c, "m3_aT", [P, 2, 2, KC, CW], F16)
        R = k.sb(c, "m3_R", [P, 2, CT, D], F32)
        pa = k.ps(c, "m3_pa", [P, 2, KC, CH])
        po = k.ps(c, "m3_po", [P, 2, CT, D])
        block = c.enter_context(nc.Block())

        @block.sync
        def _(sp):
            sp.dma_start(idr[:], ideg_dram.unsqueeze(0).to_broadcast([P, NP])).then_inc(s_ideg, 16)

            def load(c, q):
                sp.wait_ge(s_agg, c + 1)
                sp.dma_start(ad[:, q].rearrange("p t j i -> p t (j i)").bitcast(U8),
                             adjT_dram[bass.ds(c * CT, CT)].rearrange("t p n -> p t n").bitcast(U8)).then_inc(s_in[q], 16)

            def store(c):
                sp.wait_ge(s_x, c + 1)
                sp.dma_start(out_dram[bass.ds(c * CW, CW), :].rearrange("(t p) d -> p t d", p=P),
                             k.X[:, bass.ds(c * CT, CT), :]).then_inc(s_st, 16)

            load(0, 0)
            load(1, 1)
            with sp.Fori(0, NC // 2 - 1) as i:
                for q in range(2):
                    load(2 * i + 2 + q, q)
                    store(2 * i + q)
            load(NC - 1, 0)
            store(NC - 3)
            store(NC - 2)
            sp.wait_ge(s_x, NC)
            sp.dma_start(out_dram[(NT - 2) * P:(NT - 1) * P, :], k.X[:, NT - 2, :]).then_inc(s_st, 16)
            sp.dma_start(out_dram[(NT - 1) * P:N, :], k.X[0:LAST, NT - 1, :]).then_inc(s_st, 16)
            sp.wait_ge(s_st, 16 * (NC + 1))

        @block.tensor
        def _(pe):
            pe.sem_inc(s_agg, 2)
            pe.sem_inc(s_mm, 2)

            def sums(c, q):
                pe.wait_ge(s_in[q], 8 * (c - q) + 16)
                pe.wait_ge(s_T, c + 1)
                k.settle(pe)
                for kc in range(KC):
                    for jt in range(NT):
                        for a in range(2):
                            last = nc.tensor.matmul(pa[:, q, kc, 0:CW].rearrange("p (t i) -> p t i", t=CT),
                                                    Hn[:, a, jt, kc * P:(kc + 1) * P], ad[:, q, :, jt, :],
                                                    start=(jt == 0 and a == 0), stop=(jt == NT - 1 and a == 1))
                last.then_inc(s_agg, 1)

            def linear(c, q):
                pe.wait_ge(s_lo, c + 3)
                pe.wait_ge(s_t, c + 1)
                for t in range(CT):
                    for n, (kc, a, b) in enumerate(prods):
                        nc.tensor.matmul(po[:, q, t, :], hT[:, a, kc, bass.ds((c * CT + t) * P, P)], m[:, b, 0, kc, :],
                                         start=(n == 0), stop=False)
                    for n, (kc, a, b) in enumerate(prods):
                        last = nc.tensor.matmul(po[:, q, t, :], aT[:, q, a, kc, t * P:(t + 1) * P], m[:, b, 1, kc, :],
                                                start=False, stop=(n == len(prods) - 1))
                last.then_inc(s_mm, 1)

            sums(0, 0)
            with pe.Fori(0, NC // 2) as i:
                sums(2 * i + 1, 1)
                linear(2 * i, 0)
                sums(2 * i + 2, 0)
                linear(2 * i + 1, 1)
            linear(NC - 1, 0)

        @block.scalar
        def _(act):
            def chunk(c, q, last):
                act.wait_ge(s_T, c + 3)
                act.wait_ge(s_mm, c + 1)
                nc.scalar.activation(aT[:, q, 0], T[:, q], ACT.Copy).then_inc(s_hi, 1)

            over_chunks(act, chunk)

        @block.vector
        def _(dve):
            dve.sem_inc(s_T, 2)
            dve.sem_inc(s_t, 2)
            dve.sem_inc(s_lo, 2)
            dve.wait_ge(s_ideg, 16)

            def means(c, q):
                dve.wait_ge(s_agg, c + 3)
                dve.wait_ge(s_lo, c + 1)
                nc.vector.tensor_tensor(T[:, q], pa[:, q, :, 0:CW],
                                        idr[:, bass.ds(c * CW, CW)].unsqueeze(1).to_broadcast([P, KC, CW]), ALU.mult).then_inc(s_T, 1)
                dve.wait_ge(s_hi, c + 1)
                nc.vector.tensor_tensor(aT[:, q, 1], T[:, q], aT[:, q, 0], ALU.subtract).then_inc(s_lo, 1)

            def result(c, q):
                dve.wait_ge(s_mm, c + 3)
                for t in range(CT):
                    last = nc.vector.scalar_tensor_tensor(R[:, q, t, :], po[:, q, t, :], 1.0 / PSC, bias[:], ALU.mult, ALU.add)
                last.then_inc(s_t, 1)
                dve.wait_ge(s_t, c + 3)
                xs = k.X[:, bass.ds(c * CT, CT), :]
                nc.vector.scalar_tensor_tensor(xs, R[:, q], 0.0, xs, ALU.max, ALU.add).then_inc(s_x, 1)

            means(0, 0)
            with dve.Fori(0, NC // 2) as i:
                means(2 * i + 1, 1)
                result(2 * i, 0)
                means(2 * i + 2, 0)
                result(2 * i + 1, 1)
            result(NC - 1, 0)


def layer3(k, ap, adjT_dram, out_dram):
    with ExitStack() as c:
        ideg_dram = k.dram("ideg_dram", (NP,), F32)
        hT = k.sb(c, "hT3", [P, 2, KC, NP], F16)
        Hn = k.sb(c, "Hn", [P, 2, NT, D], F16)
        m = k.sb(c, "m3_w", [P, 2, 2, KC, D], F16)
        bias = k.sb(c, "m3_bias", [P, D], F32)
        normalise(k, "n3", hT, [], Hn)
        mean_weights(k, ap, m, bias, ideg_dram)
        mean_aggregate(k, hT, Hn, m, bias, ideg_dram, adjT_dram, out_dram)



def build(nc, ap, out_dram):
    with ExitStack() as ctx:
        k = Kernel(nc)
        k.s_adjT_out = nc.alloc_semaphore(name="s_adjT_out")
        k.X = k.sb(ctx, "X", [P, NT, D], F32)
        k.ident = k.sb(ctx, "ident", [P, P], F32)
        k.ident16 = k.sb(ctx, "ident16", [P, P], BF16)
        k.corner16 = k.sb(ctx, "corner16", [P, P], BF16)
        k.deg = k.sb(ctx, "deg", [P, NT], F32)
        adjT_dram = k.dram("adjT_dram", (NT, P, NP), FP8)
        setup_constants(k, ap["x"])
        with ExitStack() as c:
            k.adjT = k.sb(c, "adjT", [P, NT, NT, P], FP8)
            transpose_adjacency(k, ap["adj"])
            layer0(k, ap, adjT_dram)
        k.end_layer()
        layer1(k, ap, adjT_dram)
        k.end_layer()
        layer2(k, ap)
        k.end_layer()
        layer3(k, ap, adjT_dram, out_dram)


INPUTS = ["x", "adj", "L0_gnn_W_lin", "L0_gnn_attn_w", "L1_gnn_W", "L2_gnn_WQ", "L2_gnn_WK", "L2_gnn_WV", "L2_gnn_we",
          "L2_gnn_be", "L3_gnn_W_self", "L3_gnn_b_self", "L3_gnn_W_nb", "L3_gnn_b_nb", "L3_gnn_W_comb", "L3_gnn_b_comb"]


def kernel(**inputs):
    import numpy as np
    import concourse.bacc as bacc
    from concourse.bass_utils import run_bass_kernel_spmd

    nc = bacc.Bacc("TRN2", target_bir_lowering=False, num_devices=1)
    arrays, ap = {}, {}
    for name in INPUTS:
        a = np.ascontiguousarray(inputs[name])
        arrays[f"in_{name}_dram"] = a
        ap[name] = nc.dram_tensor(f"in_{name}_dram", a.shape, mybir.dt.from_np(a.dtype), kind="ExternalInput").ap()
    out = nc.dram_tensor("out_dram", (N, D), F32, kind="ExternalOutput").ap()
    build(nc, ap, out)
    r = run_bass_kernel_spmd(nc, [arrays], core_ids=[0])
    return r.results[0]["out_dram"]
```

```python
from contextlib import ExitStack

import concourse.bass as bass
from concourse import mybir

F32 = mybir.dt.float32
F16 = mybir.dt.float16
BF16 = mybir.dt.bfloat16
FP8 = mybir.dt.float8e4
I32 = mybir.dt.int32
U16 = mybir.dt.uint16
U8 = mybir.dt.uint8
ALU = mybir.AluOpType
ACT = mybir.ActivationFunctionType
AX = mybir.AxisListType

N = 3327
P = 128
NT = -(-N // P)
NP = NT * P
LAST = N - (NT - 1) * P
D = 256
KC = D // P
HEADS = 8
HD = D // HEADS
LN_EPS = 1e-5
SLOPE = 0.2
NORM_EPS = 1e-8
HSC = 256.0
WSC = 1024.0
PSC = HSC * WSC
FP8_ONE = 0x38
CH = 512
CHUNKS = [(c, min(CH, NP - c)) for c in range(0, NP, CH)]


def hi_lo_products(pairs):
    return [(kc, a, b) for kc in range(pairs) for a, b in ((0, 0), (0, 1), (1, 0))]


class Kernel:

    def __init__(self, nc):
        self.nc = nc
        self.layer_sems = []
        self.s_settled = nc.alloc_semaphore(name="s_settled")

    def sem(self, name):
        self.layer_sems.append(self.nc.alloc_semaphore(name=name))
        return self.layer_sems[-1]

    def end_layer(self):
        self.nc.all_engine_barrier()
        self.nc.clear_and_free_semaphores(self.layer_sems)
        self.nc.all_engine_barrier()
        self.layer_sems = []

    def settle(self, eng):
        eng.sem_inc(self.s_settled, 1)

    def sb(self, ctx, name, shape, dt):
        return ctx.enter_context(self.nc.sbuf_tensor(name, shape, dt))

    def ps(self, ctx, name, shape, dt=F32):
        return ctx.enter_context(self.nc.psum_tensor(name, shape, dt))

    def dram(self, name, shape, dt):
        return self.nc.dram_tensor(name, shape, dt, kind="Internal").ap()


def setup_constants(k, x_dram):
    nc = k.nc
    s_x, s_zero, s_ones, s_id = (k.sem(n) for n in ("s_x", "s_x_zero", "s_const_ones", "s_identity"))
    with ExitStack() as c:
        ones = k.sb(c, "ones_pp", [P, P], F32)
        corner = k.sb(c, "corner_f", [P, P], F32)
        block = c.enter_context(nc.Block())

        @block.sync
        def _(sp):
            sp.dma_start(k.X[:, 0:NT - 1, :], x_dram[0:(NT - 1) * P, :].rearrange("(t p) d -> p t d", p=P)).then_inc(s_x, 16)
            sp.wait_ge(s_zero, 1)
            sp.dma_start(k.X[0:LAST, NT - 1, :], x_dram[(NT - 1) * P:N, :]).then_inc(s_x, 16)
            sp.wait_ge(s_x, 32)

        @block.vector
        def _(dve):
            nc.vector.memset(k.X[:, NT - 1, :], 0.0).then_inc(s_zero, 1)
            nc.vector.memset(ones[:], 1.0).then_inc(s_ones, 1)
            dve.wait_ge(s_id, 2)
            nc.vector.tensor_copy(k.ident16[:], k.ident[:])
            nc.vector.tensor_copy(k.corner16[:], corner[:])

        @block.gpsimd
        def _(pool):
            pool.wait_ge(s_ones, 1)
            nc.gpsimd.affine_select(out=k.ident[:], in_=ones[:], compare_op=ALU.is_equal, fill=0.0, base=0,
                                    pattern=[[-1, P]], channel_multiplier=1).then_inc(s_id, 1)
            nc.gpsimd.affine_select(out=corner[:], in_=ones[:], compare_op=ALU.is_equal, fill=0.0, base=-2 * (P - 1),
                                    pattern=[[1, P]], channel_multiplier=1).then_inc(s_id, 1)


def transpose_adjacency(k, adj_dram):
    nc = k.nc
    s_rows = [[k.sem(f"s_adj_rows{s}{f}") for f in range(2)] for s in range(2)]
    HALF = NP // 2
    cut = lambda f: slice(f * HALF, (f + 1) * HALF)
    s_used, s_corner, s_tr, s_evac, s_pad = (
        k.sem(n) for n in ("s_adj_used", "s_corner", "s_adj_tr", "s_adj_evac", "s_adj_pad"))
    STEPS = NT // 2 - 1
    with ExitStack() as c:
        rows = k.sb(c, "adj_rows", [P, 2, NP], I32)
        a16 = k.sb(c, "adj16", [P, 2, NP], BF16)
        tr = k.ps(c, "adj_tr", [P, 2, 4 * 1024], BF16)
        block = c.enter_context(nc.Block())

        @block.sync
        def _(sp):
            sp.wait_ge(s_pad, 1)
            for s in range(2):
                for f in range(2):
                    c1 = N if f else HALF
                    sp.dma_start(rows[:, s, f * HALF:c1], adj_dram[s * P:(s + 1) * P, f * HALF:c1]).then_inc(s_rows[s][f], 16)
            with sp.Fori(0, STEPS - 1) as i:
                for s in range(2):
                    for f in range(2):
                        c1 = N if f else HALF
                        sp.wait_ge(s_used, 4 * i + 2 * s + f + 1)
                        sp.dma_start(rows[:, s, f * HALF:c1],
                                     adj_dram[bass.ds(i * (2 * P) + (s + 2) * P, P), f * HALF:c1]).then_inc(s_rows[s][f], 16)
            for f in range(2):
                c1 = N if f else HALF
                sp.wait_ge(s_used, 2 * (NT - 4) + f + 1)
                sp.dma_start(rows[:, 0, f * HALF:c1], adj_dram[(NT - 2) * P:(NT - 1) * P, f * HALF:c1]).then_inc(s_rows[0][f], 16)
            sp.wait_ge(s_pad, 2)
            for f in range(2):
                c1 = N if f else HALF
                sp.dma_start(rows[0:LAST, 1, f * HALF:c1], adj_dram[(NT - 1) * P:N, f * HALF:c1]).then_inc(s_rows[1][f], 16)

        @block.gpsimd
        def _(pool):
            nc.gpsimd.memset(rows[:, :, N:NP], 0).then_inc(s_pad, 1)
            pool.wait_ge(s_used, 2 * NT - 4)
            nc.gpsimd.memset(rows[96:P, 1, :], 0).then_inc(s_pad, 1)

        @block.scalar
        def _(act):
            def convert(t, s, step):
                act.wait_ge(s_tr, t + 1)
                for f in range(2):
                    act.wait_ge(s_rows[s][f], 16 * (step + 1))
                    nc.scalar.activation(a16[:, s, cut(f)], rows[:, s, cut(f)], ACT.Copy,
                                         accum_out=k.deg[:, f, bass.ds(t, 1)]).then_inc(s_used, 1)

            act.wait_ge(s_pad, 1)
            with act.Fori(0, STEPS) as i:
                for s in range(2):
                    convert(2 * i + s, s, i)
            convert(NT - 2, 0, STEPS)
            act.wait_ge(s_pad, 2)
            convert(NT - 1, 1, STEPS)

        @block.tensor
        def _(pe):
            pe.sem_inc(s_tr, 2)

            def transpose(t, s, final=False):
                pe.wait_ge(s_evac, t + 1)
                for f in range(2):
                    if final and f == 1:
                        pe.wait_ge(s_corner, 1)
                    else:
                        pe.wait_ge(s_used, 2 * t + f + 1)
                    for jt in range(f * NT // 2, (f + 1) * NT // 2):
                        last = nc.tensor.transpose(tr[:, s, jt * P:(jt + 1) * P], a16[:, s, jt * P:(jt + 1) * P], k.ident16[:])
                last.then_inc(s_tr, 1)

            with pe.Fori(0, STEPS) as i:
                for s in range(2):
                    transpose(2 * i + s, s)
            transpose(NT - 2, 0)
            transpose(NT - 1, 1, True)

        @block.vector
        def _(dve):
            dve.sem_inc(s_evac, 2)

            def evacuate(t, s):
                dve.wait_ge(s_tr, t + 3)
                nc.vector.tensor_scalar(k.adjT[:, bass.ds(t, 1), :, :].rearrange("p t j i -> p (t j i)").bitcast(U8),
                                        tr[:, s, 0:NP], float(FP8_ONE), None, ALU.mult).then_inc(s_evac, 1)

            with dve.Fori(0, STEPS) as i:
                for s in range(2):
                    evacuate(2 * i + s, s)
            dve.wait_ge(s_used, 2 * NT)
            nc.vector.tensor_tensor(a16[:, 1, NP - P:NP], a16[:, 1, NP - P:NP], k.corner16[:], ALU.add).then_inc(s_corner, 1)
            evacuate(NT - 2, 0)
            evacuate(NT - 1, 1)


def normalise(k, tag, hT, weights, h_nat=None, adjT_dram=None):
    nc = k.nc
    s_w, s_stat, s_sq, s_sm, s_h, s_tr, s_hi, s_lo = (
        k.sem(f"s_{tag}_{n}") for n in ("w", "stat", "sqrt", "small", "h", "tr", "hi", "lo"))
    slots = [(g, kc) for g in range(-(-NT // 4)) for kc in range(KC)]
    NB = 4
    with ExitStack() as c:
        H = k.sb(c, f"{tag}_h", [P, NT, D], F32)
        stats = k.sb(c, f"{tag}_stats", [P, NT, 6], F32)
        mv = k.sb(c, f"{tag}_mv", [P, NT, 2], F32)
        sm = k.sb(c, f"{tag}_sm", [P, 6, NT], F32)
        ve, rt, rs, t1, t2, nb = (sm[:, i, :] for i in range(6))
        raw = k.sb(c, f"{tag}_wraw", [P, max(1, len(weights)), 2, D], F32)
        pt = k.ps(c, f"{tag}_pt", [P, NB, CH])
        block = c.enter_context(nc.Block())
        nw = len(weights)

        @block.sync
        def _(sp):
            for i, (w, _) in enumerate(weights):
                sp.dma_start(raw[:, i, :, :], w.rearrange("(k p) c -> p k c", p=P)).then_inc(s_w, 16)
            if adjT_dram is not None:
                sp.dma_start(adjT_dram.rearrange("t p n -> p t n"), k.adjT[:].rearrange("p t j i -> p t (j i)")).then_inc(k.s_adjT_out, 16)

        @block.vector
        def _(dve):
            for t in range(NT):
                nc.vector.bn_stats(stats[:, t, :], k.X[:, t, :]).then_inc(s_stat, 1)
            for t in range(NT):
                dve.wait_ge(s_stat, t + 1)
                last = nc.vector.bn_aggr(mv[:, t, :], stats[:, t, :])
            last.then_inc(s_sm, 1)
            dve.wait_ge(s_sm, 1)
            nc.vector.tensor_scalar(ve, mv[:, :, 1], LN_EPS, None, ALU.add).then_inc(s_sm, 1)
            dve.wait_ge(s_sq, 1)
            nc.vector.reciprocal(rs, rt).then_inc(s_sm, 1)
            dve.wait_ge(s_sm, 3)
            nc.vector.tensor_tensor(t1, rs, rs, ALU.mult).then_inc(s_sm, 1)
            dve.wait_ge(s_sm, 4)
            nc.vector.tensor_tensor(t2, t1, ve, ALU.mult).then_inc(s_sm, 1)
            dve.wait_ge(s_sm, 5)
            nc.vector.tensor_scalar(t1, t2, -0.5, 1.5, ALU.mult, ALU.add).then_inc(s_sm, 1)
            dve.wait_ge(s_sm, 6)
            nc.vector.tensor_tensor(rt, t1, rs, ALU.mult).then_inc(s_sm, 1)
            dve.wait_ge(s_sm, 7)
            nc.vector.scalar_tensor_tensor(nb, mv[:, :, 0], -1.0, rt, ALU.mult, ALU.mult).then_inc(s_sm, 1)
            for i in range(nw):
                dve.wait_ge(s_hi, i + 1)
                wt = weights[i][1]
                nc.vector.scalar_tensor_tensor(wt(1), pt[:, i % NB, :].rearrange("p (k n) -> p k n", k=KC), WSC, wt(0),
                                               ALU.mult, ALU.subtract).then_inc(s_lo, 1)
            for j, (g, kc) in enumerate(slots):
                n0, n1 = g * CH, min(NP, (g + 1) * CH)
                dve.wait_ge(s_hi, nw + j + 1)
                nc.vector.scalar_tensor_tensor(hT[:, 1, kc, n0:n1], pt[:, (nw + j) % NB, 0:n1 - n0], HSC, hT[:, 0, kc, n0:n1],
                                               ALU.mult, ALU.subtract).then_inc(s_lo, 1)
            if h_nat is not None:
                dve.wait_ge(s_hi, nw + len(slots) + 1)
                nc.vector.scalar_tensor_tensor(h_nat[:, 1, :, :].rearrange("p t d -> p (t d)"), H[:].rearrange("p t d -> p (t d)"),
                                               HSC, h_nat[:, 0, :, :].rearrange("p t d -> p (t d)"), ALU.mult, ALU.subtract)

        @block.scalar
        def _(act):
            act.wait_ge(s_sm, 2)
            nc.scalar.activation(rt, ve, ACT.Sqrt).then_inc(s_sq, 1)
            for i in range(nw):
                act.wait_ge(s_tr, i + 1)
                nc.scalar.activation(weights[i][1](0), pt[:, i % NB, :].rearrange("p (k n) -> p k n", k=KC), ACT.Copy,
                                     scale=WSC).then_inc(s_hi, 1)
            act.wait_ge(s_sm, 8)

            def relu(t):
                nc.scalar.activation(H[:, t, :], k.X[:, t, :], ACT.Relu, scale=rt[:, t:t + 1], bias=nb[:, t:t + 1]).then_inc(s_h, 1)

            def high(j):
                g, kc = slots[j]
                n0, n1 = g * CH, min(NP, (g + 1) * CH)
                act.wait_ge(s_tr, nw + j + 1)
                nc.scalar.activation(hT[:, 0, kc, n0:n1], pt[:, (nw + j) % NB, 0:n1 - n0], ACT.Copy, scale=HSC).then_inc(s_hi, 1)

            for t in range(4):
                relu(t)
            for g in range(-(-NT // 4)):
                for t in range(4 * g + 4, min(4 * g + 8, NT)):
                    relu(t)
                high(2 * g)
                high(2 * g + 1)
            if h_nat is not None:
                act.wait_ge(s_h, NT)
                nc.scalar.activation(h_nat[:, 0, :, :].rearrange("p t d -> p (t d)"), H[:].rearrange("p t d -> p (t d)"),
                                     ACT.Copy, scale=HSC).then_inc(s_hi, 1)

        @block.tensor
        def _(pe):
            for i in range(nw):
                pe.wait_ge(s_w, 16 * nw)
                if i >= NB:
                    pe.wait_ge(s_lo, i - NB + 1)
                for kc in range(KC):
                    for kn in range(2):
                        last = nc.tensor.transpose(pt[:, i % NB, kc * D + kn * P:kc * D + (kn + 1) * P],
                                                   raw[:, i, kn, kc * P:(kc + 1) * P], k.ident[:])
                last.then_inc(s_tr, 1)
            for j, (g, kc) in enumerate(slots):
                tiles = range(4 * g, min(4 * g + 4, NT))
                pe.wait_ge(s_h, tiles[-1] + 1)
                if nw + j >= NB:
                    pe.wait_ge(s_lo, nw + j - NB + 1)
                for t in tiles:
                    last = nc.tensor.transpose(pt[:, (nw + j) % NB, (t % 4) * P:(t % 4 + 1) * P],
                                               H[:, t, kc * P:(kc + 1) * P], k.ident[:])
                last.then_inc(s_tr, 1)



G1 = HD + 1
VSC = 2048.0
STEP = 2.0 ** 60


def gat_project(k, hT, w, attn_w, el_dram, GE):
    nc = k.nc
    s_z, s_aw, s_wa, s_wahi, s_walo, s_g, s_ge, s_elp, s_elt = (
        k.sem(f"s_g0_{n}") for n in ("z", "aw", "wa", "wahi", "walo", "g", "ge", "elp", "elt"))
    s_out = [k.sem(f"s_g0_elout{i}") for i in range(2)]
    NB = 4
    prods = hi_lo_products(KC)
    with ExitStack() as c:
        raw = k.sb(c, "g0_wraw", [P, 2, D], F32)
        ad = k.sb(c, "g0_ad", [P, 2, 2 * HEADS], F32)
        elT = k.sb(c, "g0_elT", [HEADS, 2, CH], F32)
        pg = k.ps(c, "g0_pg", [P, NB, CH])
        pel = k.ps(c, "g0_pel", [HEADS, 2, CH])
        block = c.enter_context(nc.Block())

        @block.sync
        def _(sp):
            sp.wait_ge(s_z, 1)
            for h in range(HEADS):
                q, kn = h % 4, h // 4
                for side in range(2):
                    sp.dma_start(ad[HD * q:HD * q + HD, kn, side * HEADS + h:side * HEADS + h + 1],
                                 attn_w[side * HD:(side + 1) * HD].rearrange("(p o) -> p o", o=1)).then_inc(s_aw, 16)
            sp.dma_start(raw[:], k.w_lin.rearrange("(k p) c -> p k c", p=P)).then_inc(s_aw, 16)
            for m, (c0, cn) in enumerate(CHUNKS):
                sp.wait_ge(s_elt, m + 1)
                sp.dma_start(el_dram[:, c0:c0 + cn], elT[:, m % 2, 0:cn]).then_inc(s_out[m % 2], 16)
            for i in range(2):
                sp.wait_ge(s_out[i], 16 * len(range(i, len(CHUNKS), 2)))

        @block.vector
        def _(dve):
            nc.vector.memset(ad[:], 0.0).then_inc(s_z, 1)
            dve.wait_ge(s_wahi, 1)
            nc.vector.scalar_tensor_tensor(w[:, 1, :, D:D + 16], pg[:, 0, 0:32].rearrange("p (k n) -> p k n", k=KC), WSC,
                                           w[:, 0, :, D:D + 16], ALU.mult, ALU.subtract).then_inc(s_walo, 1)

        @block.tensor
        def _(pe):
            pe.wait_ge(s_aw, 17 * 16)
            for kc in range(KC):
                for kn in range(2):
                    last = nc.tensor.matmul(pg[:, 0, kc * 16:kc * 16 + 16], raw[:, kn, kc * P:(kc + 1) * P], ad[:, kn, :],
                                            start=(kn == 0), stop=(kn == 1))
            last.then_inc(s_wa, 1)
            pe.wait_ge(s_walo, 1)
            for t in range(NT):
                if t >= NB:
                    pe.wait_ge(s_ge, t - NB + 1)
                for n, (kc, a, b) in enumerate(prods):
                    last = nc.tensor.matmul(pg[:, t % NB, 0:D + 16], hT[:, a, kc, t * P:(t + 1) * P], w[:, b, kc, :],
                                            start=(n == 0), stop=(n == len(prods) - 1))
                last.then_inc(s_g, 1)
            for m, (c0, cn) in enumerate(CHUNKS):
                if m >= 2:
                    pe.wait_ge(s_elt, m - 1)
                for n, (kc, a, b) in enumerate(prods):
                    last = nc.tensor.matmul(pel[:, m % 2, 0:cn], w[:, a, kc, D:D + HEADS], hT[:, b, kc, c0:c0 + cn],
                                            start=(n == 0), stop=(n == len(prods) - 1))
                last.then_inc(s_elp, 1)

        @block.scalar
        def _(act):
            act.wait_ge(s_wa, 1)
            nc.scalar.activation(w[:, 0, :, D:D + 16], pg[:, 0, 0:32].rearrange("p (k n) -> p k n", k=KC), ACT.Copy,
                                 scale=WSC).then_inc(s_wahi, 1)
            for t in range(NT):
                act.wait_ge(s_g, t + 1)
                nc.scalar.activation(GE[:, t, :], pg[:, t % NB, 0:D + 16], ACT.Copy, scale=1.0 / PSC).then_inc(s_ge, 1)
            for m, (c0, cn) in enumerate(CHUNKS):
                act.wait_ge(s_elp, m + 1)
                if m >= 2:
                    act.wait_ge(s_out[m % 2], 16 * (m // 2))
                nc.scalar.activation(elT[:, m % 2, 0:cn], pel[:, m % 2, 0:cn], ACT.Copy, scale=1.0 / PSC).then_inc(s_elt, 1)


def gat_factors(k, xv_dram, HC, GE, spare):
    nc = k.nc
    s_red, s_rmax, s_fac, s_exp, s_f, s_xh, s_xl = (
        k.sem(f"s_x0_{n}") for n in ("red", "rmax", "fac", "exp", "f", "xh", "xl"))
    s_out = [k.sem(f"s_x0_out{i}") for i in range(2)]
    SL = NT * 2 * G1
    F = spare[:, 0:2 * SL].bitcast(F32).rearrange("p (s t d) -> p s t d", s=2, d=G1)
    X1 = spare[:, 2 * SL:4 * SL].rearrange("p (s t a d) -> p s t a d", s=2, a=2, d=G1)
    steps = [(f, h) for f in (1, 0) for h in range(HEADS)]
    er, el = GE[:, :, D + HEADS:D + 2 * HEADS], GE[:, :, D:D + HEADS]
    with ExitStack() as c:
        rm = k.sb(c, "x0_rm", [P, 2, HEADS], F32)
        vf = k.sb(c, "x0_vf", [P, 2, NT, HEADS], F32)
        dd = k.sb(c, "x0_dd", [P, 4, NT, HEADS], F32)
        block = c.enter_context(nc.Block())

        def split_out(n):
            return X1[:, n % 2]

        @block.sync
        def _(sp):
            for n, (f, h) in enumerate(steps):
                sp.wait_ge(s_xl, n + 1)
                sp.dma_start(xv_dram[f, h], split_out(n).rearrange("p t a d -> p (t a d)")).then_inc(s_out[n % 2], 16)
            for i in range(2):
                sp.wait_ge(s_out[i], 16 * len(steps) // 2)

        @block.scalar
        def _(act):
            act.wait_ge(s_fac, 1)
            nc.scalar.activation(vf[:, 1], dd[:, 0], ACT.Exp).then_inc(s_exp, 1)
            nc.scalar.activation(vf[:, 0], dd[:, 0], ACT.Exp, scale=SLOPE).then_inc(s_exp, 1)
            act.wait_ge(s_fac, 6)
            nc.scalar.activation(HC[:, :, 2, :].rearrange("p h t -> p t h"), dd[:, 1], ACT.Exp)
            nc.scalar.activation(HC[:, :, 3, :].rearrange("p h t -> p t h"), dd[:, 2], ACT.Exp)
            for n, (f, h) in enumerate(steps):
                act.wait_ge(s_f, 2 * (n + 1))
                if n >= 2:
                    act.wait_ge(s_out[n % 2], 16 * (n // 2))
                nc.scalar.activation(split_out(n)[:, :, 0, :], F[:, n % 2], ACT.Copy).then_inc(s_xh, 1)

        @block.gpsimd
        def _(pool):
            pool.wait_ge(s_red, 1)
            nc.gpsimd.partition_all_reduce(rm[:, 1, :], rm[:, 0, :], P, bass.bass_isa.ReduceOp.max).then_inc(s_rmax, 1)

        @block.vector
        def _(dve):
            nc.vector.tensor_reduce(rm[:, 0, :], er.rearrange("p t h -> p h t"), AX.X, ALU.max).then_inc(s_red, 1)
            nc.vector.tensor_scalar(HC[:, :, 0, :].rearrange("p h t -> p t h"), er, -1.0, None, ALU.mult)
            nc.vector.tensor_scalar(HC[:, :, 1, :].rearrange("p h t -> p t h"), er, STEP, None, ALU.mult)
            dve.wait_ge(s_rmax, 1)
            R = rm[:, 1, :].unsqueeze(1).to_broadcast([P, NT, HEADS])
            nc.vector.tensor_tensor(dd[:, 0], er, R, ALU.subtract).then_inc(s_fac, 1)
            nc.vector.tensor_tensor(dd[:, 1], el, R, ALU.add).then_inc(s_fac, 1)
            dve.wait_ge(s_fac, 2)
            nc.vector.tensor_scalar(dd[:, 2], dd[:, 1], SLOPE, None, ALU.mult).then_inc(s_fac, 1)
            dve.wait_ge(s_fac, 3)
            nc.vector.tensor_tensor(dd[:, 3], dd[:, 1], dd[:, 2], ALU.max).then_inc(s_fac, 1)
            dve.wait_ge(s_fac, 4)
            nc.vector.tensor_tensor(dd[:, 1], dd[:, 1], dd[:, 3], ALU.subtract).then_inc(s_fac, 1)
            nc.vector.tensor_tensor(dd[:, 2], dd[:, 2], dd[:, 3], ALU.subtract).then_inc(s_fac, 1)
            dve.wait_ge(s_exp, 2)
            nc.vector.tensor_scalar(vf[:], vf[:], VSC, None, ALU.mult).then_inc(s_fac, 1)
            dve.wait_ge(s_fac, 7)
            for n, (f, h) in enumerate(steps):
                if n >= 2:
                    dve.wait_ge(s_xl, n - 1)
                v = vf[:, f, :, h]
                nc.vector.tensor_tensor(F[:, n % 2, :, 0:HD], GE[:, :, h * HD:(h + 1) * HD],
                                        v.unsqueeze(2).to_broadcast([P, NT, HD]), ALU.mult).then_inc(s_f, 1)
                nc.vector.tensor_copy(F[:, n % 2, :, HD], v).then_inc(s_f, 1)
                if n >= 1:
                    dve.wait_ge(s_xh, n)
                    nc.vector.tensor_tensor(split_out(n - 1)[:, :, 1, :], F[:, (n - 1) % 2], split_out(n - 1)[:, :, 0, :],
                                            ALU.subtract).then_inc(s_xl, 1)
            n = len(steps) - 1
            dve.wait_ge(s_xh, n + 1)
            nc.vector.tensor_tensor(split_out(n)[:, :, 1, :], F[:, n % 2], split_out(n)[:, :, 0, :], ALU.subtract).then_inc(s_xl, 1)


GROUPS = [(0, 9), (9, 9), (18, 8)]
RING = 13
STEP_DVE = [2, 5, 7, 10, 12, 15, 17, 20, 22, 25]
STEP_ACT = [jt for jt in range(NT) if jt not in STEP_DVE]
STEP_SLOTS = ((STEP_ACT, 8, 0), (STEP_DVE, 5, 8))
STEP_RING = 13
AHEAD = 2
COPY_AT, COMBINE_AT = 4, 8


def step_slot(jt):
    for tiles, ring, base in STEP_SLOTS:
        if jt in tiles:
            n = tiles.index(jt)
            before = tiles[n - ring] if n >= ring else tiles[max(range(n, len(tiles), ring))] - NT
            return base + n % ring, before


def over_heads(eng, head):
    head(0, 0, False)
    with eng.Fori(0, HEADS // 2 - 1) as i:
        head(2 * i + 1, 1, True)
        head(2 * i + 2, 0, True)
    head(HEADS - 1, 1, True)


def gat_sums(k, group, el_dram, xv_dram, HC):
    nc = k.nc
    g0, gn = GROUPS[group]
    cols = gn * P
    tag = f"b{group}"
    s_mm, s_sel, s_rest, s_ca, s_cd, s_y, s_t, s_use = (
        k.sem(f"s_{tag}_{n}") for n in ("mm", "sel", "rest", "ca", "cd", "y", "t", "use"))
    s_in = [k.sem(f"s_{tag}_in{i}") for i in range(2)]
    TS = 5
    BANKS = -(-gn // 3)
    W = 4 * G1
    slot = lambda p, jt: (p * NT + jt) % RING
    with ExitStack() as c:
        xb = k.sb(c, f"{tag}_x", [P, 2, 2, NT, 2 * G1], F16)
        elr = k.sb(c, f"{tag}_el", [P, 2, cols], F32)
        hc = k.sb(c, f"{tag}_hc", [P, 2, 4, NT], F32)
        C = k.sb(c, f"{tag}_C", [P, STEP_RING, cols], FP8)
        B = k.sb(c, f"{tag}_B", [P, RING, cols], FP8)
        R = k.sb(c, f"{tag}_R", [P, RING, cols], FP8)
        Y = k.sb(c, f"{tag}_Y", [P, 2, gn, 4, G1], F32)
        S = k.sb(c, f"{tag}_S", [P, gn, 2, G1], F32)
        T = k.sb(c, f"{tag}_T", [P, gn, G1], F32)
        rd = k.sb(c, f"{tag}_rd", [P, gn], F32)
        pb = k.ps(c, f"{tag}_pb", [P, 2, 3, CH])
        block = c.enter_context(nc.Block())

        def step_free(eng, h, jt):
            eng.wait_ge(s_sel, h * NT + step_slot(jt)[1] + NT + 1)

        def compare(eng, h, p, jt, done):
            eng.tensor_scalar(C[:, step_slot(jt)[0], :].bitcast(U8), elr[:, p, :], hc[:, p, 0, jt:jt + 1], float(FP8_ONE),
                              ALU.is_gt, ALU.mult).then_inc(done, 1)

        @block.sync
        def _(sp):
            sp.wait_ge(k.s_adjT_out, 16)
            with sp.Fori(0, HEADS // 2) as i:
                for p in range(2):
                    h = 2 * i + p
                    sp.wait_ge(s_use, h + 1)
                    for f in range(2):
                        sp.dma_start(xb[:, p, f].rearrange("p t n -> p (t n)"),
                                     xv_dram[f, bass.ds(h, 1)].rearrange("h p n -> p (h n)")).then_inc(s_in[p], 16)
                    sp.dma_start(elr[:, p, :], el_dram[bass.ds(h, 1), g0 * P:g0 * P + cols].to_broadcast([P, cols])).then_inc(s_in[p], 16)
                    sp.dma_start(hc[:, p].rearrange("p f t -> p (f t)"),
                                 HC[:, bass.ds(h, 1)].rearrange("p h f t -> p (h f t)")).then_inc(s_in[p], 16)

        @block.scalar
        def _(act):
            def copy_sums(h, p, b):
                if b == 0:
                    act.wait_ge(s_mm, (h + 1) * NT + RING)
                    act.wait_ge(s_t, TS * h + 1)
                n = min(3, gn - 3 * b)
                last = nc.scalar.activation(Y[:, p, 3 * b:3 * b + n].rearrange("p t f d -> p (t f d)"),
                                            pb[:, p, b, 0:n * W], ACT.Copy)
                if b == BANKS - 1:
                    last.then_inc(s_y, 1)

            def head(h, p, previous):
                act.wait_ge(s_in[p], 32 * (h - p) + 64)
                for jt in range(NT):
                    if COPY_AT <= jt < COPY_AT + BANKS and previous:
                        copy_sums(h - 1, 1 - p, jt - COPY_AT)
                    if jt in STEP_ACT:
                        step_free(act, h, jt)
                        k.settle(act)
                        nc.scalar.activation(C[:, step_slot(jt)[0], :], elr[:, p, :], ACT.Sigmoid, bias=hc[:, p, 1, jt:jt + 1],
                                             scale=STEP, saturate=False).then_inc(s_ca, 1)

            act.sem_inc(s_y, 2)
            over_heads(act, head)
            for b in range(BANKS):
                copy_sums(HEADS - 1, 1, b)

        @block.gpsimd
        def _(pool):
            def head(h, p, previous):
                for jt in range(NT):
                    pool.wait_ge(s_sel, h * NT + jt + 1 + NT)
                    pool.wait_ge(s_mm, h * NT + jt + 1)
                    nc.gpsimd.tensor_tensor(R[:, slot(p, jt), :].bitcast(I32).rearrange("p (t w) -> p t w", t=gn),
                                            k.adjT[:, g0:g0 + gn, jt, :].bitcast(I32),
                                            B[:, slot(p, jt), :].bitcast(I32).rearrange("p (t w) -> p t w", t=gn),
                                            ALU.subtract).then_inc(s_rest, 1)

            over_heads(pool, head)

        @block.vector
        def _(dve):
            def combine(h, p, stage):
                v = TS * h + 2 * TS
                u, u1 = (hc[:, p, f, g0:g0 + gn].unsqueeze(2).to_broadcast([P, gn, G1]) for f in (2, 3))
                if stage > 0:
                    dve.wait_ge(s_t, v + stage)
                if stage == 0:
                    dve.wait_ge(s_y, h + 3)
                    for f in range(2):
                        last = nc.vector.tensor_tensor(S[:, :, f, :], Y[:, p, :, 2 * f, :], Y[:, p, :, 2 * f + 1, :], ALU.add)
                    last.then_inc(s_t, 1)
                elif stage == 1:
                    nc.vector.tensor_tensor(T[:], S[:, :, 0, :], u1, ALU.mult)
                    nc.vector.tensor_tensor(S[:, :, 1, :], S[:, :, 1, :], u, ALU.mult).then_inc(s_t, 1)
                elif stage == 2:
                    nc.vector.tensor_tensor(S[:, :, 0, :], T[:], S[:, :, 1, :], ALU.add).then_inc(s_t, 1)
                elif stage == 3:
                    nc.vector.reciprocal(rd[:], S[:, :, 0, HD]).then_inc(s_t, 1)
                elif stage == 4:
                    nc.vector.tensor_tensor(T[:, :, 0:HD], S[:, :, 0, 0:HD], rd[:].unsqueeze(2).to_broadcast([P, gn, HD]),
                                            ALU.mult).then_inc(s_t, 1)
                else:
                    xs = k.X[:, g0:g0 + gn, bass.ds(h * HD, HD)]
                    nc.vector.tensor_tensor(xs, xs, T[:, :, 0:HD], ALU.add).then_inc(s_use, 1)

            def head(h, p, previous):
                dve.wait_ge(s_in[p], 32 * (h - p) + 64)
                for jt in range(NT):
                    if COMBINE_AT <= jt <= COMBINE_AT + TS and previous:
                        combine(h - 1, 1 - p, jt - COMBINE_AT)
                    if jt + AHEAD in STEP_DVE:
                        step_free(dve, h, jt + AHEAD)
                        compare(nc.vector, h, p, jt + AHEAD, s_cd)
                    for tiles, done in ((STEP_ACT, s_ca), (STEP_DVE, s_cd)):
                        if jt in tiles:
                            dve.wait_ge(done, h * len(tiles) + tiles.index(jt) + 1)
                    c_in, b_out = C[:, step_slot(jt)[0], :], B[:, slot(p, jt), :]
                    dve.wait_ge(s_mm, h * NT + jt + 1)
                    nc.vector.tensor_tensor(b_out.bitcast(I32).rearrange("p (t w) -> p t w", t=gn),
                                            c_in.bitcast(I32).rearrange("p (t w) -> p t w", t=gn),
                                            k.adjT[:, g0:g0 + gn, jt, :].bitcast(I32), ALU.bitwise_and).then_inc(s_sel, 1)

            dve.sem_inc(s_use, 2)
            dve.sem_inc(s_t, 2 * TS)
            dve.sem_inc(s_sel, NT)
            over_heads(dve, head)
            for stage in range(TS + 1):
                combine(HEADS - 1, 1, stage)

        @block.tensor
        def _(pe):
            pe.sem_inc(s_mm, RING)
            with pe.Fori(0, HEADS // 2) as i:
                for p in range(2):
                    h = 2 * i + p
                    pe.wait_ge(s_in[p], 64 * i + 64)
                    pe.wait_ge(s_y, h + 1)
                    for jt in range(NT):
                        pe.wait_ge(s_sel, h * NT + jt + 1 + NT)
                        k.settle(pe)
                        for f, edges in ((1, B), (0, R)):
                            if f == 0:
                                pe.wait_ge(s_rest, h * NT + jt + 1)
                                k.settle(pe)
                            for t in range(gn):
                                b, r = t // 3, t % 3
                                last = nc.tensor.matmul(pb[:, p, b, (2 * r + f) * 2 * G1:(2 * r + f + 1) * 2 * G1],
                                                        edges[:, slot(p, jt), t * P:(t + 1) * P], xb[:, p, f, jt, :],
                                                        start=(jt == 0 and r == 0 and f == 1), stop=(jt == NT - 1),
                                                        skip_group_check=True)
                        last.then_inc(s_mm, 1)


def layer0(k, ap, adjT_dram):
    nc = k.nc
    el_dram = k.dram("el_dram", (HEADS, NP), F32)
    xv_dram = k.dram("xv_dram", (2, HEADS, P, NT * 2 * G1), F16)
    k.w_lin = ap["L0_gnn_W_lin"]
    with ExitStack() as c:
        HC = k.sb(c, "HC", [P, HEADS, 4, NT], F32)
        with ExitStack() as c1:
            w = k.sb(c1, "w_gat", [P, 2, KC, D + 16], F16)
            hT = k.sb(c1, "hT0", [P, 2 * KC * NP], F16)
            hTv = hT[:].rearrange("p (a k n) -> p a k n", a=2, k=KC)
            normalise(k, "n0", hTv, [(ap["L0_gnn_W_lin"], lambda part: w[:, part, :, 0:D])], adjT_dram=adjT_dram)
            with ExitStack() as c2:
                GE = k.sb(c2, "GE", [P, NT, D + 16], F32)
                gat_project(k, hTv, w, ap["L0_gnn_attn_w"], el_dram, GE)
                gat_factors(k, xv_dram, HC, GE, hT[:])
        for group in range(len(GROUPS)):
            gat_sums(k, group, el_dram, xv_dram, HC)



R_MIN = 1e-13
WHSC = 64.0
NSC = 4096.0
ESHIFT = 5.5
CT = 2
CW = CT * P
NC = NT // CT


def in_ring(jp, ring):
    return ring - 1 if jp == NC - 1 else jp % (ring - 1)


def prior_use(jp, ring):
    same = [j for j in range(NC) if in_ring(j, ring) == in_ring(jp, ring)]
    n = same.index(jp)
    return same[n - 1] + 1 + (NC if n else 0)


def over_chunks(eng, chunk):
    with eng.Fori(0, NC // 2) as i:
        chunk(2 * i, 0, False)
        chunk(2 * i + 1, 1, False)
    chunk(NC - 1, 0, True)


def step_ahead(c, q, jp, d, last):
    if jp + d < NC:
        return c, q, jp + d
    return None if last else (c + 1, 1 - q, jp + d - NC)


def cosine_project(k, hT, w, WnT, WHhi, WHlo, rcol, r_dram):
    nc = k.nc
    s_w, s_hi, s_lo, s_sm, s_sq, s_rt, s_rT, s_out, s_row, s_T, s_tp, s_th, s_tl = (
        k.sem(f"s_p1_{n}") for n in ("w", "hi", "lo", "sm", "sq", "rt", "rT", "out", "row", "T", "tp", "th", "tl"))
    prods = hi_lo_products(KC)
    slots = [(m, c0, cn) for c0, cn in CHUNKS for m in range(KC)]
    NB = 3
    with ExitStack() as c:
        n2 = k.sb(c, "p1_n2", [P, NT], F32)
        junk = k.sb(c, "p1_junk", [P, 2, D], F32)
        sm = k.sb(c, "p1_sm", [P, 4, NT], F32)
        rT = k.sb(c, "p1_rT", [NT, P], F32)
        rrow = k.sb(c, "p1_rrow", [P, 2, CH], F32)
        T = k.sb(c, "p1_T", [P, 2, CH], F32)
        pw = k.ps(c, "p1_pw", [P, NB, CH])
        pt = k.ps(c, "p1_pt", [P, NB, CH])
        pr = k.ps(c, "p1_pr", [P, CH])
        block = c.enter_context(nc.Block())
        s_rr = [k.sem(f"s_p1_rr{i}") for i in range(2)]

        @block.sync
        def _(sp):
            sp.wait_ge(s_rT, 1)
            sp.dma_start(r_dram.rearrange("(t p) -> t p", p=P), rT[:]).then_inc(s_out, 16)
            sp.wait_ge(s_out, 16)
            for m, (c0, cn) in enumerate(CHUNKS):
                if m >= 2:
                    sp.wait_ge(s_T, 2 * (m - 1))
                sp.dma_start(rrow[:, m % 2, 0:cn], r_dram[c0:c0 + cn].unsqueeze(0).to_broadcast([P, cn])).then_inc(s_rr[m % 2], 16)

        @block.tensor
        def _(pe):
            for t in range(NT):
                if t >= NB:
                    pe.wait_ge(s_lo, t - NB + 1)
                    pe.wait_ge(s_sq, t - NB + 1)
                for n, (kc, a, b) in enumerate(prods):
                    last = nc.tensor.matmul(pw[:, t % NB, 0:D], hT[:, a, kc, t * P:(t + 1) * P], w[:, b, kc, :],
                                            start=(n == 0), stop=(n == len(prods) - 1))
                last.then_inc(s_w, 1)
            for j, (m, c0, cn) in enumerate(slots):
                if j == 2:
                    pe.wait_ge(s_sm, 8)
                    nc.tensor.transpose(pr[0:NT, 0:P], rcol[:, 0, :], k.ident[:]).then_inc(s_rt, 1)
                if j >= NB:
                    pe.wait_ge(s_T, j - NB + 1)
                for n, (kc, a, b) in enumerate(prods):
                    last = nc.tensor.matmul(pt[:, j % NB, 0:cn], w[:, a, kc, m * P:(m + 1) * P], hT[:, b, kc, c0:c0 + cn],
                                            start=(n == 0), stop=(n == len(prods) - 1))
                last.then_inc(s_tp, 1)

        @block.scalar
        def _(act):
            for t in range(NT):
                act.wait_ge(s_w, t + 1)
                nc.scalar.activation(WHhi[:, t, 0:D], pw[:, t % NB, 0:D], ACT.Copy, scale=WHSC / PSC).then_inc(s_hi, 1)
                if t >= 2:
                    act.wait_ge(s_sq, t - 1)
                nc.scalar.activation(junk[:, t % 2, :], pw[:, t % NB, 0:D], ACT.Square, scale=1.0 / PSC,
                                     accum_out=n2[:, t:t + 1]).then_inc(s_sq, 1)
            act.wait_ge(s_sm, 1)
            nc.scalar.activation(sm[:, 1, :], sm[:, 0, :], ACT.Sqrt).then_inc(s_sm, 1)
            act.wait_ge(s_rt, 1)
            nc.scalar.activation(rT[:], pr[0:NT, 0:P], ACT.Copy).then_inc(s_rT, 1)
            for j, (m, c0, cn) in enumerate(slots):
                act.wait_ge(s_T, j + 1)
                nc.scalar.activation(WnT[:, 0, m, c0:c0 + cn], T[:, j % 2, 0:cn], ACT.Copy).then_inc(s_th, 1)

        @block.vector
        def _(dve):
            nc.vector.memset(WHhi[:, :, D], WHSC)
            for t in range(NT):
                dve.wait_ge(s_sq, t + 1)
                nc.vector.scalar_tensor_tensor(WHlo[:, t, :], pw[:, t % NB, 0:D], WHSC / PSC, WHhi[:, t, 0:D],
                                               ALU.mult, ALU.subtract).then_inc(s_lo, 1)
            dve.wait_ge(s_sq, NT)
            nc.vector.tensor_scalar(sm[:, 0, :], n2[:], R_MIN * R_MIN, None, ALU.max).then_inc(s_sm, 1)
            dve.wait_ge(s_sm, 2)
            nc.vector.reciprocal(sm[:, 2, :], sm[:, 1, :]).then_inc(s_sm, 1)
            dve.wait_ge(s_sm, 3)
            nc.vector.tensor_tensor(sm[:, 3, :], sm[:, 2, :], sm[:, 0, :], ALU.mult).then_inc(s_sm, 1)
            dve.wait_ge(s_sm, 4)
            nc.vector.tensor_tensor(sm[:, 3, :], sm[:, 3, :], sm[:, 2, :], ALU.mult).then_inc(s_sm, 1)
            dve.wait_ge(s_sm, 5)
            nc.vector.tensor_scalar(sm[:, 3, :], sm[:, 3, :], -0.5, 1.5, ALU.mult, ALU.add).then_inc(s_sm, 1)
            dve.wait_ge(s_sm, 6)
            nc.vector.tensor_tensor(rcol[:, 0, :], sm[:, 3, :], sm[:, 2, :], ALU.mult).then_inc(s_sm, 1)
            dve.wait_ge(s_sm, 7)
            nc.vector.tensor_scalar(rcol[:, 1, :], rcol[:, 0, :], NORM_EPS, None, ALU.mult).then_inc(s_sm, 1)
            nc.vector.tensor_scalar(k.ident8[:].bitcast(U8), k.ident[:], float(FP8_ONE), None, ALU.mult)
            for j, (m, c0, cn) in enumerate(slots):
                dve.wait_ge(s_tp, j + 1)
                dve.wait_ge(s_rr[(j // 2) % 2], 16 * (j // 4 + 1))
                if j >= 2:
                    dve.wait_ge(s_tl, j - 1)
                nc.vector.scalar_tensor_tensor(T[:, j % 2, 0:cn], pt[:, j % NB, 0:cn], NSC / PSC, rrow[:, (j // 2) % 2, 0:cn],
                                               ALU.mult, ALU.mult).then_inc(s_T, 1)
                dve.wait_ge(s_th, j + 1)
                nc.vector.tensor_tensor(WnT[:, 1, m, c0:c0 + cn], T[:, j % 2, 0:cn], WnT[:, 0, m, c0:c0 + cn],
                                        ALU.subtract).then_inc(s_tl, 1)


def cosine_attend(k, WnT, WHhi, WHlo, rcol, r_dram, adjT_dram, spare):
    nc = k.nc
    s_q, s_ln, s_cf, s_dot, s_t, s_e, s_em, s_hi, s_lo, s_mm, s_rd, s_x, s_own = (
        k.sem(f"s_c1_{n}") for n in ("q", "ln", "cf", "dot", "t", "e", "em", "hi", "lo", "mm", "rd", "x", "own"))
    s_in = [k.sem(f"s_c1_in{i}") for i in range(2)]
    prods = hi_lo_products(KC)
    RD, RC, RT, RE, RM, RS = 4, 3, 3, 3, 3, 7
    DOTS_AHEAD = 6
    FINISH_AT = 7
    W = 2 * CW
    with ExitStack() as c:
        Q1 = k.sb(c, "c1_Q", [P, NC, W], F32)
        Q = (spare.bitcast(F32).rearrange("p (j w) -> p j w", j=NC), Q1[:])
        CF = k.sb(c, "c1_CF", [P, RC, W], F32)
        T = k.sb(c, "c1_T", [P, RT, W], F32)
        E = k.sb(c, "c1_E", [P, RE, W], F32)
        EM = k.sb(c, "c1_EM", [P, RM, W], F32)
        rr = k.sb(c, "c1_rr", [P, 2, CW], F32)
        EH = k.sb(c, "c1_EH", [P, RS, W], F16)
        EL = k.sb(c, "c1_EL", [P, RS, W], F16)
        mv = k.sb(c, "c1_mv", [P, 2, 2, KC, CW], F16)
        ad = k.sb(c, "c1_ad", [P, 2, CT, NT, P], FP8)
        rden = k.sb(c, "c1_rden", [P, 2, CT], F32)
        shift = k.sb(c, "c1_shift", [P, 1], F32)
        pd = k.ps(c, "c1_pd", [P, RD, CH])
        pa = k.ps(c, "c1_pa", [P, 2, CT, CH])
        s_c = k.sem("s_c1_shift")
        block = c.enter_context(nc.Block())

        @block.sync
        def _(sp):
            def chunk(c, q, last):
                sp.wait_ge(s_em, (c + 1) * NC)
                sp.dma_start(mv[:, q].rearrange("p a k n -> p (a k) n"),
                             WnT[:, :, :, bass.ds(c * CW, CW)].rearrange("p a k n -> p (a k) n")).then_inc(s_in[q], 16)
                sp.dma_start(rr[:, q, :], r_dram[bass.ds(c * CW, CW)].unsqueeze(0).to_broadcast([P, CW])).then_inc(s_in[q], 16)
                sp.dma_start(ad[:, q].rearrange("p t j i -> p t (j i)").bitcast(U8),
                             adjT_dram[bass.ds(c * CT, CT)].rearrange("t p n -> p t n").bitcast(U8)).then_inc(s_in[q], 16)

            over_chunks(sp, chunk)

        def arrived(eng, c, q):
            eng.wait_ge(s_in[q], 24 * (c - q) + 48)

        @block.gpsimd
        def _(pool):
            nc.gpsimd.memset(shift[:], ESHIFT).then_inc(s_c, 1)

            def chunk(c, q, last):
                arrived(pool, c, q)
                pool.wait_ge(s_cf, (c + 1) * NC)
                k.settle(pool)
                for jp in range(NC):
                    for j in range(2):
                        ins = nc.gpsimd.tensor_scalar(Q[q][:, jp, j * CW:(j + 1) * CW], rr[:, q, :],
                                                      rcol[:, 1, 2 * jp + j:2 * jp + j + 1], 1.0, ALU.mult, ALU.add)
                ins.then_inc(s_q, 1)

            over_chunks(pool, chunk)

        @block.scalar
        def _(act):
            act.sem_inc(s_cf, 2 * NC)
            act.wait_ge(s_c, 1)

            def factor(c, q, jp):
                if jp == 0:
                    act.wait_ge(s_q, c + 1)
                    nc.scalar.activation(Q[q], Q[q], ACT.Ln).then_inc(s_ln, 1)
                    act.wait_ge(s_ln, c + 1)
                act.wait_ge(s_t, c * NC + prior_use(jp, RC))
                nc.scalar.activation(CF[:, in_ring(jp, RC), :], Q[q][:, jp, :], ACT.Exp, scale=-1.0).then_inc(s_cf, 1)

            def weight(c, q, jp):
                act.wait_ge(s_t, c * NC + jp + 1 + NC)
                act.wait_ge(s_em, (c + 1) * NC + prior_use(jp, RE))
                nc.scalar.activation(E[:, in_ring(jp, RE), :], T[:, in_ring(jp, RT), :], ACT.Exp, scale=1.0 / (NSC * NSC),
                                     bias=shift[:, 0:1]).then_inc(s_e, 1)

            def chunk(c, q, last):
                for jp in range(NC):
                    for d, what in ((2, factor), (1, weight)):
                        at_ = step_ahead(c, q, jp, d, last)
                        if at_:
                            what(*at_)

            factor(0, 0, 0)
            factor(0, 0, 1)
            weight(0, 0, 0)
            over_chunks(act, chunk)

        @block.vector
        def _(dve):
            dve.sem_inc(s_t, NC)
            dve.sem_inc(s_em, 2 * NC)
            dve.sem_inc(s_x, 2)

            def sim(c, q, jp):
                dve.wait_ge(s_cf, (c + 2) * NC + jp + 1)
                dve.wait_ge(s_dot, c * NC + jp + 1)
                dve.wait_ge(s_e, c * NC + prior_use(jp, RT))
                nc.vector.tensor_tensor(T[:, in_ring(jp, RT), :], pd[:, in_ring(jp, RD), :], CF[:, in_ring(jp, RC), :], ALU.mult).then_inc(s_t, 1)

            def select(c, q, jp):
                dve.wait_ge(s_e, c * NC + jp + 1 + NC)
                dve.wait_ge(s_lo, c * NC + prior_use(jp, RM))
                k.settle(dve)
                nc.vector.tensor_tensor(EM[:, in_ring(jp, RM), :].rearrange("p (j t i) -> p j t i", j=2, t=CT),
                                        E[:, in_ring(jp, RE), :].rearrange("p (j t i) -> p j t i", j=2, t=CT),
                                        ad[:, q, :, 2 * jp:2 * jp + 2, :].rearrange("p t j i -> p j t i"), ALU.mult).then_inc(s_em, 1)

            def high(c, q, jp):
                dve.wait_ge(s_em, (c + 2) * NC + jp + 1)
                dve.wait_ge(s_mm, c * NC + prior_use(jp, RS))
                nc.vector.tensor_copy(EH[:, in_ring(jp, RS), :], EM[:, in_ring(jp, RM), :]).then_inc(s_hi, 1)

            def low(c, q, jp):
                dve.wait_ge(s_hi, c * NC + jp + 1)
                nc.vector.tensor_tensor(EL[:, in_ring(jp, RS), :], EM[:, in_ring(jp, RM), :], EH[:, in_ring(jp, RS), :],
                                        ALU.subtract).then_inc(s_lo, 1)

            def finish(c, q):
                dve.wait_ge(s_mm, (c + 1) * NC + NC)
                nc.vector.reciprocal(rden[:, q, :], pa[:, q, :, D]).then_inc(s_rd, 1)
                dve.wait_ge(s_rd, c + 1)
                for t in range(CT):
                    xs = k.X[:, bass.ds(c * CT + t, 1), :].rearrange("p t d -> p (t d)")
                    ins = nc.vector.scalar_tensor_tensor(xs, pa[:, q, t, 0:D], rden[:, q, t:t + 1], xs, ALU.mult, ALU.add)
                ins.then_inc(s_x, 1)

            def chunk(c, q, last, first=False):
                arrived(dve, c, q)
                for t in range(CT):
                    own = ad[:, q, t, bass.ds(c * CT + t, 1), :].rearrange("p t i -> p (t i)").bitcast(I32)
                    ins = nc.vector.tensor_tensor(own, own, k.ident8[:].bitcast(I32), ALU.bitwise_or)
                ins.then_inc(s_own, 1)
                dve.wait_ge(s_own, c + 1)
                for jp in range(NC):
                    if jp == FINISH_AT and not first:
                        finish(c - 1, 1 - q)
                    ahead = step_ahead(c, q, jp, 1, last)
                    if ahead:
                        sim(*ahead)
                    select(c, q, jp)
                    if jp > 0:
                        low(c, q, jp - 1)
                    elif not first:
                        low(c - 1, 1 - q, NC - 1)
                    high(c, q, jp)

            dve.sem_inc(s_lo, NC)
            sim(0, 0, 0)
            chunk(0, 0, False, True)
            with dve.Fori(0, NC // 2 - 1) as i:
                chunk(2 * i + 1, 1, False)
                chunk(2 * i + 2, 0, False)
            chunk(NC - 2, 1, False)
            chunk(NC - 1, 0, True)
            low(NC - 1, 0, NC - 1)
            finish(NC - 1, 0)

        @block.tensor
        def _(pe):
            pe.sem_inc(s_mm, NC)
            pe.sem_inc(s_e, NC)

            def dots(c, q, jp):
                if jp == 0:
                    arrived(pe, c, q)
                pe.wait_ge(s_t, c * NC + prior_use(jp, RD))
                for j in range(2):
                    jt = 2 * jp + j
                    for n, (kc, a, b) in enumerate(prods):
                        last = nc.tensor.matmul(pd[:, in_ring(jp, RD), j * CW:(j + 1) * CW], WnT[:, a, kc, jt * P:(jt + 1) * P],
                                                mv[:, q, b, kc, :], start=(n == 0), stop=(n == len(prods) - 1))
                last.then_inc(s_dot, 1)

            def sums(c, q, jp):
                if jp == 0:
                    pe.wait_ge(s_x, c + 1)
                pe.wait_ge(s_lo, c * NC + jp + 1 + NC)
                for j in range(2):
                    jt = 2 * jp + j
                    for t in range(CT):
                        col = j * CW + t * P
                        first, final = jt == 0, jt == NT - 1
                        hi, lo = EH[:, in_ring(jp, RS), col:col + P], EL[:, in_ring(jp, RS), col:col + P]
                        nc.tensor.matmul(pa[:, q, t, 0:D + 1], hi, WHhi[:, jt, :], start=first, stop=False, skip_group_check=True)
                        nc.tensor.matmul(pa[:, q, t, 0:D], hi, WHlo[:, jt, :], start=False, stop=False, skip_group_check=True)
                        last = nc.tensor.matmul(pa[:, q, t, 0:D + 1], lo, WHhi[:, jt, :], start=False, stop=final, skip_group_check=True)
                last.then_inc(s_mm, 1)

            def chunk(c, q, last):
                for jp in range(NC):
                    ahead = step_ahead(c, q, jp, DOTS_AHEAD, last)
                    if ahead:
                        dots(*ahead)
                    sums(c, q, jp)

            for jp in range(DOTS_AHEAD):
                dots(0, 0, jp)
            over_chunks(pe, chunk)


def layer1(k, ap, adjT_dram):
    with ExitStack() as c:
        r_dram = k.dram("r_dram", (NP,), F32)
        w = k.sb(c, "w_cos", [P, 2, KC, D], F16)
        rcol = k.sb(c, "rcol", [P, 2, NT], F32)
        k.ident8 = k.sb(c, "ident8", [P, P], FP8)
        hT = k.sb(c, "hT1", [P, 2 * KC * NP], F16)
        hTv = hT[:].rearrange("p (a k n) -> p a k n", a=2, k=KC)
        normalise(k, "n1", hTv, [(ap["L1_gnn_W"], lambda part: w[:, part, :, :])])
        WnT = k.sb(c, "WnT", [P, 2, KC, NP], F16)
        WHhi = k.sb(c, "WHhi", [P, NT, D + 1], F16)
        WHlo = k.sb(c, "WHlo", [P, NT, D], F16)
        cosine_project(k, hTv, w, WnT, WHhi, WHlo, rcol, r_dram)
        cosine_attend(k, WnT, WHhi, WHlo, rcol, r_dram, adjT_dram, hT[:])



KROWS = 3 * HD + 2
QKSC = 1024.0
SHARP = 2.0 ** 20
MASK = 2.0 ** 60
SCH = 4
SW = NP // SCH
SB = SW // 2
NB2 = NP // (2 * P)
TA = 8
RESULT_AT = 2


def hard_project(k, ap, hT, w, QT, KT, KS, Vhl, q_dram):
    nc = k.nc
    s_in, s_v, s_vh, s_vl, s_p, s_T, s_hi, s_lo, s_we, s_be, s_st = (
        k.sem(f"s_p2_{n}") for n in ("in", "v", "vh", "vl", "p", "T", "hi", "lo", "we", "be", "st"))
    prods = hi_lo_products(KC)
    NB = 3
    slots = [(s, m, c0, cn) for s in range(2) for m in range(KC) for c0, cn in CHUNKS]
    with ExitStack() as c:
        T = k.sb(c, "p2_T", [P, 2, CH], F32)
        we = k.sb(c, "p2_we", [P, 2], F32)
        be = k.sb(c, "p2_be", [KROWS, 4], F32)
        beh = k.sb(c, "p2_beh", [KROWS, 1], F16)
        pv = k.ps(c, "p2_pv", [P, NB, CH])
        pt = k.ps(c, "p2_pt", [P, NB, CH])
        block = c.enter_context(nc.Block())
        B0 = 3 * HD

        @block.sync
        def _(sp):
            for q in range(P // HD):
                sp.dma_start(we[q * HD:(q + 1) * HD, 0:1], ap["L2_gnn_we"].rearrange("o d -> d o")).then_inc(s_in, 16)
            sp.dma_start(be[B0:KROWS, 0:1], ap["L2_gnn_be"].unsqueeze(0).to_broadcast([2, 1])).then_inc(s_in, 16)
            for s, src in ((0, KT), (1, QT)):
                for m in range(KC):
                    sp.wait_ge(s_lo, len(CHUNKS) * (s * KC + m + 1))
                    for q in range(4):
                        for r in range(3):
                            part = (0, 0, 1)[r] if s == 0 else (0, 1, 0)[r]
                            rows = slice(r * HD, (r + 1) * HD)
                            dst = KS[rows, 4 * m + q, :] if s == 0 else q_dram[rows, 4 * m + q, :]
                            sp.dma_start(dst, src[q * HD:(q + 1) * HD, part, m, :]).then_inc(s_st, 16)
            sp.wait_ge(s_st, 16 * 2 * HEADS * 3)

        @block.gpsimd
        def _(pool):
            pool.wait_ge(s_be, 4)
            nc.gpsimd.tensor_copy(KS[B0:KROWS].rearrange("p h n -> p (h n)"), be[B0:KROWS, 3:4].to_broadcast([2, HEADS * NP]))

        @block.vector
        def _(dve):
            dve.wait_ge(s_in, 16 * (P // HD + 1))
            nc.vector.tensor_scalar(we[:, 1:2], we[:, 0:1], QKSC, None, ALU.mult).then_inc(s_we, 1)
            nc.vector.tensor_scalar(be[B0:KROWS, 1:2], be[B0:KROWS, 0:1], QKSC, None, ALU.mult).then_inc(s_be, 1)
            dve.wait_ge(s_be, 1)
            nc.vector.tensor_copy(beh[B0:KROWS], be[B0:KROWS, 1:2]).then_inc(s_be, 1)
            dve.wait_ge(s_be, 2)
            nc.vector.tensor_tensor(be[B0:KROWS, 2:3], beh[B0:KROWS], k.ident[B0:KROWS, B0 + 1:B0 + 2], ALU.mult).then_inc(s_be, 1)
            dve.wait_ge(s_be, 3)
            nc.vector.tensor_tensor(be[B0:KROWS, 3:4], be[B0:KROWS, 1:2], be[B0:KROWS, 2:3], ALU.subtract).then_inc(s_be, 1)
            dve.wait_ge(s_we, 1)
            for j, (s, m, c0, cn) in enumerate(slots):
                dve.wait_ge(s_p, j + 1)
                if j >= 2:
                    dve.wait_ge(s_lo, j - 1)
                if s == 0:
                    nc.vector.tensor_scalar(T[:, j % 2, 0:cn], pt[:, j % NB, 0:cn], HD ** -0.5 * QKSC / PSC, we[:, 1:2],
                                            ALU.mult, ALU.add).then_inc(s_T, 1)
                else:
                    nc.vector.tensor_scalar(T[:, j % 2, 0:cn], pt[:, j % NB, 0:cn], QKSC / PSC, None, ALU.mult).then_inc(s_T, 1)
                dst = (KT, QT)[s]
                dve.wait_ge(s_hi, j + 1)
                nc.vector.tensor_tensor(dst[:, 1, m, c0:c0 + cn], T[:, j % 2, 0:cn], dst[:, 0, m, c0:c0 + cn],
                                        ALU.subtract).then_inc(s_lo, 1)
            for t in range(NT):
                b, e = t // 2, t % 2
                dve.wait_ge(s_vh, t + 1)
                nc.vector.scalar_tensor_tensor(Vhl[:, b, e, :, HD:2 * HD], pv[:, t % NB, 0:D].rearrange("p (h d) -> p h d", d=HD),
                                               QKSC / HEADS / PSC, Vhl[:, b, e, :, 0:HD], ALU.mult, ALU.subtract).then_inc(s_vl, 1)

        @block.scalar
        def _(act):
            for j, (s, m, c0, cn) in enumerate(slots):
                act.wait_ge(s_T, j + 1)
                nc.scalar.activation((KT, QT)[s][:, 0, m, c0:c0 + cn], T[:, j % 2, 0:cn], ACT.Copy).then_inc(s_hi, 1)
            for t in range(NT):
                act.wait_ge(s_v, t + 1)
                nc.scalar.activation(Vhl[:, t // 2, t % 2, :, 0:HD], pv[:, t % NB, 0:D].rearrange("p (h d) -> p h d", d=HD),
                                     ACT.Copy, scale=QKSC / HEADS / PSC).then_inc(s_vh, 1)

        @block.tensor
        def _(pe):
            for j, (s, m, c0, cn) in enumerate(slots):
                if j >= NB:
                    pe.wait_ge(s_T, j - NB + 1)
                for n, (kc, a, b) in enumerate(prods):
                    last = nc.tensor.matmul(pt[:, j % NB, 0:cn], w[:, 1 - s, a, kc, m * P:(m + 1) * P], hT[:, b, kc, c0:c0 + cn],
                                            start=(n == 0), stop=(n == len(prods) - 1))
                last.then_inc(s_p, 1)
            for t in range(NT):
                blk, e = t // 2, t % 2
                if t >= NB:
                    pe.wait_ge(s_vl, t - NB + 1)
                for n, (kc, a, b) in enumerate(prods):
                    nodes = hT[:, a, kc, blk * 2 * P:(blk + 1) * 2 * P].rearrange("p (n e) -> p n e", e=2)[:, :, e]
                    last = nc.tensor.matmul(pv[:, t % NB, 0:D], nodes, w[:, 2, b, kc, :], start=(n == 0), stop=(n == len(prods) - 1))
                last.then_inc(s_v, 1)


def over_tiles(eng, tile):
    with eng.Fori(0, NT // 2 - 1) as i:
        tile(2 * i, 0, False)
        tile(2 * i + 1, 1, False)
    tile(NT - 2, 0, False)
    tile(NT - 1, 1, True)


def head_ahead(i, q, h, d, last):
    if h + d < HEADS:
        return i, q, h + d
    return None if last else (i + 1, 1 - q, h + d - HEADS)


def hard_attend(k, adj_dram, KS, Vhl, q_dram):
    nc = k.nc
    s_pad, s_nb, s_sc, s_tt, s_mx, s_hA, s_hB, s_trA, s_trB, s_evA, s_evB, s_av, s_x, s_r = (
        k.sem(f"s_h2_{n}") for n in ("pad", "nb", "sc", "tt", "mx", "hA", "hB", "trA", "trB", "evA", "evB", "av", "x", "r"))
    s_rows = [k.sem(f"s_h2_rows{i}") for i in range(2)]
    s_q = [k.sem(f"s_h2_q{i}") for i in range(2)]
    with ExitStack() as c:
        rows = k.sb(c, "h2_rows", [P, 2, NP], I32)
        off = k.sb(c, "h2_off", [P, 2, NP], F32)
        S = k.sb(c, "h2_S", [P, 2, NP], F32)
        H = k.sb(c, "h2_H", [P, 2 * NP], FP8)
        HT = k.sb(c, "h2_HT", [P, 2 * NP], FP8)
        QS = k.sb(c, "h2_QS", [KROWS, 2, HEADS, P], F16)
        mx = k.sb(c, "h2_mx", [P, 2, SCH], F32)
        nmx = k.sb(c, "h2_nmx", [P, 2], F32)
        ps = k.ps(c, "h2_ps", [P, 2, 2, CH])
        pT = k.ps(c, "h2_pT", [P, 2, 1024], BF16)
        po = k.ps(c, "h2_po", [P, 2, CH])
        block = c.enter_context(nc.Block())
        g_of = lambda i, h: i * HEADS + h

        @block.sync
        def _(sp):
            def load(i, s):
                sp.wait_ge(s_nb, i + 1)
                k.settle(sp)
                sp.dma_start(rows[:, s, 0:N], adj_dram[bass.ds(i * P, P), :]).then_inc(s_rows[s], 16)
                load_q(i, s)

            def load_q(i, s):
                sp.wait_ge(s_x, i + 1)
                k.settle(sp)
                sp.dma_start(QS[0:3 * HD, s], q_dram[:, :, bass.ds(i * P, P)]).then_inc(s_q[s], 16)

            sp.wait_ge(s_pad, 2)
            with sp.Fori(0, NT // 2 - 1) as i:
                load(2 * i, 0)
                load(2 * i + 1, 1)
            load(NT - 2, 0)
            sp.wait_ge(s_pad, 3)
            sp.dma_start(rows[0:LAST, 1, 0:N], adj_dram[(NT - 1) * P:N, :]).then_inc(s_rows[1], 16)
            load_q(NT - 1, 1)

        @block.gpsimd
        def _(pool):
            nc.gpsimd.memset(QS[3 * HD:KROWS], QKSC).then_inc(s_pad, 1)
            pool.wait_ge(s_pad, 1)
            nc.gpsimd.memset(rows[:, :, N:NP], 0).then_inc(s_pad, 1)
            pool.sem_inc(s_nb, 2)

            def offsets(i, s):
                pool.wait_ge(s_rows[s], 8 * (i - s) + 16)
                pool.wait_ge(s_x, i + 1)
                k.settle(pool)
                nc.gpsimd.tensor_scalar(off[:, s, :], rows[:, s, :], -1.0, MASK, ALU.add, ALU.mult).then_inc(s_nb, 1)

            pool.wait_ge(s_pad, 2)
            with pool.Fori(0, NT // 2 - 1) as i:
                offsets(2 * i, 0)
                offsets(2 * i + 1, 1)
            pool.wait_ge(s_nb, NT)
            nc.gpsimd.memset(rows[96:P, 1, :], 0).then_inc(s_pad, 1)
            pool.wait_ge(s_pad, 3)
            offsets(NT - 2, 0)
            offsets(NT - 1, 1)

        @block.tensor
        def _(pe):
            pe.sem_inc(s_trA, 2)
            pe.sem_inc(s_trB, 2)
            pe.sem_inc(s_av, 2)

            def scores(i, q, h, chunks):
                for ch in chunks:
                    if h == 0 and ch == 0:
                        pe.wait_ge(s_q[q], 8 * (i - q) + 16)
                    pe.wait_ge(s_tt, g_of(i, h) * SCH + ch + 1)
                    for b in range(2):
                        c0 = ch * SW + b * SB
                        last = nc.tensor.matmul(ps[:, ch % 2, b, 0:SB], QS[:, q, h, :], KS[:, h, c0:c0 + SB], start=True, stop=True)
                    last.then_inc(s_sc, 1)

            def transposes(i, q, h):
                g = g_of(i, h)
                for part, (b0, b1), written, free, done in ((0, (0, TA), s_hA, s_evA, s_trA), (1, (TA, NB2), s_hB, s_evB, s_trB)):
                    pe.wait_ge(written, g + 3)
                    pe.wait_ge(free, g + 1)
                    for b in range(b0, b1):
                        src = H[:, (h % 2) * NP + b * 2 * P:(h % 2) * NP + (b + 1) * 2 * P].bitcast(BF16)
                        last = nc.tensor.transpose(pT[:, part, (b - b0) * P:(b - b0 + 1) * P], src, k.ident16[:])
                    last.then_inc(done, 1)

            def sums(i, q, h):
                g = g_of(i, h)
                if h == 0:
                    pe.wait_ge(s_x, i + 1)
                pe.wait_ge(s_evA, g + 2)
                pe.wait_ge(s_evB, g + 2)
                k.settle(pe)
                wt = HT[:, (h % 2) * NP:(h % 2 + 1) * NP].rearrange("p (b i e) -> p b i e", b=NB2, e=2)
                for b in range(NB2):
                    for e in range(2):
                        last = nc.tensor.matmul(po[:, q, h * 2 * HD:(h + 1) * 2 * HD], wt[:, b, :, e], Vhl[:, b, e, h, :],
                                                start=(b == 0 and e == 0), stop=(b == NB2 - 1 and e == 1), skip_group_check=True)
                last.then_inc(s_av, 1)

            def steps(i, q, h, last):
                s1, s2, s3 = (head_ahead(i, q, h, d, last) for d in (1, 2, 3))
                if s2:
                    scores(*s2, range(1, 3))
                sums(i, q, h)
                if s2:
                    scores(*s2, range(3, SCH))
                if s3:
                    scores(*s3, range(1))
                if s1:
                    transposes(*s1)

            scores(0, 0, 0, range(SCH))
            scores(0, 0, 1, range(SCH))
            scores(0, 0, 2, range(1))
            transposes(0, 0, 0)
            over_tiles(pe, lambda i, q, last: [steps(i, q, h, last) for h in range(HEADS)])

        @block.scalar
        def _(act):
            act.sem_inc(s_hA, 2)
            act.sem_inc(s_hB, 2)
            act.sem_inc(s_evA, 1)

            def weights(i, q, h):
                g = g_of(i, h)
                act.wait_ge(s_mx, g + 1)
                for (c0, c1), free, done in (((0, TA * 2 * P), s_trA, s_hA), ((TA * 2 * P, NP), s_trB, s_hB)):
                    act.wait_ge(free, g + 1)
                    k.settle(act)
                    nc.scalar.activation(H[:, (h % 2) * NP + c0:(h % 2) * NP + c1], S[:, h % 2, c0:c1], ACT.Exp,
                                         bias=nmx[:, h % 2:h % 2 + 1], scale=1.0, saturate=False).then_inc(done, 1)

            def evacuate(i, q, h):
                g = g_of(i, h)
                act.wait_ge(s_trA, g + 3)
                act.wait_ge(s_av, g + 1)
                dst = HT[:, (h % 2) * NP:(h % 2) * NP + TA * 2 * P]
                nc.scalar.activation(dst.bitcast(U16), pT[:, 0, :].bitcast(U16), ACT.Copy).then_inc(s_evA, 1)

            def steps(i, q, h, last):
                weights(i, q, h)
                evacuate(i, q, h)

            over_tiles(act, lambda i, q, last: [steps(i, q, h, last) for h in range(HEADS)])

        @block.vector
        def _(dve):
            dve.sem_inc(s_tt, 2)
            dve.sem_inc(s_evB, 1)
            dve.sem_inc(s_x, 2)

            def maxima(i, q, h, chunks):
                g = g_of(i, h)
                for ch in chunks:
                    if h == 0 and ch == 0:
                        dve.wait_ge(s_nb, i + 3)
                    if ch == 0:
                        dve.wait_ge(s_hA, g + 1)
                    if ch == 2:
                        dve.wait_ge(s_hB, g + 1)
                    dve.wait_ge(s_sc, g * SCH + ch + 1)
                    k.settle(dve)
                    two = lambda x: x.rearrange("p (b n) -> p b n", b=2)
                    nc.vector.tensor_tensor_reduce(out=two(S[:, h % 2, ch * SW:(ch + 1) * SW]), in0=ps[:, ch % 2, :, 0:SB],
                                                   in1=two(off[:, q, ch * SW:(ch + 1) * SW]), scale=SHARP, scalar=-3e38,
                                                   op0=ALU.add, op1=ALU.max, accum_out=mx[:, h % 2, ch:ch + 1]).then_inc(s_tt, 1)

            def maximum(i, q, h):
                dve.wait_ge(s_tt, (g_of(i, h) + 1) * SCH + 2)
                nc.vector.tensor_reduce(nmx[:, h % 2:h % 2 + 1], mx[:, h % 2, :], AX.X, ALU.max, negate=True).then_inc(s_mx, 1)

            def evacuate(i, q, h):
                g = g_of(i, h)
                dve.wait_ge(s_trB, g + 3)
                dve.wait_ge(s_av, g + 1)
                dst = HT[:, (h % 2) * NP + TA * 2 * P:(h % 2 + 1) * NP]
                nc.vector.tensor_scalar(dst.bitcast(I32), pT[:, 1, 0:(NB2 - TA) * P].bitcast(I32), 0, None,
                                        ALU.bitwise_or).then_inc(s_evB, 1)

            def result(i, q):
                dve.wait_ge(s_av, i * HEADS + HEADS + 2)
                xs = k.X[:, bass.ds(i, 1), :].rearrange("p t (h d) -> p (t h) d", d=HD)
                both = po[:, q, :].rearrange("p (h a d) -> p h a d", a=2, d=HD)
                nc.vector.scalar_tensor_tensor(xs, both[:, :, 0, :], 1.0 / QKSC, xs, ALU.mult, ALU.add).then_inc(s_r, 1)
                dve.wait_ge(s_r, i + 1)
                nc.vector.scalar_tensor_tensor(xs, both[:, :, 1, :], 1.0 / QKSC, xs, ALU.mult, ALU.add).then_inc(s_x, 1)

            def steps(i, q, h, last, first=False):
                s1, s2 = (head_ahead(i, q, h, d, last) for d in (1, 2))
                if s1:
                    maxima(*s1, range(1, SCH))
                if s2:
                    maxima(*s2, range(1))
                if s1:
                    maximum(*s1)
                evacuate(i, q, h)
                if h == RESULT_AT and not first:
                    result(i - 1, 1 - q)

            maxima(0, 0, 0, range(SCH))
            maxima(0, 0, 1, range(1))
            maximum(0, 0, 0)
            for h in range(HEADS):
                steps(0, 0, h, False, True)
            with dve.Fori(0, NT // 2 - 1) as i:
                for h in range(HEADS):
                    steps(2 * i + 1, 1, h, False)
                for h in range(HEADS):
                    steps(2 * i + 2, 0, h, False)
            for h in range(HEADS):
                steps(NT - 1, 1, h, True)
            result(NT - 1, 1)


def layer2(k, ap):
    with ExitStack() as c:
        q_dram = k.dram("q_dram", (3 * HD, HEADS, NP), F16)
        KS = k.sb(c, "KS", [KROWS, HEADS, NP], F16)
        Vhl = k.sb(c, "Vhl", [P, NB2, 2, HEADS, 2 * HD], F16)
        with ExitStack() as c1:
            w = k.sb(c1, "w_hard", [P, 3, 2, KC, D], F16)
            hT = k.sb(c1, "hT2", [P, 2, KC, NP], F16)
            part_of = lambda i: lambda part: w[:, i, part, :, :]
            normalise(k, "n2", hT, [(ap[f"L2_gnn_W{n}"], part_of(i)) for i, n in enumerate("QKV")])
            QT = k.sb(c1, "QT", [P, 2, KC, NP], F16)
            KT = k.sb(c1, "KT", [P, 2, KC, NP], F16)
            hard_project(k, ap, hT, w, QT, KT, KS, Vhl, q_dram)
        hard_attend(k, ap["adj"], KS, Vhl, q_dram)




def mean_weights(k, ap, m, bias, ideg_dram):
    nc = k.nc
    s_in, s_tr, s_cp, s_bb, s_mm, s_hi, s_deg, s_rT, s_out, s_b = (
        k.sem(f"s_w3_{n}") for n in ("in", "tr", "cp", "bb", "mm", "hi", "deg", "rT", "out", "b"))
    with ExitStack() as c:
        raw = k.sb(c, "w3_raw", [P, 2, KC, D], F32)
        wt = k.sb(c, "w3_t", [P, 2, KC, D], F32)
        comb = k.sb(c, "w3_comb", [P, 2, KC, D], F32)
        bcol = k.sb(c, "w3_bcol", [P, 2, KC], F32)
        bb = k.sb(c, "w3_bb", [P, 2, KC, P], F32)
        bc = k.sb(c, "w3_bc", [P, D], F32)
        dg = k.sb(c, "w3_deg", [P, 2, NT], F32)
        dT = k.sb(c, "w3_degT", [NT, P], F32)
        pt = k.ps(c, "w3_pt", [P, 2, CH])
        pm = k.ps(c, "w3_pm", [P, 2, CH])
        pb = k.ps(c, "w3_pb", [P, CH])
        pd = k.ps(c, "w3_pd", [P, CH])
        block = c.enter_context(nc.Block())
        srcs = [(ap["L3_gnn_W_self"], ap["L3_gnn_b_self"]), (ap["L3_gnn_W_nb"], ap["L3_gnn_b_nb"])]
        LOADS = 2 * (1 + KC) + 2

        @block.sync
        def _(sp):
            for s, (w, b) in enumerate(srcs):
                sp.dma_start(raw[:, s], w.rearrange("(k p) c -> p k c", p=P)).then_inc(s_in, 16)
                for kc in range(KC):
                    sp.dma_start(bcol[:, s, kc:kc + 1], b[kc * P:(kc + 1) * P].rearrange("(p o) -> p o", o=1)).then_inc(s_in, 16)
            sp.dma_start(comb[:].rearrange("p s k c -> p (s k) c"),
                         ap["L3_gnn_W_comb"].rearrange("(k p) c -> p k c", p=P)).then_inc(s_in, 16)
            sp.dma_start(bc[:], ap["L3_gnn_b_comb"].unsqueeze(0).to_broadcast([P, D])).then_inc(s_in, 16)
            sp.wait_ge(s_rT, 1)
            sp.dma_start(ideg_dram.rearrange("(t p) -> t p", p=P), dT[:]).then_inc(s_out, 16)
            sp.wait_ge(s_out, 16)

        @block.vector
        def _(dve):
            nc.vector.tensor_tensor(dg[:, 1, :], k.deg[:, 0, :], k.deg[:, 1, :], ALU.add).then_inc(s_deg, 1)
            dve.wait_ge(s_deg, 1)
            nc.vector.tensor_scalar(dg[:, 0, :], dg[:, 1, :], 1.0, None, ALU.max).then_inc(s_deg, 1)
            dve.wait_ge(s_deg, 2)
            nc.vector.reciprocal(dg[:, 1, :], dg[:, 0, :]).then_inc(s_deg, 1)
            dve.wait_ge(s_in, 16 * LOADS)
            nc.vector.tensor_copy(bb[:], bcol[:].unsqueeze(3).to_broadcast([P, 2, KC, P])).then_inc(s_bb, 1)
            for s in range(2):
                dve.wait_ge(s_hi, s + 1)
                nc.vector.scalar_tensor_tensor(m[:, 1, s], pm[:, s, :].rearrange("p (k n) -> p k n", k=KC), WSC, m[:, 0, s],
                                               ALU.mult, ALU.subtract)
            dve.wait_ge(s_b, 1)
            nc.vector.tensor_tensor(bias[:], pb[:, 0:D], bc[:], ALU.add)

        @block.tensor
        def _(pe):
            pe.wait_ge(s_deg, 3)
            nc.tensor.transpose(pd[0:NT, 0:P], dg[:, 1, :], k.ident[:]).then_inc(s_tr, 1)
            pe.wait_ge(s_in, 16 * LOADS)
            for s in range(2):
                for kc in range(KC):
                    for kn in range(KC):
                        last = nc.tensor.transpose(pt[:, s, kc * D + kn * P:kc * D + (kn + 1) * P],
                                                   raw[:, s, kn, kc * P:(kc + 1) * P], k.ident[:])
                last.then_inc(s_tr, 1)
            for s in range(2):
                pe.wait_ge(s_cp, s + 1)
                for kn in range(KC):
                    for kc in range(KC):
                        last = nc.tensor.matmul(pm[:, s, kn * D:(kn + 1) * D], wt[:, s, kc, kn * P:(kn + 1) * P], comb[:, s, kc, :],
                                                start=(kc == 0), stop=(kc == KC - 1))
                last.then_inc(s_mm, 1)
            pe.wait_ge(s_bb, 1)
            for n, (s, kc) in enumerate([(s, kc) for s in range(2) for kc in range(KC)]):
                last = nc.tensor.matmul(pb[:, 0:D], bb[:, s, kc, :], comb[:, s, kc, :], start=(n == 0), stop=(n == 2 * KC - 1))
            last.then_inc(s_b, 1)

        @block.scalar
        def _(act):
            act.wait_ge(s_tr, 1)
            nc.scalar.activation(dT[:], pd[0:NT, 0:P], ACT.Copy).then_inc(s_rT, 1)
            for s in range(2):
                act.wait_ge(s_tr, s + 2)
                nc.scalar.activation(wt[:, s].rearrange("p k n -> p (k n)"), pt[:, s, :], ACT.Copy).then_inc(s_cp, 1)
            for s in range(2):
                act.wait_ge(s_mm, s + 1)
                nc.scalar.activation(m[:, 0, s], pm[:, s, :].rearrange("p (k n) -> p k n", k=KC), ACT.Copy, scale=WSC).then_inc(s_hi, 1)


def mean_aggregate(k, hT, Hn, m, bias, ideg_dram, adjT_dram, out_dram):
    nc = k.nc
    s_agg, s_T, s_hi, s_lo, s_mm, s_t, s_x, s_ideg, s_st = (
        k.sem(f"s_m3_{n}") for n in ("agg", "T", "hi", "lo", "mm", "t", "x", "ideg", "st"))
    s_in = [k.sem(f"s_m3_in{i}") for i in range(2)]
    prods = hi_lo_products(KC)
    with ExitStack() as c:
        ad = k.sb(c, "m3_ad", [P, 2, CT, NT, P], FP8)
        idr = k.sb(c, "m3_ideg", [P, NP], F32)
        T = k.sb(c, "m3_T", [P, 2, KC, CW], F32)
        aT = k.sb(c, "m3_aT", [P, 2, 2, KC, CW], F16)
        R = k.sb(c, "m3_R", [P, 2, CT, D], F32)
        pa = k.ps(c, "m3_pa", [P, 2, KC, CH])
        po = k.ps(c, "m3_po", [P, 2, CT, D])
        block = c.enter_context(nc.Block())

        @block.sync
        def _(sp):
            sp.dma_start(idr[:], ideg_dram.unsqueeze(0).to_broadcast([P, NP])).then_inc(s_ideg, 16)

            def load(c, q):
                sp.wait_ge(s_agg, c + 1)
                sp.dma_start(ad[:, q].rearrange("p t j i -> p t (j i)").bitcast(U8),
                             adjT_dram[bass.ds(c * CT, CT)].rearrange("t p n -> p t n").bitcast(U8)).then_inc(s_in[q], 16)

            def store(c):
                sp.wait_ge(s_x, c + 1)
                sp.dma_start(out_dram[bass.ds(c * CW, CW), :].rearrange("(t p) d -> p t d", p=P),
                             k.X[:, bass.ds(c * CT, CT), :]).then_inc(s_st, 16)

            load(0, 0)
            load(1, 1)
            with sp.Fori(0, NC // 2 - 1) as i:
                for q in range(2):
                    load(2 * i + 2 + q, q)
                    store(2 * i + q)
            load(NC - 1, 0)
            store(NC - 3)
            store(NC - 2)
            sp.wait_ge(s_x, NC)
            sp.dma_start(out_dram[(NT - 2) * P:(NT - 1) * P, :], k.X[:, NT - 2, :]).then_inc(s_st, 16)
            sp.dma_start(out_dram[(NT - 1) * P:N, :], k.X[0:LAST, NT - 1, :]).then_inc(s_st, 16)
            sp.wait_ge(s_st, 16 * (NC + 1))

        @block.tensor
        def _(pe):
            pe.sem_inc(s_agg, 2)
            pe.sem_inc(s_mm, 2)

            def sums(c, q):
                pe.wait_ge(s_in[q], 8 * (c - q) + 16)
                pe.wait_ge(s_T, c + 1)
                k.settle(pe)
                for kc in range(KC):
                    for jt in range(NT):
                        for a in range(2):
                            last = nc.tensor.matmul(pa[:, q, kc, 0:CW].rearrange("p (t i) -> p t i", t=CT),
                                                    Hn[:, a, jt, kc * P:(kc + 1) * P], ad[:, q, :, jt, :],
                                                    start=(jt == 0 and a == 0), stop=(jt == NT - 1 and a == 1))
                last.then_inc(s_agg, 1)

            def linear(c, q):
                pe.wait_ge(s_lo, c + 3)
                pe.wait_ge(s_t, c + 1)
                for t in range(CT):
                    for n, (kc, a, b) in enumerate(prods):
                        nc.tensor.matmul(po[:, q, t, :], hT[:, a, kc, bass.ds((c * CT + t) * P, P)], m[:, b, 0, kc, :],
                                         start=(n == 0), stop=False)
                    for n, (kc, a, b) in enumerate(prods):
                        last = nc.tensor.matmul(po[:, q, t, :], aT[:, q, a, kc, t * P:(t + 1) * P], m[:, b, 1, kc, :],
                                                start=False, stop=(n == len(prods) - 1))
                last.then_inc(s_mm, 1)

            sums(0, 0)
            with pe.Fori(0, NC // 2) as i:
                sums(2 * i + 1, 1)
                linear(2 * i, 0)
                sums(2 * i + 2, 0)
                linear(2 * i + 1, 1)
            linear(NC - 1, 0)

        @block.scalar
        def _(act):
            def chunk(c, q, last):
                act.wait_ge(s_T, c + 3)
                act.wait_ge(s_mm, c + 1)
                nc.scalar.activation(aT[:, q, 0], T[:, q], ACT.Copy).then_inc(s_hi, 1)

            over_chunks(act, chunk)

        @block.vector
        def _(dve):
            dve.sem_inc(s_T, 2)
            dve.sem_inc(s_t, 2)
            dve.sem_inc(s_lo, 2)
            dve.wait_ge(s_ideg, 16)

            def means(c, q):
                dve.wait_ge(s_agg, c + 3)
                dve.wait_ge(s_lo, c + 1)
                nc.vector.tensor_tensor(T[:, q], pa[:, q, :, 0:CW],
                                        idr[:, bass.ds(c * CW, CW)].unsqueeze(1).to_broadcast([P, KC, CW]), ALU.mult).then_inc(s_T, 1)
                dve.wait_ge(s_hi, c + 1)
                nc.vector.tensor_tensor(aT[:, q, 1], T[:, q], aT[:, q, 0], ALU.subtract).then_inc(s_lo, 1)

            def result(c, q):
                dve.wait_ge(s_mm, c + 3)
                for t in range(CT):
                    last = nc.vector.scalar_tensor_tensor(R[:, q, t, :], po[:, q, t, :], 1.0 / PSC, bias[:], ALU.mult, ALU.add)
                last.then_inc(s_t, 1)
                dve.wait_ge(s_t, c + 3)
                xs = k.X[:, bass.ds(c * CT, CT), :]
                nc.vector.scalar_tensor_tensor(xs, R[:, q], 0.0, xs, ALU.max, ALU.add).then_inc(s_x, 1)

            means(0, 0)
            with dve.Fori(0, NC // 2) as i:
                means(2 * i + 1, 1)
                result(2 * i, 0)
                means(2 * i + 2, 0)
                result(2 * i + 1, 1)
            result(NC - 1, 0)


def layer3(k, ap, adjT_dram, out_dram):
    with ExitStack() as c:
        ideg_dram = k.dram("ideg_dram", (NP,), F32)
        hT = k.sb(c, "hT3", [P, 2, KC, NP], F16)
        Hn = k.sb(c, "Hn", [P, 2, NT, D], F16)
        m = k.sb(c, "m3_w", [P, 2, 2, KC, D], F16)
        bias = k.sb(c, "m3_bias", [P, D], F32)
        normalise(k, "n3", hT, [], Hn)
        mean_weights(k, ap, m, bias, ideg_dram)
        mean_aggregate(k, hT, Hn, m, bias, ideg_dram, adjT_dram, out_dram)



def build(nc, ap, out_dram):
    with ExitStack() as ctx:
        k = Kernel(nc)
        k.s_adjT_out = nc.alloc_semaphore(name="s_adjT_out")
        k.X = k.sb(ctx, "X", [P, NT, D], F32)
        k.ident = k.sb(ctx, "ident", [P, P], F32)
        k.ident16 = k.sb(ctx, "ident16", [P, P], BF16)
        k.corner16 = k.sb(ctx, "corner16", [P, P], BF16)
        k.deg = k.sb(ctx, "deg", [P, 2, NT], F32)
        adjT_dram = k.dram("adjT_dram", (NT, P, NP), FP8)
        setup_constants(k, ap["x"])
        with ExitStack() as c:
            k.adjT = k.sb(c, "adjT", [P, NT, NT, P], FP8)
            transpose_adjacency(k, ap["adj"])
            layer0(k, ap, adjT_dram)
        k.end_layer()
        layer1(k, ap, adjT_dram)
        k.end_layer()
        layer2(k, ap)
        k.end_layer()
        layer3(k, ap, adjT_dram, out_dram)


INPUTS = ["x", "adj", "L0_gnn_W_lin", "L0_gnn_attn_w", "L1_gnn_W", "L2_gnn_WQ", "L2_gnn_WK", "L2_gnn_WV", "L2_gnn_we",
          "L2_gnn_be", "L3_gnn_W_self", "L3_gnn_b_self", "L3_gnn_W_nb", "L3_gnn_b_nb", "L3_gnn_W_comb", "L3_gnn_b_comb"]


def kernel(**inputs):
    import numpy as np
    import concourse.bacc as bacc
    from concourse.bass_utils import run_bass_kernel_spmd

    nc = bacc.Bacc("TRN2", target_bir_lowering=False, num_devices=1)
    arrays, ap = {}, {}
    for name in INPUTS:
        a = np.ascontiguousarray(inputs[name])
        arrays[f"in_{name}_dram"] = a
        ap[name] = nc.dram_tensor(f"in_{name}_dram", a.shape, mybir.dt.from_np(a.dtype), kind="ExternalInput").ap()
    out = nc.dram_tensor("out_dram", (N, D), F32, kind="ExternalOutput").ap()
    build(nc, ap, out)
    r = run_bass_kernel_spmd(nc, [arrays], core_ids=[0])
    return r.results[0]["out_dram"]
```

```python
from contextlib import ExitStack

import concourse.bass as bass
from concourse import mybir

F32 = mybir.dt.float32
F16 = mybir.dt.float16
BF16 = mybir.dt.bfloat16
FP8 = mybir.dt.float8e4
I32 = mybir.dt.int32
U16 = mybir.dt.uint16
U8 = mybir.dt.uint8
ALU = mybir.AluOpType
ACT = mybir.ActivationFunctionType
AX = mybir.AxisListType

N = 3327
P = 128
NT = -(-N // P)
NP = NT * P
LAST = N - (NT - 1) * P
D = 256
KC = D // P
HEADS = 8
HD = D // HEADS
LN_EPS = 1e-5
SLOPE = 0.2
NORM_EPS = 1e-8
HSC = 256.0
WSC = 1024.0
PSC = HSC * WSC
FP8_ONE = 0x38
CH = 512
CHUNKS = [(c, min(CH, NP - c)) for c in range(0, NP, CH)]


def hi_lo_products(pairs):
    return [(kc, a, b) for kc in range(pairs) for a, b in ((0, 0), (0, 1), (1, 0))]


class Kernel:

    def __init__(self, nc):
        self.nc = nc
        self.layer_sems = []
        self.s_settled = nc.alloc_semaphore(name="s_settled")

    def sem(self, name):
        self.layer_sems.append(self.nc.alloc_semaphore(name=name))
        return self.layer_sems[-1]

    def end_layer(self):
        self.nc.all_engine_barrier()
        self.nc.clear_and_free_semaphores(self.layer_sems)
        self.nc.all_engine_barrier()
        self.layer_sems = []

    def settle(self, eng):
        eng.sem_inc(self.s_settled, 1)

    def sb(self, ctx, name, shape, dt):
        return ctx.enter_context(self.nc.sbuf_tensor(name, shape, dt))

    def ps(self, ctx, name, shape, dt=F32):
        return ctx.enter_context(self.nc.psum_tensor(name, shape, dt))

    def dram(self, name, shape, dt):
        return self.nc.dram_tensor(name, shape, dt, kind="Internal").ap()


def setup_constants(k, x_dram, attn_w):
    nc = k.nc
    s_x, s_zero, s_ones, s_id, s_cols = (k.sem(n) for n in ("s_x", "s_x_zero", "s_const_ones", "s_identity", "s_attn_cols"))
    k.inputs_in = lambda eng: eng.wait_ge(s_x, 16 * (2 + 2 * HEADS))
    with ExitStack() as c:
        ones = k.sb(c, "ones_pp", [P, P], F32)
        corner = k.sb(c, "corner_f", [P, P], F32)
        block = c.enter_context(nc.Block())

        @block.sync
        def _(sp):
            sp.dma_start(k.X[:, 0:NT - 1, :], x_dram[0:(NT - 1) * P, :].rearrange("(t p) d -> p t d", p=P)).then_inc(s_x, 16)
            sp.wait_ge(s_zero, 1)
            sp.dma_start(k.X[0:LAST, NT - 1, :], x_dram[(NT - 1) * P:N, :]).then_inc(s_x, 16)
            sp.wait_ge(s_cols, 1)
            for h in range(HEADS):
                q, kn = h % 4, h // 4
                for side in range(2):
                    sp.dma_start(k.attn_cols[HD * q:HD * q + HD, kn, side * HEADS + h:side * HEADS + h + 1],
                                 attn_w[side * HD:(side + 1) * HD].rearrange("(p o) -> p o", o=1)).then_inc(s_x, 16)

        @block.vector
        def _(dve):
            nc.vector.memset(k.X[:, NT - 1, :], 0.0).then_inc(s_zero, 1)
            nc.vector.memset(k.attn_cols[:], 0.0).then_inc(s_cols, 1)
            nc.vector.memset(ones[:], 1.0).then_inc(s_ones, 1)
            dve.wait_ge(s_id, 2)
            nc.vector.tensor_copy(k.ident16[:], k.ident[:])
            nc.vector.tensor_copy(k.corner16[:], corner[:])

        @block.gpsimd
        def _(pool):
            pool.wait_ge(s_ones, 1)
            nc.gpsimd.affine_select(out=k.ident[:], in_=ones[:], compare_op=ALU.is_equal, fill=0.0, base=0,
                                    pattern=[[-1, P]], channel_multiplier=1).then_inc(s_id, 1)
            nc.gpsimd.affine_select(out=corner[:], in_=ones[:], compare_op=ALU.is_equal, fill=0.0, base=-2 * (P - 1),
                                    pattern=[[1, P]], channel_multiplier=1).then_inc(s_id, 1)


def transpose_adjacency(k, adj_dram):
    nc = k.nc
    s_rows = [[k.sem(f"s_adj_rows{s}{f}") for f in range(2)] for s in range(2)]
    HALF = NP // 2
    cut = lambda f: slice(f * HALF, (f + 1) * HALF)
    s_used, s_corner, s_tr, s_evac, s_pad = (
        k.sem(n) for n in ("s_adj_used", "s_corner", "s_adj_tr", "s_adj_evac", "s_adj_pad"))
    STEPS = NT // 2 - 1
    with ExitStack() as c:
        rows = k.sb(c, "adj_rows", [P, 2, NP], I32)
        a16 = k.sb(c, "adj16", [P, 2, NP], BF16)
        tr = k.ps(c, "adj_tr", [P, 2, 4 * 1024], BF16)
        block = c.enter_context(nc.Block())

        @block.sync
        def _(sp):
            sp.wait_ge(s_pad, 1)
            for s in range(2):
                for f in range(2):
                    c1 = N if f else HALF
                    sp.dma_start(rows[:, s, f * HALF:c1], adj_dram[s * P:(s + 1) * P, f * HALF:c1]).then_inc(s_rows[s][f], 16)
            with sp.Fori(0, STEPS - 1) as i:
                for s in range(2):
                    for f in range(2):
                        c1 = N if f else HALF
                        sp.wait_ge(s_used, 4 * i + 2 * s + f + 1)
                        sp.dma_start(rows[:, s, f * HALF:c1],
                                     adj_dram[bass.ds(i * (2 * P) + (s + 2) * P, P), f * HALF:c1]).then_inc(s_rows[s][f], 16)
            for f in range(2):
                c1 = N if f else HALF
                sp.wait_ge(s_used, 2 * (NT - 4) + f + 1)
                sp.dma_start(rows[:, 0, f * HALF:c1], adj_dram[(NT - 2) * P:(NT - 1) * P, f * HALF:c1]).then_inc(s_rows[0][f], 16)
            sp.wait_ge(s_pad, 2)
            for f in range(2):
                c1 = N if f else HALF
                sp.dma_start(rows[0:LAST, 1, f * HALF:c1], adj_dram[(NT - 1) * P:N, f * HALF:c1]).then_inc(s_rows[1][f], 16)

        @block.gpsimd
        def _(pool):
            nc.gpsimd.memset(rows[:, :, N:NP], 0).then_inc(s_pad, 1)
            pool.wait_ge(s_used, 2 * NT - 4)
            nc.gpsimd.memset(rows[96:P, 1, :], 0).then_inc(s_pad, 1)

        @block.scalar
        def _(act):
            def convert(t, s, step):
                act.wait_ge(s_tr, t + 1)
                for f in range(2):
                    act.wait_ge(s_rows[s][f], 16 * (step + 1))
                    nc.scalar.activation(a16[:, s, cut(f)], rows[:, s, cut(f)], ACT.Copy,
                                         accum_out=k.deg[:, f, bass.ds(t, 1)]).then_inc(s_used, 1)

            act.wait_ge(s_pad, 1)
            with act.Fori(0, STEPS) as i:
                for s in range(2):
                    convert(2 * i + s, s, i)
            convert(NT - 2, 0, STEPS)
            act.wait_ge(s_pad, 2)
            convert(NT - 1, 1, STEPS)

        @block.tensor
        def _(pe):
            pe.sem_inc(s_tr, 2)

            def transpose(t, s, final=False):
                pe.wait_ge(s_evac, t + 1)
                for f in range(2):
                    if final and f == 1:
                        pe.wait_ge(s_corner, 1)
                    else:
                        pe.wait_ge(s_used, 2 * t + f + 1)
                    for jt in range(f * NT // 2, (f + 1) * NT // 2):
                        last = nc.tensor.transpose(tr[:, s, jt * P:(jt + 1) * P], a16[:, s, jt * P:(jt + 1) * P], k.ident16[:])
                last.then_inc(s_tr, 1)

            with pe.Fori(0, STEPS) as i:
                for s in range(2):
                    transpose(2 * i + s, s)
            transpose(NT - 2, 0)
            transpose(NT - 1, 1, True)

        @block.vector
        def _(dve):
            dve.sem_inc(s_evac, 2)

            def evacuate(t, s):
                dve.wait_ge(s_tr, t + 3)
                nc.vector.tensor_scalar(k.adjT[:, bass.ds(t, 1), :, :].rearrange("p t j i -> p (t j i)").bitcast(U8),
                                        tr[:, s, 0:NP], float(FP8_ONE), None, ALU.mult).then_inc(s_evac, 1)

            with dve.Fori(0, STEPS) as i:
                for s in range(2):
                    evacuate(2 * i + s, s)
            dve.wait_ge(s_used, 2 * NT)
            nc.vector.tensor_tensor(a16[:, 1, NP - P:NP], a16[:, 1, NP - P:NP], k.corner16[:], ALU.add).then_inc(s_corner, 1)
            evacuate(NT - 2, 0)
            evacuate(NT - 1, 1)


def normalise(k, tag, hT, weights, h_nat=None, adjT_dram=None, also=None):
    nc = k.nc
    s_w, s_stat, s_sq, s_sm, s_h, s_tr, s_hi, s_lo = (
        k.sem(f"s_{tag}_{n}") for n in ("w", "stat", "sqrt", "small", "h", "tr", "hi", "lo"))
    slots = [(g, kc) for g in range(-(-NT // 4)) for kc in range(KC)]
    NB = 4
    halves = ((0, 8), (8, NT))
    pieces = ((0, 9), (9, 18), (18, NT))
    COUNTED = 8
    with ExitStack() as c:
        H = k.sb(c, f"{tag}_h", [P, NT, D], F32)
        stats = k.sb(c, f"{tag}_stats", [P, NT, 6], F32)
        mv = k.sb(c, f"{tag}_mv", [P, NT, 2], F32)
        sm = k.sb(c, f"{tag}_sm", [P, 6, NT], F32)
        rt, nb = sm[:, 1, :], sm[:, 5, :]
        raw = k.sb(c, f"{tag}_wraw", [P, max(1, len(weights)), 2, D], F32)
        pt = k.ps(c, f"{tag}_pt", [P, NB, CH])
        extra = also(c) if also else {}

        def more(place, eng):
            if place in extra:
                extra[place](eng)

        block = c.enter_context(nc.Block())
        nw = len(weights)

        @block.sync
        def _(sp):
            more("sync", sp)
            for i, (w, _) in enumerate(weights):
                sp.dma_start(raw[:, i, :, :], w.rearrange("(k p) c -> p k c", p=P)).then_inc(s_w, 16)
            if adjT_dram is not None:
                sp.dma_start(adjT_dram.rearrange("t p n -> p t n"), k.adjT[:].rearrange("p t j i -> p t (j i)")).then_inc(k.s_adjT_out, 16)

        @block.vector
        def _(dve):
            more("vector_first", dve)
            def factors(half, n):
                t0, t1 = halves[half]
                ve, rt, rs, a, b, nb = (sm[:, i, t0:t1] for i in range(6))
                if n == 1:
                    dve.wait_ge(s_sq, half + 1)
                dve.wait_ge(s_sm, COUNTED * half + n + 1)
                if n == 0:
                    ins = nc.vector.tensor_scalar(ve, mv[:, t0:t1, 1], LN_EPS, None, ALU.add)
                elif n == 1:
                    ins = nc.vector.reciprocal(rs, rt)
                elif n == 2:
                    ins = nc.vector.tensor_tensor(a, rs, rs, ALU.mult)
                elif n == 3:
                    ins = nc.vector.tensor_tensor(b, a, ve, ALU.mult)
                elif n == 4:
                    ins = nc.vector.tensor_scalar(a, b, -0.5, 1.5, ALU.mult, ALU.add)
                elif n == 5:
                    ins = nc.vector.tensor_tensor(rt, a, rs, ALU.mult)
                else:
                    ins = nc.vector.scalar_tensor_tensor(nb, mv[:, t0:t1, 0], -1.0, rt, ALU.mult, ALU.mult)
                ins.then_inc(s_sm, 1)

            for half, (t0, t1) in enumerate(halves):
                for t in range(t0, t1):
                    nc.vector.bn_stats(stats[:, t, :], k.X[:, t, :]).then_inc(s_stat, 1)
                    if half and t - t0 < COUNTED - 1:
                        factors(0, t - t0)
                for t in range(t0, t1):
                    dve.wait_ge(s_stat, t + 1)
                    last = nc.vector.bn_aggr(mv[:, t, :], stats[:, t, :])
                last.then_inc(s_sm, 1)
            for i in range(nw):
                dve.wait_ge(s_hi, i + 1)
                wt = weights[i][1]
                nc.vector.scalar_tensor_tensor(wt(1), pt[:, i % NB, :].rearrange("p (k n) -> p k n", k=KC), WSC, wt(0),
                                               ALU.mult, ALU.subtract).then_inc(s_lo, 1)
            more("vector_mid", dve)
            for n in range(COUNTED - 1):
                factors(1, n)
            for j, (g, kc) in enumerate(slots):
                n0, n1 = g * CH, min(NP, (g + 1) * CH)
                dve.wait_ge(s_hi, nw + j + 1)
                nc.vector.scalar_tensor_tensor(hT[:, 1, kc, n0:n1], pt[:, (nw + j) % NB, 0:n1 - n0], HSC, hT[:, 0, kc, n0:n1],
                                               ALU.mult, ALU.subtract).then_inc(s_lo, 1)
            if h_nat is not None:
                for n, (t0, t1) in enumerate(pieces):
                    dve.wait_ge(s_hi, nw + len(slots) + 1 + n)
                    nc.vector.scalar_tensor_tensor(h_nat[:, 1, t0:t1], H[:, t0:t1], HSC, h_nat[:, 0, t0:t1], ALU.mult, ALU.subtract)
            more("vector_last", dve)

        @block.scalar
        def _(act):
            more("scalar_first", act)
            def root(half):
                t0, t1 = halves[half]
                act.wait_ge(s_sm, COUNTED * half + 2)
                nc.scalar.activation(sm[:, 1, t0:t1], sm[:, 0, t0:t1], ACT.Sqrt).then_inc(s_sq, 1)

            root(0)
            more("scalar_mid", act)
            for i in range(nw):
                act.wait_ge(s_tr, i + 1)
                nc.scalar.activation(weights[i][1](0), pt[:, i % NB, :].rearrange("p (k n) -> p k n", k=KC), ACT.Copy,
                                     scale=WSC).then_inc(s_hi, 1)

            def relu(t):
                if t in (0, halves[1][0]):
                    act.wait_ge(s_sm, COUNTED if t == 0 else 2 * COUNTED)
                nc.scalar.activation(H[:, t, :], k.X[:, t, :], ACT.Relu, scale=rt[:, t:t + 1], bias=nb[:, t:t + 1]).then_inc(s_h, 1)

            def high(j):
                g, kc = slots[j]
                n0, n1 = g * CH, min(NP, (g + 1) * CH)
                act.wait_ge(s_tr, nw + j + 1)
                nc.scalar.activation(hT[:, 0, kc, n0:n1], pt[:, (nw + j) % NB, 0:n1 - n0], ACT.Copy, scale=HSC).then_inc(s_hi, 1)

            for g in range(-(-NT // 4)):
                if 4 * g == halves[1][0]:
                    root(1)
                for t in range(4 * g, min(4 * g + 4, NT)):
                    relu(t)
                if g >= 1:
                    high(2 * g - 2)
                    high(2 * g - 1)
            high(len(slots) - 2)
            high(len(slots) - 1)
            if h_nat is not None:
                act.wait_ge(s_h, NT)
                for t0, t1 in pieces:
                    nc.scalar.activation(h_nat[:, 0, t0:t1], H[:, t0:t1], ACT.Copy, scale=HSC).then_inc(s_hi, 1)
            more("scalar_last", act)

        @block.tensor
        def _(pe):
            more("tensor_first", pe)
            for i in range(nw):
                pe.wait_ge(s_w, 16 * nw)
                if i >= NB:
                    pe.wait_ge(s_lo, i - NB + 1)
                for kc in range(KC):
                    for kn in range(2):
                        last = nc.tensor.transpose(pt[:, i % NB, kc * D + kn * P:kc * D + (kn + 1) * P],
                                                   raw[:, i, kn, kc * P:(kc + 1) * P], k.ident[:])
                last.then_inc(s_tr, 1)
            for j, (g, kc) in enumerate(slots):
                tiles = range(4 * g, min(4 * g + 4, NT))
                pe.wait_ge(s_h, tiles[-1] + 1)
                if nw + j >= NB:
                    pe.wait_ge(s_lo, nw + j - NB + 1)
                for t in tiles:
                    last = nc.tensor.transpose(pt[:, (nw + j) % NB, (t % 4) * P:(t % 4 + 1) * P],
                                               H[:, t, kc * P:(kc + 1) * P], k.ident[:])
                last.then_inc(s_tr, 1)
            more("tensor_last", pe)



G1 = HD + 1
VSC = 2048.0
STEP = 2.0 ** 60


def gat_project(k, hT, w, el_dram, GE):
    nc = k.nc
    s_in, s_wa, s_wahi, s_walo, s_g, s_ge, s_elp, s_elt = (
        k.sem(f"s_g0_{n}") for n in ("in", "wa", "wahi", "walo", "g", "ge", "elp", "elt"))
    ad = k.attn_cols
    s_out = [k.sem(f"s_g0_elout{i}") for i in range(2)]
    NB = 4
    prods = hi_lo_products(KC)
    with ExitStack() as c:
        raw = k.sb(c, "g0_wraw", [P, 2, D], F32)
        elT = k.sb(c, "g0_elT", [HEADS, 2, CH], F32)
        pg = k.ps(c, "g0_pg", [P, NB, CH])
        pel = k.ps(c, "g0_pel", [HEADS, 2, CH])
        block = c.enter_context(nc.Block())

        @block.sync
        def _(sp):
            sp.dma_start(raw[:], k.w_lin.rearrange("(k p) c -> p k c", p=P)).then_inc(s_in, 16)
            for m, (c0, cn) in enumerate(CHUNKS):
                sp.wait_ge(s_elt, m + 1)
                sp.dma_start(el_dram[:, c0:c0 + cn], elT[:, m % 2, 0:cn]).then_inc(s_out[m % 2], 16)
            for i in range(2):
                sp.wait_ge(s_out[i], 16 * len(range(i, len(CHUNKS), 2)))

        @block.vector
        def _(dve):
            dve.wait_ge(s_wahi, 1)
            nc.vector.scalar_tensor_tensor(w[:, 1, :, D:D + 16], pg[:, 0, 0:32].rearrange("p (k n) -> p k n", k=KC), WSC,
                                           w[:, 0, :, D:D + 16], ALU.mult, ALU.subtract).then_inc(s_walo, 1)

        @block.tensor
        def _(pe):
            pe.wait_ge(s_in, 16)
            for kc in range(KC):
                for kn in range(2):
                    last = nc.tensor.matmul(pg[:, 0, kc * 16:kc * 16 + 16], raw[:, kn, kc * P:(kc + 1) * P], ad[:, kn, :],
                                            start=(kn == 0), stop=(kn == 1))
            last.then_inc(s_wa, 1)
            pe.wait_ge(s_walo, 1)
            for t in range(NT):
                if t >= NB:
                    pe.wait_ge(s_ge, t - NB + 1)
                for n, (kc, a, b) in enumerate(prods):
                    last = nc.tensor.matmul(pg[:, t % NB, 0:D + 16], hT[:, a, kc, t * P:(t + 1) * P], w[:, b, kc, :],
                                            start=(n == 0), stop=(n == len(prods) - 1))
                last.then_inc(s_g, 1)
            for m, (c0, cn) in enumerate(CHUNKS):
                if m >= 2:
                    pe.wait_ge(s_elt, m - 1)
                for n, (kc, a, b) in enumerate(prods):
                    last = nc.tensor.matmul(pel[:, m % 2, 0:cn], w[:, a, kc, D:D + HEADS], hT[:, b, kc, c0:c0 + cn],
                                            start=(n == 0), stop=(n == len(prods) - 1))
                last.then_inc(s_elp, 1)

        @block.scalar
        def _(act):
            act.wait_ge(s_wa, 1)
            nc.scalar.activation(w[:, 0, :, D:D + 16], pg[:, 0, 0:32].rearrange("p (k n) -> p k n", k=KC), ACT.Copy,
                                 scale=WSC).then_inc(s_wahi, 1)
            for t in range(NT):
                act.wait_ge(s_g, t + 1)
                nc.scalar.activation(GE[:, t, :], pg[:, t % NB, 0:D + 16], ACT.Copy, scale=1.0 / PSC).then_inc(s_ge, 1)
            for m, (c0, cn) in enumerate(CHUNKS):
                act.wait_ge(s_elp, m + 1)
                if m >= 2:
                    act.wait_ge(s_out[m % 2], 16 * (m // 2))
                nc.scalar.activation(elT[:, m % 2, 0:cn], pel[:, m % 2, 0:cn], ACT.Copy, scale=1.0 / PSC).then_inc(s_elt, 1)


def gat_factors(k, xv_dram, HC, GE, spare):
    nc = k.nc
    s_red, s_rmax, s_fac, s_exp, s_fv, s_fp, s_xh, s_xl = (
        k.sem(f"s_x0_{n}") for n in ("red", "rmax", "fac", "exp", "fv", "fp", "xh", "xl"))
    NX, NF = 4, 3
    s_out = [k.sem(f"s_x0_out{i}") for i in range(NX)]
    SL = NT * 2 * G1
    F = spare[:, 0:NF * SL].bitcast(F32).rearrange("p (s t d) -> p s t d", s=NF, d=G1)
    X1 = spare[:, NF * SL:(NF + NX) * SL].rearrange("p (s t a d) -> p s t a d", s=NX, a=2, d=G1)
    steps = [(f, h) for f in (1, 0) for h in range(HEADS)]
    er, el = GE[:, :, D + HEADS:D + 2 * HEADS], GE[:, :, D:D + HEADS]
    with ExitStack() as c:
        rm = k.sb(c, "x0_rm", [P, 2, HEADS], F32)
        vf = k.sb(c, "x0_vf", [P, 2, NT, HEADS], F32)
        dd = k.sb(c, "x0_dd", [P, 4, NT, HEADS], F32)
        block = c.enter_context(nc.Block())

        def split_out(n):
            return X1[:, n % NX]

        @block.sync
        def _(sp):
            for n, (f, h) in enumerate(steps):
                sp.wait_ge(s_xl, n + 1)
                sp.dma_start(xv_dram[f, h], split_out(n).rearrange("p t a d -> p (t a d)")).then_inc(s_out[n % NX], 16)
            for i in range(NX):
                sp.wait_ge(s_out[i], 16 * len(steps) // NX)

        @block.scalar
        def _(act):
            act.wait_ge(s_fac, 1)
            nc.scalar.activation(vf[:, 1], dd[:, 0], ACT.Exp).then_inc(s_exp, 1)
            nc.scalar.activation(vf[:, 0], dd[:, 0], ACT.Exp, scale=SLOPE).then_inc(s_exp, 1)
            act.wait_ge(s_fac, 6)
            nc.scalar.activation(HC[:, :, 2, :].rearrange("p h t -> p t h"), dd[:, 1], ACT.Exp)
            nc.scalar.activation(HC[:, :, 3, :].rearrange("p h t -> p t h"), dd[:, 2], ACT.Exp)
            for n, (f, h) in enumerate(steps):
                act.wait_ge((s_fv, s_fp)[n % 2], 2 * (n // 2 + 1))
                if n >= NX:
                    act.wait_ge(s_out[n % NX], 16 * (n // NX))
                nc.scalar.activation(split_out(n)[:, :, 0, :], F[:, n % NF], ACT.Copy).then_inc(s_xh, 1)

        def product(eng, api, n, done):
            f, h = steps[n]
            v = vf[:, f, :, h]
            if n >= NF:
                eng.wait_ge(s_xl, n - NF + 1)
            api.tensor_tensor(F[:, n % NF, :, 0:HD], GE[:, :, h * HD:(h + 1) * HD],
                              v.unsqueeze(2).to_broadcast([P, NT, HD]), ALU.mult).then_inc(done, 1)

        @block.gpsimd
        def _(pool):
            pool.wait_ge(s_red, 1)
            nc.gpsimd.partition_all_reduce(rm[:, 1, :], rm[:, 0, :], P, bass.bass_isa.ReduceOp.max).then_inc(s_rmax, 1)
            pool.wait_ge(s_fac, 7)
            for n in range(1, len(steps), 2):
                if n > 1:
                    pool.wait_ge(s_fp, n - 1)
                product(pool, nc.gpsimd, n, s_fp)
                f, h = steps[n]
                pool.wait_ge(s_fp, n)
                nc.gpsimd.tensor_copy(F[:, n % NF, :, HD], vf[:, f, :, h]).then_inc(s_fp, 1)

        @block.vector
        def _(dve):
            nc.vector.tensor_reduce(rm[:, 0, :], er.rearrange("p t h -> p h t"), AX.X, ALU.max).then_inc(s_red, 1)
            nc.vector.tensor_scalar(HC[:, :, 0, :].rearrange("p h t -> p t h"), er, -1.0, None, ALU.mult)
            nc.vector.tensor_scalar(HC[:, :, 1, :].rearrange("p h t -> p t h"), er, STEP, None, ALU.mult)
            dve.wait_ge(s_rmax, 1)
            R = rm[:, 1, :].unsqueeze(1).to_broadcast([P, NT, HEADS])
            nc.vector.tensor_tensor(dd[:, 0], er, R, ALU.subtract).then_inc(s_fac, 1)
            nc.vector.tensor_tensor(dd[:, 1], el, R, ALU.add).then_inc(s_fac, 1)
            dve.wait_ge(s_fac, 2)
            nc.vector.tensor_scalar(dd[:, 2], dd[:, 1], SLOPE, None, ALU.mult).then_inc(s_fac, 1)
            dve.wait_ge(s_fac, 3)
            nc.vector.tensor_tensor(dd[:, 3], dd[:, 1], dd[:, 2], ALU.max).then_inc(s_fac, 1)
            dve.wait_ge(s_fac, 4)
            nc.vector.tensor_tensor(dd[:, 1], dd[:, 1], dd[:, 3], ALU.subtract).then_inc(s_fac, 1)
            nc.vector.tensor_tensor(dd[:, 2], dd[:, 2], dd[:, 3], ALU.subtract).then_inc(s_fac, 1)
            dve.wait_ge(s_exp, 2)
            nc.vector.tensor_scalar(vf[:], vf[:], VSC, None, ALU.mult).then_inc(s_fac, 1)
            dve.wait_ge(s_fac, 7)

            def low(n):
                dve.wait_ge(s_xh, n + 1)
                nc.vector.tensor_tensor(split_out(n)[:, :, 1, :], F[:, n % NF], split_out(n)[:, :, 0, :], ALU.subtract).then_inc(s_xl, 1)

            for n, (f, h) in enumerate(steps):
                if n % 2 == 0:
                    product(dve, nc.vector, n, s_fv)
                    nc.vector.tensor_copy(F[:, n % NF, :, HD], vf[:, f, :, h]).then_inc(s_fv, 1)
                if n >= 1:
                    low(n - 1)
            low(len(steps) - 1)


GROUPS = [(0, 9), (9, 9), (18, 8)]
RING = 13
STEP_DVE = [2, 5, 7, 10, 12, 15, 17, 20, 22, 25]
STEP_ACT = [jt for jt in range(NT) if jt not in STEP_DVE]
STEP_SLOTS = ((STEP_ACT, 8, 0), (STEP_DVE, 5, 8))
STEP_RING = 13
AHEAD = 2
COPY_AT, COMBINE_AT = 10, 14


def step_slot(jt):
    for tiles, ring, base in STEP_SLOTS:
        if jt in tiles:
            n = tiles.index(jt)
            before = tiles[n - ring] if n >= ring else tiles[max(range(n, len(tiles), ring))] - NT
            return base + n % ring, before


def over_heads(eng, head):
    for group in range(len(GROUPS)):
        head(group, 0, 0, (group - 1, HEADS - 1) if group else None)
        with eng.Fori(0, HEADS // 2 - 1) as i:
            head(group, 2 * i + 1, 1, (group, 2 * i))
            head(group, 2 * i + 2, 0, (group, 2 * i + 1))
        head(group, HEADS - 1, 1, (group, HEADS - 2))


def gat_sums(k, el_dram, xv_dram, HC):
    nc = k.nc
    tag = "b0"
    GN = max(gn for _, gn in GROUPS)
    count = lambda group, h: group * HEADS + h
    s_mm, s_sel, s_rest, s_ca, s_cd, s_y, s_t, s_use = (
        k.sem(f"s_{tag}_{n}") for n in ("mm", "sel", "rest", "ca", "cd", "y", "t", "use"))
    s_in = [k.sem(f"s_{tag}_in{i}") for i in range(2)]
    TS = 5
    BANKS = -(-GN // 3)
    W = 4 * G1
    slot = lambda p, jt: (p * NT + jt) % RING
    with ExitStack() as c:
        xb = k.sb(c, f"{tag}_x", [P, 2, 2, NT, 2 * G1], F16)
        elr = k.sb(c, f"{tag}_el", [P, 2, GN * P], F32)
        hc = k.sb(c, f"{tag}_hc", [P, 2, 2, NT], F32)
        C = k.sb(c, f"{tag}_C", [P, STEP_RING, GN * P], FP8)
        B = k.sb(c, f"{tag}_B", [P, RING, GN * P], FP8)
        R = k.sb(c, f"{tag}_R", [P, RING, GN * P], FP8)
        Y = k.sb(c, f"{tag}_Y", [P, 2, GN, 4, G1], F32)
        S = k.sb(c, f"{tag}_S", [P, GN, 2, G1], F32)
        T = k.sb(c, f"{tag}_T", [P, GN, G1], F32)
        rd = k.sb(c, f"{tag}_rd", [P, GN], F32)
        pb = k.ps(c, f"{tag}_pb", [P, 2, 3, CH])
        block = c.enter_context(nc.Block())

        def step_free(eng, n, jt):
            eng.wait_ge(s_sel, n * NT + step_slot(jt)[1] + NT + 1)

        def arrived(eng, n, p):
            eng.wait_ge(s_in[p], 32 * (n - p) + 64)

        def words(x, gn):
            return x[:, 0:gn * P].bitcast(I32).rearrange("p (t w) -> p t w", t=gn)

        @block.sync
        def _(sp):
            sp.wait_ge(k.s_adjT_out, 16)
            for group, (g0, gn) in enumerate(GROUPS):
                with sp.Fori(0, HEADS // 2) as i:
                    for p in range(2):
                        h = 2 * i + p
                        sp.wait_ge(s_y, count(group, h) + 1)
                        for f in range(2):
                            sp.dma_start(xb[:, p, f].rearrange("p t n -> p (t n)"),
                                         xv_dram[f, bass.ds(h, 1)].rearrange("h p n -> p (h n)")).then_inc(s_in[p], 16)
                        sp.dma_start(elr[:, p, 0:gn * P],
                                     el_dram[bass.ds(h, 1), g0 * P:(g0 + gn) * P].to_broadcast([P, gn * P])).then_inc(s_in[p], 16)
                        sp.dma_start(hc[:, p].rearrange("p f t -> p (f t)"),
                                     HC[:, bass.ds(h, 1), 0:2].rearrange("p h f t -> p (h f t)")).then_inc(s_in[p], 16)

        @block.scalar
        def _(act):
            def copy_sums(group, h, p, b):
                n, gn = count(group, h), GROUPS[group][1]
                if b == 0:
                    act.wait_ge(s_mm, (n + 1) * NT + RING)
                    act.wait_ge(s_t, TS * n + 1)
                tiles = min(3, gn - 3 * b)
                last = nc.scalar.activation(Y[:, p, 3 * b:3 * b + tiles].rearrange("p t f d -> p (t f d)"),
                                            pb[:, p, b, 0:tiles * W], ACT.Copy)
                if b == BANKS - 1:
                    last.then_inc(s_y, 1)

            def head(group, h, p, previous):
                n, cols = count(group, h), GROUPS[group][1] * P
                arrived(act, n, p)
                for jt in range(NT):
                    if COPY_AT <= jt < COPY_AT + BANKS and previous:
                        copy_sums(*previous, 1 - p, jt - COPY_AT)
                    if jt in STEP_ACT:
                        step_free(act, n, jt)
                        k.settle(act)
                        nc.scalar.activation(C[:, step_slot(jt)[0], 0:cols], elr[:, p, 0:cols], ACT.Sigmoid,
                                             bias=hc[:, p, 1, jt:jt + 1], scale=STEP, saturate=False).then_inc(s_ca, 1)

            act.sem_inc(s_y, 2)
            over_heads(act, head)
            for b in range(BANKS):
                copy_sums(len(GROUPS) - 1, HEADS - 1, 1, b)

        @block.gpsimd
        def _(pool):
            def head(group, h, p, previous):
                n, (g0, gn) = count(group, h), GROUPS[group]
                for jt in range(NT):
                    pool.wait_ge(s_sel, n * NT + jt + 1 + NT)
                    pool.wait_ge(s_mm, n * NT + jt + 1)
                    nc.gpsimd.tensor_tensor(words(R[:, slot(p, jt)], gn), k.adjT[:, g0:g0 + gn, jt, :].bitcast(I32),
                                            words(B[:, slot(p, jt)], gn), ALU.subtract).then_inc(s_rest, 1)

            over_heads(pool, head)

        @block.vector
        def _(dve):
            def combine(group, h, p, stage):
                n, (g0, gn) = count(group, h), GROUPS[group]
                v = TS * n + 2 * TS
                u, u1 = (HC[:, bass.ds(h, 1), f, g0:g0 + gn].rearrange("p h t -> p (h t)").unsqueeze(2).to_broadcast([P, gn, G1])
                         for f in (2, 3))
                Sg, Tg, rg = S[:, 0:gn], T[:, 0:gn], rd[:, 0:gn]
                if stage > 0:
                    dve.wait_ge(s_t, v + stage)
                if stage == 0:
                    dve.wait_ge(s_y, n + 3)
                    dve.wait_ge(s_use, n + 2)
                    for f in range(2):
                        last = nc.vector.tensor_tensor(Sg[:, :, f, :], Y[:, p, 0:gn, 2 * f, :], Y[:, p, 0:gn, 2 * f + 1, :], ALU.add)
                    last.then_inc(s_t, 1)
                elif stage == 1:
                    nc.vector.tensor_tensor(Tg, Sg[:, :, 0, :], u1, ALU.mult)
                    nc.vector.tensor_tensor(Sg[:, :, 1, :], Sg[:, :, 1, :], u, ALU.mult).then_inc(s_t, 1)
                elif stage == 2:
                    nc.vector.tensor_tensor(Sg[:, :, 0, :], Tg, Sg[:, :, 1, :], ALU.add).then_inc(s_t, 1)
                elif stage == 3:
                    nc.vector.reciprocal(rg, Sg[:, :, 0, HD]).then_inc(s_t, 1)
                elif stage == 4:
                    nc.vector.tensor_tensor(Tg[:, :, 0:HD], Sg[:, :, 0, 0:HD], rg.unsqueeze(2).to_broadcast([P, gn, HD]),
                                            ALU.mult).then_inc(s_t, 1)
                else:
                    xs = k.X[:, g0:g0 + gn, bass.ds(h * HD, HD)]
                    nc.vector.tensor_tensor(xs, xs, Tg[:, :, 0:HD], ALU.add).then_inc(s_use, 1)

            def head(group, h, p, previous):
                n, (g0, gn) = count(group, h), GROUPS[group]
                cols = gn * P
                arrived(dve, n, p)
                for jt in range(NT):
                    if COMBINE_AT <= jt <= COMBINE_AT + TS and previous:
                        combine(*previous, 1 - p, jt - COMBINE_AT)
                    if jt + AHEAD in STEP_DVE:
                        step_free(dve, n, jt + AHEAD)
                        nc.vector.tensor_scalar(C[:, step_slot(jt + AHEAD)[0], 0:cols].bitcast(U8), elr[:, p, 0:cols],
                                                hc[:, p, 0, jt + AHEAD:jt + AHEAD + 1], float(FP8_ONE),
                                                ALU.is_gt, ALU.mult).then_inc(s_cd, 1)
                    for tiles, done in ((STEP_ACT, s_ca), (STEP_DVE, s_cd)):
                        if jt in tiles:
                            dve.wait_ge(done, n * len(tiles) + tiles.index(jt) + 1)
                    dve.wait_ge(s_mm, n * NT + jt + 1)
                    nc.vector.tensor_tensor(words(B[:, slot(p, jt)], gn), words(C[:, step_slot(jt)[0]], gn),
                                            k.adjT[:, g0:g0 + gn, jt, :].bitcast(I32), ALU.bitwise_and).then_inc(s_sel, 1)

            dve.sem_inc(s_use, 2)
            dve.sem_inc(s_t, 2 * TS)
            dve.sem_inc(s_sel, NT)
            over_heads(dve, head)
            for stage in range(TS + 1):
                combine(len(GROUPS) - 1, HEADS - 1, 1, stage)

        @block.tensor
        def _(pe):
            pe.sem_inc(s_mm, RING)
            for group, (g0, gn) in enumerate(GROUPS):
                with pe.Fori(0, HEADS // 2) as i:
                    for p in range(2):
                        n = count(group, 2 * i + p)
                        arrived(pe, n, p)
                        pe.wait_ge(s_y, n + 1)
                        for jt in range(NT):
                            pe.wait_ge(s_sel, n * NT + jt + 1 + NT)
                            k.settle(pe)
                            for f, edges in ((1, B), (0, R)):
                                if f == 0:
                                    pe.wait_ge(s_rest, n * NT + jt + 1)
                                    k.settle(pe)
                                for t in range(gn):
                                    b, r = t // 3, t % 3
                                    last = nc.tensor.matmul(pb[:, p, b, (2 * r + f) * 2 * G1:(2 * r + f + 1) * 2 * G1],
                                                            edges[:, slot(p, jt), t * P:(t + 1) * P], xb[:, p, f, jt, :],
                                                            start=(jt == 0 and r == 0 and f == 1), stop=(jt == NT - 1),
                                                            skip_group_check=True)
                            last.then_inc(s_mm, 1)


def layer0(k, ap, adjT_dram):
    nc = k.nc
    el_dram = k.dram("el_dram", (HEADS, NP), F32)
    xv_dram = k.dram("xv_dram", (2, HEADS, P, NT * 2 * G1), F16)
    k.w_lin = ap["L0_gnn_W_lin"]
    with ExitStack() as c:
        HC = k.sb(c, "HC", [P, HEADS, 4, NT], F32)
        with ExitStack() as c1:
            w = k.sb(c1, "w_gat", [P, 2, KC, D + 16], F16)
            hT = k.sb(c1, "hT0", [P, 2 * KC * NP], F16)
            hTv = hT[:].rearrange("p (a k n) -> p a k n", a=2, k=KC)
            normalise(k, "n0", hTv, [(ap["L0_gnn_W_lin"], lambda part: w[:, part, :, 0:D])], adjT_dram=adjT_dram,
                      also=lambda c2: {"vector_first": k.inputs_in})
            with ExitStack() as c2:
                GE = k.sb(c2, "GE", [P, NT, D + 16], F32)
                gat_project(k, hTv, w, el_dram, GE)
                gat_factors(k, xv_dram, HC, GE, hT[:])
        gat_sums(k, el_dram, xv_dram, HC)



R_MIN = 1e-13
WHSC = 64.0
NSC = 4096.0
ESHIFT = 5.5
CT = 2
CW = CT * P
NC = NT // CT


def in_ring(jp, ring):
    return ring - 1 if jp == NC - 1 else jp % (ring - 1)


def prior_use(jp, ring):
    same = [j for j in range(NC) if in_ring(j, ring) == in_ring(jp, ring)]
    n = same.index(jp)
    return same[n - 1] + 1 + (NC if n else 0)


def over_chunks(eng, chunk):
    with eng.Fori(0, NC // 2) as i:
        chunk(2 * i, 0, False)
        chunk(2 * i + 1, 1, False)
    chunk(NC - 1, 0, True)


def step_ahead(c, q, jp, d, last):
    if jp + d < NC:
        return c, q, jp + d
    return None if last else (c + 1, 1 - q, jp + d - NC)


def cosine_project(k, hT, w, WnT, WHhi, WHlo, rcol, r_dram):
    nc = k.nc
    s_w, s_hi, s_lo, s_sm, s_sq, s_rt, s_rT, s_out, s_row, s_T, s_tp, s_th, s_tl = (
        k.sem(f"s_p1_{n}") for n in ("w", "hi", "lo", "sm", "sq", "rt", "rT", "out", "row", "T", "tp", "th", "tl"))
    prods = hi_lo_products(KC)
    slots = [(m, c0, cn) for c0, cn in CHUNKS for m in range(KC)]
    NB = 3
    with ExitStack() as c:
        n2 = k.sb(c, "p1_n2", [P, NT], F32)
        junk = k.sb(c, "p1_junk", [P, 2, D], F32)
        sm = k.sb(c, "p1_sm", [P, 4, NT], F32)
        rT = k.sb(c, "p1_rT", [NT, P], F32)
        rrow = k.sb(c, "p1_rrow", [P, 2, CH], F32)
        T = k.sb(c, "p1_T", [P, 3, CH], F32)
        pw = k.ps(c, "p1_pw", [P, NB, CH])
        pt = k.ps(c, "p1_pt", [P, NB, CH])
        pr = k.ps(c, "p1_pr", [P, CH])
        block = c.enter_context(nc.Block())
        s_rr = [k.sem(f"s_p1_rr{i}") for i in range(2)]

        @block.sync
        def _(sp):
            sp.wait_ge(s_rT, 1)
            sp.dma_start(r_dram.rearrange("(t p) -> t p", p=P), rT[:]).then_inc(s_out, 16)
            sp.wait_ge(s_out, 16)
            for m, (c0, cn) in enumerate(CHUNKS):
                if m >= 2:
                    sp.wait_ge(s_T, 2 * (m - 1))
                sp.dma_start(rrow[:, m % 2, 0:cn], r_dram[c0:c0 + cn].unsqueeze(0).to_broadcast([P, cn])).then_inc(s_rr[m % 2], 16)

        @block.tensor
        def _(pe):
            for t in range(NT):
                if t >= NB:
                    pe.wait_ge(s_lo, t - NB + 1)
                    pe.wait_ge(s_sq, t - NB + 1)
                for n, (kc, a, b) in enumerate(prods):
                    last = nc.tensor.matmul(pw[:, t % NB, 0:D], hT[:, a, kc, t * P:(t + 1) * P], w[:, b, kc, :],
                                            start=(n == 0), stop=(n == len(prods) - 1))
                last.then_inc(s_w, 1)
            for j, (m, c0, cn) in enumerate(slots):
                if j == 2:
                    pe.wait_ge(s_sm, 8)
                    nc.tensor.transpose(pr[0:NT, 0:P], rcol[:, 0, :], k.ident[:]).then_inc(s_rt, 1)
                if j >= NB:
                    pe.wait_ge(s_T, j - NB + 1)
                for n, (kc, a, b) in enumerate(prods):
                    last = nc.tensor.matmul(pt[:, j % NB, 0:cn], w[:, a, kc, m * P:(m + 1) * P], hT[:, b, kc, c0:c0 + cn],
                                            start=(n == 0), stop=(n == len(prods) - 1))
                last.then_inc(s_tp, 1)

        @block.scalar
        def _(act):
            for t in range(NT):
                act.wait_ge(s_w, t + 1)
                nc.scalar.activation(WHhi[:, t, 0:D], pw[:, t % NB, 0:D], ACT.Copy, scale=WHSC / PSC).then_inc(s_hi, 1)
                if t >= 2:
                    act.wait_ge(s_sq, t - 1)
                nc.scalar.activation(junk[:, t % 2, :], pw[:, t % NB, 0:D], ACT.Square, scale=1.0 / PSC,
                                     accum_out=n2[:, t:t + 1]).then_inc(s_sq, 1)
            act.wait_ge(s_sm, 1)
            nc.scalar.activation(sm[:, 1, :], sm[:, 0, :], ACT.Sqrt).then_inc(s_sm, 1)
            act.wait_ge(s_rt, 1)
            nc.scalar.activation(rT[:], pr[0:NT, 0:P], ACT.Copy).then_inc(s_rT, 1)
            for j, (m, c0, cn) in enumerate(slots):
                act.wait_ge(s_T, j + 1)
                nc.scalar.activation(WnT[:, 0, m, c0:c0 + cn], T[:, j % 3, 0:cn], ACT.Copy).then_inc(s_th, 1)

        @block.vector
        def _(dve):
            nc.vector.memset(WHhi[:, :, D], WHSC)
            for t in range(NT):
                dve.wait_ge(s_sq, t + 1)
                nc.vector.scalar_tensor_tensor(WHlo[:, t, :], pw[:, t % NB, 0:D], WHSC / PSC, WHhi[:, t, 0:D],
                                               ALU.mult, ALU.subtract).then_inc(s_lo, 1)
            dve.wait_ge(s_sq, NT)
            nc.vector.tensor_scalar(sm[:, 0, :], n2[:], R_MIN * R_MIN, None, ALU.max).then_inc(s_sm, 1)
            dve.wait_ge(s_sm, 2)
            nc.vector.reciprocal(sm[:, 2, :], sm[:, 1, :]).then_inc(s_sm, 1)
            dve.wait_ge(s_sm, 3)
            nc.vector.tensor_tensor(sm[:, 3, :], sm[:, 2, :], sm[:, 0, :], ALU.mult).then_inc(s_sm, 1)
            dve.wait_ge(s_sm, 4)
            nc.vector.tensor_tensor(sm[:, 3, :], sm[:, 3, :], sm[:, 2, :], ALU.mult).then_inc(s_sm, 1)
            dve.wait_ge(s_sm, 5)
            nc.vector.tensor_scalar(sm[:, 3, :], sm[:, 3, :], -0.5, 1.5, ALU.mult, ALU.add).then_inc(s_sm, 1)
            dve.wait_ge(s_sm, 6)
            nc.vector.tensor_tensor(rcol[:, 0, :], sm[:, 3, :], sm[:, 2, :], ALU.mult).then_inc(s_sm, 1)
            dve.wait_ge(s_sm, 7)
            nc.vector.tensor_scalar(rcol[:, 1, :], rcol[:, 0, :], NORM_EPS, None, ALU.mult).then_inc(s_sm, 1)
            nc.vector.tensor_scalar(k.ident8[:].bitcast(U8), k.ident[:], float(FP8_ONE), None, ALU.mult)

            def low(j):
                m, c0, cn = slots[j]
                dve.wait_ge(s_th, j + 1)
                nc.vector.tensor_tensor(WnT[:, 1, m, c0:c0 + cn], T[:, j % 3, 0:cn], WnT[:, 0, m, c0:c0 + cn],
                                        ALU.subtract).then_inc(s_tl, 1)

            for j, (m, c0, cn) in enumerate(slots):
                dve.wait_ge(s_tp, j + 1)
                dve.wait_ge(s_rr[(j // 2) % 2], 16 * (j // 4 + 1))
                if j >= 3:
                    dve.wait_ge(s_tl, j - 2)
                nc.vector.scalar_tensor_tensor(T[:, j % 3, 0:cn], pt[:, j % NB, 0:cn], NSC / PSC, rrow[:, (j // 2) % 2, 0:cn],
                                               ALU.mult, ALU.mult).then_inc(s_T, 1)
                if j >= 1:
                    low(j - 1)
            low(len(slots) - 1)


def cosine_attend(k, WnT, WHhi, WHlo, rcol, r_dram, adjT_dram, spare):
    nc = k.nc
    s_q, s_ln, s_cf, s_dot, s_t, s_e, s_em, s_hi, s_lo, s_mm, s_rd, s_x, s_own = (
        k.sem(f"s_c1_{n}") for n in ("q", "ln", "cf", "dot", "t", "e", "em", "hi", "lo", "mm", "rd", "x", "own"))
    s_in = [k.sem(f"s_c1_in{i}") for i in range(2)]
    prods = hi_lo_products(KC)
    RD, RC, RT, RE, RM, RS = 4, 3, 3, 3, 3, 8
    EARLY = 3
    DOTS_AHEAD = 7
    FINISH_AT = 7
    W = 2 * CW
    with ExitStack() as c:
        Q1 = k.sb(c, "c1_Q", [P, NC, W], F32)
        Q = (spare.bitcast(F32).rearrange("p (j w) -> p j w", j=NC), Q1[:])
        CF = k.sb(c, "c1_CF", [P, RC, W], F32)
        T = k.sb(c, "c1_T", [P, RT, W], F32)
        E = k.sb(c, "c1_E", [P, RE, W], F32)
        EM = k.sb(c, "c1_EM", [P, RM, W], F32)
        rr = k.sb(c, "c1_rr", [P, 2, CW], F32)
        EH = k.sb(c, "c1_EH", [P, RS, W], F16)
        EL = k.sb(c, "c1_EL", [P, RS, W], F16)
        mv = k.sb(c, "c1_mv", [P, 2, 2, KC, CW], F16)
        ad = k.sb(c, "c1_ad", [P, 2, CT, NT, P], FP8)
        rden = k.sb(c, "c1_rden", [P, 2, CT], F32)
        shift = k.sb(c, "c1_shift", [P, 1], F32)
        pd = k.ps(c, "c1_pd", [P, RD, CH])
        pa = k.ps(c, "c1_pa", [P, 2, CT, CH])
        s_c = k.sem("s_c1_shift")
        block = c.enter_context(nc.Block())

        @block.sync
        def _(sp):
            def chunk(c, q, last):
                sp.wait_ge(s_em, (c + 1) * NC)
                sp.dma_start(mv[:, q].rearrange("p a k n -> p (a k) n"),
                             WnT[:, :, :, bass.ds(c * CW, CW)].rearrange("p a k n -> p (a k) n")).then_inc(s_in[q], 16)
                sp.dma_start(rr[:, q, :], r_dram[bass.ds(c * CW, CW)].unsqueeze(0).to_broadcast([P, CW])).then_inc(s_in[q], 16)
                sp.dma_start(ad[:, q].rearrange("p t j i -> p t (j i)").bitcast(U8),
                             adjT_dram[bass.ds(c * CT, CT)].rearrange("t p n -> p t n").bitcast(U8)).then_inc(s_in[q], 16)

            over_chunks(sp, chunk)

        def arrived(eng, c, q):
            eng.wait_ge(s_in[q], 24 * (c - q) + 48)

        @block.gpsimd
        def _(pool):
            nc.gpsimd.memset(shift[:], ESHIFT).then_inc(s_c, 1)

            def chunk(c, q, last):
                arrived(pool, c, q)
                pool.wait_ge(s_cf, (c + 1) * NC)
                k.settle(pool)
                for jp in range(NC):
                    for j in range(2):
                        ins = nc.gpsimd.tensor_scalar(Q[q][:, jp, j * CW:(j + 1) * CW], rr[:, q, :],
                                                      rcol[:, 1, 2 * jp + j:2 * jp + j + 1], 1.0, ALU.mult, ALU.add)
                    ins.then_inc(s_q, 1)

            over_chunks(pool, chunk)

        @block.scalar
        def _(act):
            act.sem_inc(s_cf, 2 * NC)
            act.wait_ge(s_c, 1)

            def factor(c, q, jp):
                first = isinstance(c, int) and c == 0
                if jp == 0 or first and jp == EARLY:
                    j0, j1 = (jp, NC if jp else EARLY) if first else (0, NC)
                    act.wait_ge(s_q, c * NC + j1)
                    nc.scalar.activation(Q[q][:, j0:j1], Q[q][:, j0:j1], ACT.Ln).then_inc(s_ln, 1)
                    act.wait_ge(s_ln, 1 if first and jp == 0 else c + 2)
                act.wait_ge(s_t, c * NC + prior_use(jp, RC))
                nc.scalar.activation(CF[:, in_ring(jp, RC), :], Q[q][:, jp, :], ACT.Exp, scale=-1.0).then_inc(s_cf, 1)

            def weight(c, q, jp):
                act.wait_ge(s_t, c * NC + jp + 1 + NC)
                act.wait_ge(s_em, (c + 1) * NC + prior_use(jp, RE))
                nc.scalar.activation(E[:, in_ring(jp, RE), :], T[:, in_ring(jp, RT), :], ACT.Exp, scale=1.0 / (NSC * NSC),
                                     bias=shift[:, 0:1]).then_inc(s_e, 1)

            def chunk(c, q, last):
                for jp in range(NC):
                    for d, what in ((2, factor), (1, weight)):
                        at_ = step_ahead(c, q, jp, d, last)
                        if at_:
                            what(*at_)

            factor(0, 0, 0)
            factor(0, 0, 1)
            weight(0, 0, 0)
            chunk(0, 0, False)
            with act.Fori(0, NC // 2 - 1) as i:
                chunk(2 * i + 1, 1, False)
                chunk(2 * i + 2, 0, False)
            chunk(NC - 2, 1, False)
            chunk(NC - 1, 0, True)

        @block.vector
        def _(dve):
            dve.sem_inc(s_t, NC)
            dve.sem_inc(s_em, 2 * NC)
            dve.sem_inc(s_x, 2)

            def sim(c, q, jp):
                dve.wait_ge(s_cf, (c + 2) * NC + jp + 1)
                dve.wait_ge(s_dot, c * NC + jp + 1)
                dve.wait_ge(s_e, c * NC + prior_use(jp, RT))
                nc.vector.tensor_tensor(T[:, in_ring(jp, RT), :], pd[:, in_ring(jp, RD), :], CF[:, in_ring(jp, RC), :], ALU.mult).then_inc(s_t, 1)

            def select(c, q, jp):
                dve.wait_ge(s_e, c * NC + jp + 1 + NC)
                dve.wait_ge(s_lo, c * NC + prior_use(jp, RM))
                k.settle(dve)
                nc.vector.tensor_tensor(EM[:, in_ring(jp, RM), :].rearrange("p (j t i) -> p j t i", j=2, t=CT),
                                        E[:, in_ring(jp, RE), :].rearrange("p (j t i) -> p j t i", j=2, t=CT),
                                        ad[:, q, :, 2 * jp:2 * jp + 2, :].rearrange("p t j i -> p j t i"), ALU.mult).then_inc(s_em, 1)

            def high(c, q, jp):
                dve.wait_ge(s_em, (c + 2) * NC + jp + 1)
                dve.wait_ge(s_mm, c * NC + prior_use(jp, RS))
                nc.vector.tensor_copy(EH[:, in_ring(jp, RS), :], EM[:, in_ring(jp, RM), :]).then_inc(s_hi, 1)

            def low(c, q, jp):
                dve.wait_ge(s_hi, c * NC + jp + 1)
                nc.vector.tensor_tensor(EL[:, in_ring(jp, RS), :], EM[:, in_ring(jp, RM), :], EH[:, in_ring(jp, RS), :],
                                        ALU.subtract).then_inc(s_lo, 1)

            def finish(c, q):
                dve.wait_ge(s_mm, (c + 1) * NC + NC)
                nc.vector.reciprocal(rden[:, q, :], pa[:, q, :, D]).then_inc(s_rd, 1)
                dve.wait_ge(s_rd, c + 1)
                for t in range(CT):
                    xs = k.X[:, bass.ds(c * CT + t, 1), :].rearrange("p t d -> p (t d)")
                    ins = nc.vector.scalar_tensor_tensor(xs, pa[:, q, t, 0:D], rden[:, q, t:t + 1], xs, ALU.mult, ALU.add)
                ins.then_inc(s_x, 1)

            def chunk(c, q, last, first=False):
                arrived(dve, c, q)
                for t in range(CT):
                    own = ad[:, q, t, bass.ds(c * CT + t, 1), :].rearrange("p t i -> p (t i)").bitcast(I32)
                    ins = nc.vector.tensor_tensor(own, own, k.ident8[:].bitcast(I32), ALU.bitwise_or)
                ins.then_inc(s_own, 1)
                dve.wait_ge(s_own, c + 1)
                for jp in range(NC):
                    if jp == FINISH_AT and not first:
                        finish(c - 1, 1 - q)
                    ahead = step_ahead(c, q, jp, 1, last)
                    if ahead:
                        sim(*ahead)
                    select(c, q, jp)
                    if jp > 0:
                        low(c, q, jp - 1)
                    elif not first:
                        low(c - 1, 1 - q, NC - 1)
                    high(c, q, jp)

            dve.sem_inc(s_lo, NC)
            sim(0, 0, 0)
            chunk(0, 0, False, True)
            with dve.Fori(0, NC // 2 - 1) as i:
                chunk(2 * i + 1, 1, False)
                chunk(2 * i + 2, 0, False)
            chunk(NC - 2, 1, False)
            chunk(NC - 1, 0, True)
            low(NC - 1, 0, NC - 1)
            finish(NC - 1, 0)

        @block.tensor
        def _(pe):
            pe.sem_inc(s_mm, NC)
            pe.sem_inc(s_e, NC)

            def dots(c, q, jp):
                if jp == 0:
                    arrived(pe, c, q)
                pe.wait_ge(s_t, c * NC + prior_use(jp, RD))
                for j in range(2):
                    jt = 2 * jp + j
                    for n, (kc, a, b) in enumerate(prods):
                        last = nc.tensor.matmul(pd[:, in_ring(jp, RD), j * CW:(j + 1) * CW], WnT[:, a, kc, jt * P:(jt + 1) * P],
                                                mv[:, q, b, kc, :], start=(n == 0), stop=(n == len(prods) - 1))
                last.then_inc(s_dot, 1)

            def sums(c, q, jp):
                if jp == 0:
                    pe.wait_ge(s_x, c + 1)
                pe.wait_ge(s_lo, c * NC + jp + 1 + NC)
                for j in range(2):
                    jt = 2 * jp + j
                    for t in range(CT):
                        col = j * CW + t * P
                        first, final = jt == 0, jt == NT - 1
                        hi, lo = EH[:, in_ring(jp, RS), col:col + P], EL[:, in_ring(jp, RS), col:col + P]
                        nc.tensor.matmul(pa[:, q, t, 0:D + 1], hi, WHhi[:, jt, :], start=first, stop=False, skip_group_check=True)
                        nc.tensor.matmul(pa[:, q, t, 0:D], hi, WHlo[:, jt, :], start=False, stop=False, skip_group_check=True)
                        last = nc.tensor.matmul(pa[:, q, t, 0:D + 1], lo, WHhi[:, jt, :], start=False, stop=final, skip_group_check=True)
                last.then_inc(s_mm, 1)

            def chunk(c, q, last):
                for jp in range(NC):
                    ahead = step_ahead(c, q, jp, DOTS_AHEAD, last)
                    if ahead:
                        dots(*ahead)
                    sums(c, q, jp)

            for jp in range(DOTS_AHEAD):
                dots(0, 0, jp)
            over_chunks(pe, chunk)


def layer1(k, ap, adjT_dram):
    with ExitStack() as c:
        r_dram = k.dram("r_dram", (NP,), F32)
        w = k.sb(c, "w_cos", [P, 2, KC, D], F16)
        rcol = k.sb(c, "rcol", [P, 2, NT], F32)
        k.ident8 = k.sb(c, "ident8", [P, P], FP8)
        hT = k.sb(c, "hT1", [P, 2 * KC * NP], F16)
        hTv = hT[:].rearrange("p (a k n) -> p a k n", a=2, k=KC)
        normalise(k, "n1", hTv, [(ap["L1_gnn_W"], lambda part: w[:, part, :, :])])
        WnT = k.sb(c, "WnT", [P, 2, KC, NP], F16)
        WHhi = k.sb(c, "WHhi", [P, NT, D + 1], F16)
        WHlo = k.sb(c, "WHlo", [P, NT, D], F16)
        cosine_project(k, hTv, w, WnT, WHhi, WHlo, rcol, r_dram)
        cosine_attend(k, WnT, WHhi, WHlo, rcol, r_dram, adjT_dram, hT[:])



KROWS = 3 * HD + 2
QKSC = 1024.0
SHARP = 2.0 ** 20
MASK = 2.0 ** 60
SCH = 4
SW = NP // SCH
SB = SW // 2
NB2 = NP // (2 * P)
TA = 8
RESULT_AT = 2


def hard_project(k, ap, hT, w, QT, KT, KS, Vhl, be, q_dram):
    nc = k.nc
    s_in, s_v, s_vh, s_vl, s_p, s_T, s_hi, s_lo, s_we, s_be, s_st = (
        k.sem(f"s_p2_{n}") for n in ("in", "v", "vh", "vl", "p", "T", "hi", "lo", "we", "be", "st"))
    prods = hi_lo_products(KC)
    NB = 3
    slots = [(s, m, c0, cn) for s in range(2) for m in range(KC) for c0, cn in CHUNKS]
    with ExitStack() as c:
        T = k.sb(c, "p2_T", [P, 3, CH], F32)
        we = k.sb(c, "p2_we", [P, 2], F32)
        beh = k.sb(c, "p2_beh", [KROWS, 1], F16)
        pv = k.ps(c, "p2_pv", [P, NB, CH])
        pt = k.ps(c, "p2_pt", [P, NB, CH])
        block = c.enter_context(nc.Block())
        B0 = 3 * HD

        @block.gpsimd
        def _(pool):
            nc.gpsimd.memset(KS[B0:KROWS], QKSC)

        @block.sync
        def _(sp):
            for q in range(P // HD):
                sp.dma_start(we[q * HD:(q + 1) * HD, 0:1], ap["L2_gnn_we"].rearrange("o d -> d o")).then_inc(s_in, 16)
            sp.dma_start(be[B0:KROWS, 0:1], ap["L2_gnn_be"].unsqueeze(0).to_broadcast([2, 1])).then_inc(s_in, 16)
            for s, src in ((0, KT), (1, QT)):
                for m in range(KC):
                    sp.wait_ge(s_lo, len(CHUNKS) * (s * KC + m + 1))
                    for q in range(4):
                        for r in range(3):
                            part = (0, 0, 1)[r] if s == 0 else (0, 1, 0)[r]
                            rows = slice(r * HD, (r + 1) * HD)
                            dst = KS[rows, 4 * m + q, :] if s == 0 else q_dram[rows, 4 * m + q, :]
                            sp.dma_start(dst, src[q * HD:(q + 1) * HD, part, m, :]).then_inc(s_st, 16)
            sp.wait_ge(s_st, 16 * 2 * HEADS * 3)

        @block.vector
        def _(dve):
            dve.wait_ge(s_in, 16 * (P // HD + 1))
            nc.vector.tensor_scalar(we[:, 1:2], we[:, 0:1], QKSC, None, ALU.mult).then_inc(s_we, 1)
            nc.vector.tensor_scalar(be[B0:KROWS, 1:2], be[B0:KROWS, 0:1], QKSC, None, ALU.mult).then_inc(s_be, 1)
            dve.wait_ge(s_be, 1)
            nc.vector.tensor_copy(beh[B0:KROWS], be[B0:KROWS, 1:2]).then_inc(s_be, 1)
            dve.wait_ge(s_be, 2)
            nc.vector.tensor_tensor(be[B0:KROWS, 2:3], beh[B0:KROWS], k.ident[B0:KROWS, B0 + 1:B0 + 2], ALU.mult).then_inc(s_be, 1)
            dve.wait_ge(s_be, 3)
            nc.vector.tensor_tensor(be[B0:KROWS, 3:4], be[B0:KROWS, 1:2], be[B0:KROWS, 2:3], ALU.subtract).then_inc(s_be, 1)
            dve.wait_ge(s_we, 1)

            def low(j):
                s, m, c0, cn = slots[j]
                dst = (KT, QT)[s]
                dve.wait_ge(s_hi, j + 1)
                nc.vector.tensor_tensor(dst[:, 1, m, c0:c0 + cn], T[:, j % 3, 0:cn], dst[:, 0, m, c0:c0 + cn],
                                        ALU.subtract).then_inc(s_lo, 1)

            for j, (s, m, c0, cn) in enumerate(slots):
                dve.wait_ge(s_p, j + 1)
                if j >= 3:
                    dve.wait_ge(s_lo, j - 2)
                if s == 0:
                    nc.vector.tensor_scalar(T[:, j % 3, 0:cn], pt[:, j % NB, 0:cn], HD ** -0.5 * QKSC / PSC, we[:, 1:2],
                                            ALU.mult, ALU.add).then_inc(s_T, 1)
                else:
                    nc.vector.tensor_scalar(T[:, j % 3, 0:cn], pt[:, j % NB, 0:cn], QKSC / PSC, None, ALU.mult).then_inc(s_T, 1)
                if j >= 1:
                    low(j - 1)
            low(len(slots) - 1)
            for t in range(NT):
                b, e = t // 2, t % 2
                dve.wait_ge(s_vh, t + 1)
                nc.vector.scalar_tensor_tensor(Vhl[:, b, e, :, HD:2 * HD], pv[:, t % NB, 0:D].rearrange("p (h d) -> p h d", d=HD),
                                               QKSC / HEADS / PSC, Vhl[:, b, e, :, 0:HD], ALU.mult, ALU.subtract).then_inc(s_vl, 1)

        @block.scalar
        def _(act):
            for j, (s, m, c0, cn) in enumerate(slots):
                act.wait_ge(s_T, j + 1)
                nc.scalar.activation((KT, QT)[s][:, 0, m, c0:c0 + cn], T[:, j % 3, 0:cn], ACT.Copy).then_inc(s_hi, 1)
            for t in range(NT):
                act.wait_ge(s_v, t + 1)
                nc.scalar.activation(Vhl[:, t // 2, t % 2, :, 0:HD], pv[:, t % NB, 0:D].rearrange("p (h d) -> p h d", d=HD),
                                     ACT.Copy, scale=QKSC / HEADS / PSC).then_inc(s_vh, 1)

        @block.tensor
        def _(pe):
            for j, (s, m, c0, cn) in enumerate(slots):
                if j >= NB:
                    pe.wait_ge(s_T, j - NB + 1)
                for n, (kc, a, b) in enumerate(prods):
                    last = nc.tensor.matmul(pt[:, j % NB, 0:cn], w[:, 1 - s, a, kc, m * P:(m + 1) * P], hT[:, b, kc, c0:c0 + cn],
                                            start=(n == 0), stop=(n == len(prods) - 1))
                last.then_inc(s_p, 1)
            for t in range(NT):
                blk, e = t // 2, t % 2
                if t >= NB:
                    pe.wait_ge(s_vl, t - NB + 1)
                for n, (kc, a, b) in enumerate(prods):
                    nodes = hT[:, a, kc, blk * 2 * P:(blk + 1) * 2 * P].rearrange("p (n e) -> p n e", e=2)[:, :, e]
                    last = nc.tensor.matmul(pv[:, t % NB, 0:D], nodes, w[:, 2, b, kc, :], start=(n == 0), stop=(n == len(prods) - 1))
                last.then_inc(s_v, 1)


def over_tiles(eng, tile):
    with eng.Fori(0, NT // 2 - 1) as i:
        tile(2 * i, 0, False)
        tile(2 * i + 1, 1, False)
    tile(NT - 2, 0, False)
    tile(NT - 1, 1, True)


def head_ahead(i, q, h, d, last):
    if h + d < HEADS:
        return i, q, h + d
    return None if last else (i + 1, 1 - q, h + d - HEADS)


def hard_attend(k, adj_dram, KS, Vhl, be, q_dram):
    nc = k.nc
    s_pad, s_nb, s_sc, s_tt, s_mx, s_hA, s_hB, s_trA, s_trB, s_evA, s_evB, s_av, s_x, s_r, s_be = (
        k.sem(f"s_h2_{n}") for n in ("pad", "nb", "sc", "tt", "mx", "hA", "hB", "trA", "trB", "evA", "evB", "av", "x", "r", "be"))
    s_rows = [k.sem(f"s_h2_rows{i}") for i in range(2)]
    s_q = [k.sem(f"s_h2_q{i}") for i in range(2)]
    with ExitStack() as c:
        rows = k.sb(c, "h2_rows", [P, 2, NP], I32)
        off = k.sb(c, "h2_off", [P, 2, NP], F32)
        S = k.sb(c, "h2_S", [P, 2, NP], F32)
        H = k.sb(c, "h2_H", [P, 2 * NP], FP8)
        HT = k.sb(c, "h2_HT", [P, 2 * NP], FP8)
        QS = k.sb(c, "h2_QS", [KROWS, 2, HEADS, P], F16)
        mx = k.sb(c, "h2_mx", [P, 2, SCH], F32)
        nmx = k.sb(c, "h2_nmx", [P, 2], F32)
        ps = k.ps(c, "h2_ps", [P, 2, 2, CH])
        pT = k.ps(c, "h2_pT", [P, 2, 1024], BF16)
        po = k.ps(c, "h2_po", [P, 2, CH])
        block = c.enter_context(nc.Block())
        g_of = lambda i, h: i * HEADS + h

        @block.sync
        def _(sp):
            def load(i, s):
                sp.wait_ge(s_nb, i + 1)
                k.settle(sp)
                sp.dma_start(rows[:, s, 0:N], adj_dram[bass.ds(i * P, P), :]).then_inc(s_rows[s], 16)
                load_q(i, s)

            def load_q(i, s):
                sp.wait_ge(s_x, i + 1)
                k.settle(sp)
                sp.dma_start(QS[0:3 * HD, s], q_dram[:, :, bass.ds(i * P, P)]).then_inc(s_q[s], 16)

            sp.wait_ge(s_pad, 1)
            with sp.Fori(0, NT // 2 - 1) as i:
                load(2 * i, 0)
                load(2 * i + 1, 1)
            load(NT - 2, 0)
            sp.wait_ge(s_pad, 2)
            sp.dma_start(rows[0:LAST, 1, 0:N], adj_dram[(NT - 1) * P:N, :]).then_inc(s_rows[1], 16)
            load_q(NT - 1, 1)

        @block.gpsimd
        def _(pool):
            nc.gpsimd.memset(rows[:, :, N:NP], 0).then_inc(s_pad, 1)
            pool.sem_inc(s_nb, 2)

            def offsets(i, s):
                pool.wait_ge(s_rows[s], 8 * (i - s) + 16)
                pool.wait_ge(s_x, i + 1)
                k.settle(pool)
                nc.gpsimd.tensor_scalar(off[:, s, :], rows[:, s, :], -1.0, MASK, ALU.add, ALU.mult).then_inc(s_nb, 1)

            pool.wait_ge(s_pad, 1)
            with pool.Fori(0, NT // 2 - 1) as i:
                offsets(2 * i, 0)
                offsets(2 * i + 1, 1)
            pool.wait_ge(s_nb, NT)
            nc.gpsimd.memset(rows[96:P, 1, :], 0).then_inc(s_pad, 1)
            pool.wait_ge(s_pad, 2)
            offsets(NT - 2, 0)
            offsets(NT - 1, 1)

        @block.tensor
        def _(pe):
            pe.sem_inc(s_trA, 2)
            pe.sem_inc(s_trB, 2)
            pe.sem_inc(s_av, 2)

            def scores(i, q, h, chunks):
                for ch in chunks:
                    if h == 0 and ch == 0:
                        pe.wait_ge(s_be, 1)
                        pe.wait_ge(s_q[q], 8 * (i - q) + 16)
                    pe.wait_ge(s_tt, g_of(i, h) * SCH + ch + 1)
                    for b in range(2):
                        c0 = ch * SW + b * SB
                        last = nc.tensor.matmul(ps[:, ch % 2, b, 0:SB], QS[:, q, h, :], KS[:, h, c0:c0 + SB], start=True, stop=True)
                    last.then_inc(s_sc, 1)

            def transposes(i, q, h):
                g = g_of(i, h)
                for part, (b0, b1), written, free, done in ((0, (0, TA), s_hA, s_evA, s_trA), (1, (TA, NB2), s_hB, s_evB, s_trB)):
                    pe.wait_ge(written, g + 3)
                    pe.wait_ge(free, g + 1)
                    for b in range(b0, b1):
                        src = H[:, (h % 2) * NP + b * 2 * P:(h % 2) * NP + (b + 1) * 2 * P].bitcast(BF16)
                        last = nc.tensor.transpose(pT[:, part, (b - b0) * P:(b - b0 + 1) * P], src, k.ident16[:])
                    last.then_inc(done, 1)

            def sums(i, q, h):
                g = g_of(i, h)
                if h == 0:
                    pe.wait_ge(s_x, i + 1)
                pe.wait_ge(s_evA, g + 2)
                pe.wait_ge(s_evB, g + 2)
                k.settle(pe)
                wt = HT[:, (h % 2) * NP:(h % 2 + 1) * NP].rearrange("p (b i e) -> p b i e", b=NB2, e=2)
                for b in range(NB2):
                    for e in range(2):
                        last = nc.tensor.matmul(po[:, q, h * 2 * HD:(h + 1) * 2 * HD], wt[:, b, :, e], Vhl[:, b, e, h, :],
                                                start=(b == 0 and e == 0), stop=(b == NB2 - 1 and e == 1), skip_group_check=True)
                last.then_inc(s_av, 1)

            def steps(i, q, h, last):
                s1, s2, s3 = (head_ahead(i, q, h, d, last) for d in (1, 2, 3))
                if s2:
                    scores(*s2, range(1, 3))
                sums(i, q, h)
                if s2:
                    scores(*s2, range(3, SCH))
                if s3:
                    scores(*s3, range(1))
                if s1:
                    transposes(*s1)

            scores(0, 0, 0, range(SCH))
            scores(0, 0, 1, range(SCH))
            scores(0, 0, 2, range(1))
            transposes(0, 0, 0)
            over_tiles(pe, lambda i, q, last: [steps(i, q, h, last) for h in range(HEADS)])

        @block.scalar
        def _(act):
            act.sem_inc(s_hA, 2)
            act.sem_inc(s_hB, 2)
            act.sem_inc(s_evA, 1)

            def weights(i, q, h):
                g = g_of(i, h)
                act.wait_ge(s_mx, g + 1)
                for (c0, c1), free, done in (((0, TA * 2 * P), s_trA, s_hA), ((TA * 2 * P, NP), s_trB, s_hB)):
                    act.wait_ge(free, g + 1)
                    k.settle(act)
                    nc.scalar.activation(H[:, (h % 2) * NP + c0:(h % 2) * NP + c1], S[:, h % 2, c0:c1], ACT.Exp,
                                         bias=nmx[:, h % 2:h % 2 + 1], scale=1.0, saturate=False).then_inc(done, 1)

            def evacuate(i, q, h):
                g = g_of(i, h)
                act.wait_ge(s_trA, g + 3)
                act.wait_ge(s_av, g + 1)
                dst = HT[:, (h % 2) * NP:(h % 2) * NP + TA * 2 * P]
                nc.scalar.activation(dst.bitcast(U16), pT[:, 0, :].bitcast(U16), ACT.Copy).then_inc(s_evA, 1)

            def steps(i, q, h, last):
                weights(i, q, h)
                evacuate(i, q, h)

            over_tiles(act, lambda i, q, last: [steps(i, q, h, last) for h in range(HEADS)])

        @block.vector
        def _(dve):
            nc.vector.tensor_copy(QS[3 * HD:KROWS].rearrange("p s h n -> p (s h n)"),
                                  be[3 * HD:KROWS, 3:4].to_broadcast([2, 2 * HEADS * P])).then_inc(s_be, 1)
            dve.sem_inc(s_tt, 2)
            dve.sem_inc(s_evB, 1)
            dve.sem_inc(s_x, 2)

            def maxima(i, q, h, chunks):
                g = g_of(i, h)
                for ch in chunks:
                    if h == 0 and ch == 0:
                        dve.wait_ge(s_nb, i + 3)
                    if ch == 0:
                        dve.wait_ge(s_hA, g + 1)
                    if ch == 2:
                        dve.wait_ge(s_hB, g + 1)
                    dve.wait_ge(s_sc, g * SCH + ch + 1)
                    k.settle(dve)
                    two = lambda x: x.rearrange("p (b n) -> p b n", b=2)
                    nc.vector.tensor_tensor_reduce(out=two(S[:, h % 2, ch * SW:(ch + 1) * SW]), in0=ps[:, ch % 2, :, 0:SB],
                                                   in1=two(off[:, q, ch * SW:(ch + 1) * SW]), scale=SHARP, scalar=-3e38,
                                                   op0=ALU.add, op1=ALU.max, accum_out=mx[:, h % 2, ch:ch + 1]).then_inc(s_tt, 1)

            def maximum(i, q, h):
                dve.wait_ge(s_tt, (g_of(i, h) + 1) * SCH + 2)
                nc.vector.tensor_reduce(nmx[:, h % 2:h % 2 + 1], mx[:, h % 2, :], AX.X, ALU.max, negate=True).then_inc(s_mx, 1)

            def evacuate(i, q, h):
                g = g_of(i, h)
                dve.wait_ge(s_trB, g + 3)
                dve.wait_ge(s_av, g + 1)
                dst = HT[:, (h % 2) * NP + TA * 2 * P:(h % 2 + 1) * NP]
                nc.vector.tensor_scalar(dst.bitcast(I32), pT[:, 1, 0:(NB2 - TA) * P].bitcast(I32), 0, None,
                                        ALU.bitwise_or).then_inc(s_evB, 1)

            def result(i, q):
                dve.wait_ge(s_av, i * HEADS + HEADS + 2)
                xs = k.X[:, bass.ds(i, 1), :].rearrange("p t (h d) -> p (t h) d", d=HD)
                both = po[:, q, :].rearrange("p (h a d) -> p h a d", a=2, d=HD)
                nc.vector.scalar_tensor_tensor(xs, both[:, :, 0, :], 1.0 / QKSC, xs, ALU.mult, ALU.add).then_inc(s_r, 1)
                dve.wait_ge(s_r, i + 1)
                nc.vector.scalar_tensor_tensor(xs, both[:, :, 1, :], 1.0 / QKSC, xs, ALU.mult, ALU.add).then_inc(s_x, 1)

            def steps(i, q, h, last, first=False):
                s1, s2 = (head_ahead(i, q, h, d, last) for d in (1, 2))
                if s1:
                    maxima(*s1, range(1, SCH))
                if s2:
                    maxima(*s2, range(1))
                if s1:
                    maximum(*s1)
                evacuate(i, q, h)
                if h == RESULT_AT and not first:
                    result(i - 1, 1 - q)

            maxima(0, 0, 0, range(SCH))
            maxima(0, 0, 1, range(1))
            maximum(0, 0, 0)
            for h in range(HEADS):
                steps(0, 0, h, False, True)
            with dve.Fori(0, NT // 2 - 1) as i:
                for h in range(HEADS):
                    steps(2 * i + 1, 1, h, False)
                for h in range(HEADS):
                    steps(2 * i + 2, 0, h, False)
            for h in range(HEADS):
                steps(NT - 1, 1, h, True)
            result(NT - 1, 1)


def layer2(k, ap):
    with ExitStack() as c:
        q_dram = k.dram("q_dram", (3 * HD, HEADS, NP), F16)
        KS = k.sb(c, "KS", [KROWS, HEADS, NP], F16)
        be = k.sb(c, "be", [KROWS, 4], F32)
        Vhl = k.sb(c, "Vhl", [P, NB2, 2, HEADS, 2 * HD], F16)
        with ExitStack() as c1:
            w = k.sb(c1, "w_hard", [P, 3, 2, KC, D], F16)
            hT = k.sb(c1, "hT2", [P, 2, KC, NP], F16)
            part_of = lambda i: lambda part: w[:, i, part, :, :]
            normalise(k, "n2", hT, [(ap[f"L2_gnn_W{n}"], part_of(i)) for i, n in enumerate("QKV")])
            QT = k.sb(c1, "QT", [P, 2, KC, NP], F16)
            KT = k.sb(c1, "KT", [P, 2, KC, NP], F16)
            hard_project(k, ap, hT, w, QT, KT, KS, Vhl, be, q_dram)
        hard_attend(k, ap["adj"], KS, Vhl, be, q_dram)




def mean_weights(k, c, ap, m, bias, ideg_dram):
    nc = k.nc
    s_in, s_tr, s_cp, s_bb, s_mm, s_hi, s_deg, s_rT, s_out, s_b = (
        k.sem(f"s_w3_{n}") for n in ("in", "tr", "cp", "bb", "mm", "hi", "deg", "rT", "out", "b"))
    raw = k.sb(c, "w3_raw", [P, 2, KC, D], F32)
    wt = k.sb(c, "w3_t", [P, 2, KC, D], F32)
    comb = k.sb(c, "w3_comb", [P, 2, KC, D], F32)
    bcol = k.sb(c, "w3_bcol", [P, 2, KC], F32)
    bb = k.sb(c, "w3_bb", [P, 2, KC, P], F32)
    bc = k.sb(c, "w3_bc", [P, D], F32)
    dg = k.sb(c, "w3_deg", [P, 2, NT], F32)
    dT = k.sb(c, "w3_degT", [NT, P], F32)
    pt = k.ps(c, "w3_pt", [P, 2, CH])
    pm = k.ps(c, "w3_pm", [P, 2, CH])
    pd, pb = pm[:, 1, :], pt[:, 0, :]
    srcs = [(ap["L3_gnn_W_self"], ap["L3_gnn_b_self"]), (ap["L3_gnn_W_nb"], ap["L3_gnn_b_nb"])]
    LOADS = 2 * (1 + KC) + 2

    def on_sync(sp):
        for s, (w, b) in enumerate(srcs):
            sp.dma_start(raw[:, s], w.rearrange("(k p) c -> p k c", p=P)).then_inc(s_in, 16)
            for kc in range(KC):
                sp.dma_start(bcol[:, s, kc:kc + 1], b[kc * P:(kc + 1) * P].rearrange("(p o) -> p o", o=1)).then_inc(s_in, 16)
        sp.dma_start(comb[:].rearrange("p s k c -> p (s k) c"),
                     ap["L3_gnn_W_comb"].rearrange("(k p) c -> p k c", p=P)).then_inc(s_in, 16)
        sp.dma_start(bc[:], ap["L3_gnn_b_comb"].unsqueeze(0).to_broadcast([P, D])).then_inc(s_in, 16)
        sp.wait_ge(s_rT, 1)
        sp.dma_start(ideg_dram.rearrange("(t p) -> t p", p=P), dT[:]).then_inc(s_out, 16)
        sp.wait_ge(s_out, 16)

    def vector_first(dve):
        nc.vector.tensor_tensor(dg[:, 1, :], k.deg[:, 0, :], k.deg[:, 1, :], ALU.add).then_inc(s_deg, 1)
        dve.wait_ge(s_deg, 1)
        nc.vector.tensor_scalar(dg[:, 0, :], dg[:, 1, :], 1.0, None, ALU.max).then_inc(s_deg, 1)
        dve.wait_ge(s_deg, 2)
        nc.vector.reciprocal(dg[:, 1, :], dg[:, 0, :]).then_inc(s_deg, 1)

    def vector_mid(dve):
        dve.wait_ge(s_in, 16 * LOADS)
        nc.vector.tensor_copy(bb[:], bcol[:].unsqueeze(3).to_broadcast([P, 2, KC, P])).then_inc(s_bb, 1)

    def vector_last(dve):
        for s in range(2):
            dve.wait_ge(s_hi, s + 1)
            nc.vector.scalar_tensor_tensor(m[:, 1, s], pm[:, s, :].rearrange("p (k n) -> p k n", k=KC), WSC, m[:, 0, s],
                                           ALU.mult, ALU.subtract)
        dve.wait_ge(s_b, 1)
        nc.vector.tensor_tensor(bias[:], pb[:, 0:D], bc[:], ALU.add)

    def tensor_first(pe):
        pe.wait_ge(s_deg, 3)
        nc.tensor.transpose(pd[0:NT, 0:P], dg[:, 1, :], k.ident[:]).then_inc(s_tr, 1)
        pe.wait_ge(s_in, 16 * LOADS)
        for s in range(2):
            for kc in range(KC):
                for kn in range(KC):
                    last = nc.tensor.transpose(pt[:, s, kc * D + kn * P:kc * D + (kn + 1) * P],
                                               raw[:, s, kn, kc * P:(kc + 1) * P], k.ident[:])
            last.then_inc(s_tr, 1)
        for s in range(2):
            pe.wait_ge(s_cp, s + 1)
            if s == 1:
                pe.wait_ge(s_rT, 1)
            for kn in range(KC):
                for kc in range(KC):
                    last = nc.tensor.matmul(pm[:, s, kn * D:(kn + 1) * D], wt[:, s, kc, kn * P:(kn + 1) * P], comb[:, s, kc, :],
                                            start=(kc == 0), stop=(kc == KC - 1))
            last.then_inc(s_mm, 1)

    def tensor_last(pe):
        pe.wait_ge(s_bb, 1)
        pe.wait_ge(s_cp, 1)
        for n, (s, kc) in enumerate([(s, kc) for s in range(2) for kc in range(KC)]):
            last = nc.tensor.matmul(pb[:, 0:D], bb[:, s, kc, :], comb[:, s, kc, :], start=(n == 0), stop=(n == 2 * KC - 1))
        last.then_inc(s_b, 1)

    def scalar_first(act):
        act.wait_ge(s_tr, 1)
        nc.scalar.activation(dT[:], pd[0:NT, 0:P], ACT.Copy).then_inc(s_rT, 1)

    def scalar_mid(act):
        for s in range(2):
            act.wait_ge(s_tr, s + 2)
            nc.scalar.activation(wt[:, s].rearrange("p k n -> p (k n)"), pt[:, s, :], ACT.Copy).then_inc(s_cp, 1)

    def scalar_last(act):
        for s in range(2):
            act.wait_ge(s_mm, s + 1)
            nc.scalar.activation(m[:, 0, s], pm[:, s, :].rearrange("p (k n) -> p k n", k=KC), ACT.Copy, scale=WSC).then_inc(s_hi, 1)

    return {"sync": on_sync, "vector_first": vector_first, "vector_mid": vector_mid, "vector_last": vector_last,
            "scalar_first": scalar_first, "scalar_mid": scalar_mid, "scalar_last": scalar_last,
            "tensor_first": tensor_first, "tensor_last": tensor_last}


def mean_aggregate(k, hT, Hn, m, bias, ideg_dram, adjT_dram, out_dram):
    nc = k.nc
    s_agg, s_T, s_hi, s_lo, s_mm, s_t, s_x, s_ideg, s_st = (
        k.sem(f"s_m3_{n}") for n in ("agg", "T", "hi", "lo", "mm", "t", "x", "ideg", "st"))
    s_in = [k.sem(f"s_m3_in{i}") for i in range(2)]
    prods = hi_lo_products(KC)
    with ExitStack() as c:
        ad = k.sb(c, "m3_ad", [P, 2, CT, NT, P], FP8)
        idr = k.sb(c, "m3_ideg", [P, NP], F32)
        T = k.sb(c, "m3_T", [P, 2, KC, CW], F32)
        aT = k.sb(c, "m3_aT", [P, 2, 2, KC, CW], F16)
        R = k.sb(c, "m3_R", [P, 2, CT, D], F32)
        pa = k.ps(c, "m3_pa", [P, 2, KC, CH])
        po = k.ps(c, "m3_po", [P, 2, CT, D])
        block = c.enter_context(nc.Block())

        @block.sync
        def _(sp):
            def load(c, q):
                sp.wait_ge(s_agg, c + 1)
                sp.dma_start(ad[:, q].rearrange("p t j i -> p t (j i)").bitcast(U8),
                             adjT_dram[bass.ds(c * CT, CT)].rearrange("t p n -> p t n").bitcast(U8)).then_inc(s_in[q], 16)

            def store(c):
                sp.wait_ge(s_x, c + 1)
                sp.dma_start(out_dram[bass.ds(c * CW, CW), :].rearrange("(t p) d -> p t d", p=P),
                             k.X[:, bass.ds(c * CT, CT), :]).then_inc(s_st, 16)

            load(0, 0)
            sp.dma_start(idr[:], ideg_dram.unsqueeze(0).to_broadcast([P, NP])).then_inc(s_ideg, 16)
            load(1, 1)
            with sp.Fori(0, NC // 2 - 1) as i:
                for q in range(2):
                    load(2 * i + 2 + q, q)
                    store(2 * i + q)
            load(NC - 1, 0)
            store(NC - 3)
            store(NC - 2)
            sp.wait_ge(s_x, NC)
            sp.dma_start(out_dram[(NT - 2) * P:(NT - 1) * P, :], k.X[:, NT - 2, :]).then_inc(s_st, 16)
            sp.dma_start(out_dram[(NT - 1) * P:N, :], k.X[0:LAST, NT - 1, :]).then_inc(s_st, 16)
            sp.wait_ge(s_st, 16 * (NC + 1))

        @block.tensor
        def _(pe):
            pe.sem_inc(s_agg, 2)
            pe.sem_inc(s_mm, 2)

            def sums(c, q):
                pe.wait_ge(s_in[q], 8 * (c - q) + 16)
                pe.wait_ge(s_T, c + 1)
                k.settle(pe)
                for kc in range(KC):
                    for jt in range(NT):
                        for a in range(2):
                            last = nc.tensor.matmul(pa[:, q, kc, 0:CW].rearrange("p (t i) -> p t i", t=CT),
                                                    Hn[:, a, jt, kc * P:(kc + 1) * P], ad[:, q, :, jt, :],
                                                    start=(jt == 0 and a == 0), stop=(jt == NT - 1 and a == 1))
                last.then_inc(s_agg, 1)

            def linear(c, q):
                pe.wait_ge(s_lo, c + 3)
                pe.wait_ge(s_t, c + 1)
                for t in range(CT):
                    for n, (kc, a, b) in enumerate(prods):
                        nc.tensor.matmul(po[:, q, t, :], hT[:, a, kc, bass.ds((c * CT + t) * P, P)], m[:, b, 0, kc, :],
                                         start=(n == 0), stop=False)
                    for n, (kc, a, b) in enumerate(prods):
                        last = nc.tensor.matmul(po[:, q, t, :], aT[:, q, a, kc, t * P:(t + 1) * P], m[:, b, 1, kc, :],
                                                start=False, stop=(n == len(prods) - 1))
                last.then_inc(s_mm, 1)

            sums(0, 0)
            with pe.Fori(0, NC // 2) as i:
                sums(2 * i + 1, 1)
                linear(2 * i, 0)
                sums(2 * i + 2, 0)
                linear(2 * i + 1, 1)
            linear(NC - 1, 0)

        @block.scalar
        def _(act):
            def chunk(c, q, last):
                act.wait_ge(s_T, c + 3)
                act.wait_ge(s_mm, c + 1)
                nc.scalar.activation(aT[:, q, 0], T[:, q], ACT.Copy).then_inc(s_hi, 1)

            over_chunks(act, chunk)

        @block.vector
        def _(dve):
            dve.sem_inc(s_T, 2)
            dve.sem_inc(s_t, 2)
            dve.sem_inc(s_lo, 2)
            dve.wait_ge(s_ideg, 16)

            def means(c, q):
                dve.wait_ge(s_agg, c + 3)
                dve.wait_ge(s_lo, c + 1)
                nc.vector.tensor_tensor(T[:, q], pa[:, q, :, 0:CW],
                                        idr[:, bass.ds(c * CW, CW)].unsqueeze(1).to_broadcast([P, KC, CW]), ALU.mult).then_inc(s_T, 1)
                dve.wait_ge(s_hi, c + 1)
                nc.vector.tensor_tensor(aT[:, q, 1], T[:, q], aT[:, q, 0], ALU.subtract).then_inc(s_lo, 1)

            def result(c, q):
                dve.wait_ge(s_mm, c + 3)
                for t in range(CT):
                    last = nc.vector.scalar_tensor_tensor(R[:, q, t, :], po[:, q, t, :], 1.0 / PSC, bias[:], ALU.mult, ALU.add)
                last.then_inc(s_t, 1)
                dve.wait_ge(s_t, c + 3)
                xs = k.X[:, bass.ds(c * CT, CT), :]
                nc.vector.scalar_tensor_tensor(xs, R[:, q], 0.0, xs, ALU.max, ALU.add).then_inc(s_x, 1)

            means(0, 0)
            with dve.Fori(0, NC // 2) as i:
                means(2 * i + 1, 1)
                result(2 * i, 0)
                means(2 * i + 2, 0)
                result(2 * i + 1, 1)
            result(NC - 1, 0)


def layer3(k, ap, adjT_dram, out_dram):
    with ExitStack() as c:
        ideg_dram = k.dram("ideg_dram", (NP,), F32)
        hT = k.sb(c, "hT3", [P, 2, KC, NP], F16)
        Hn = k.sb(c, "Hn", [P, 2, NT, D], F16)
        m = k.sb(c, "m3_w", [P, 2, 2, KC, D], F16)
        bias = k.sb(c, "m3_bias", [P, D], F32)
        normalise(k, "n3", hT, [], Hn, also=lambda c1: mean_weights(k, c1, ap, m, bias, ideg_dram))
        mean_aggregate(k, hT, Hn, m, bias, ideg_dram, adjT_dram, out_dram)



def build(nc, ap, out_dram):
    with ExitStack() as ctx:
        k = Kernel(nc)
        k.s_adjT_out = nc.alloc_semaphore(name="s_adjT_out")
        k.X = k.sb(ctx, "X", [P, NT, D], F32)
        k.ident = k.sb(ctx, "ident", [P, P], F32)
        k.ident16 = k.sb(ctx, "ident16", [P, P], BF16)
        k.corner16 = k.sb(ctx, "corner16", [P, P], BF16)
        k.deg = k.sb(ctx, "deg", [P, 2, NT], F32)
        adjT_dram = k.dram("adjT_dram", (NT, P, NP), FP8)
        k.attn_cols = k.sb(ctx, "attn_cols", [P, KC, 2 * HEADS], F32)
        setup_constants(k, ap["x"], ap["L0_gnn_attn_w"])
        with ExitStack() as c:
            k.adjT = k.sb(c, "adjT", [P, NT, NT, P], FP8)
            transpose_adjacency(k, ap["adj"])
            layer0(k, ap, adjT_dram)
        k.end_layer()
        layer1(k, ap, adjT_dram)
        k.end_layer()
        layer2(k, ap)
        k.end_layer()
        layer3(k, ap, adjT_dram, out_dram)


INPUTS = ["x", "adj", "L0_gnn_W_lin", "L0_gnn_attn_w", "L1_gnn_W", "L2_gnn_WQ", "L2_gnn_WK", "L2_gnn_WV", "L2_gnn_we",
          "L2_gnn_be", "L3_gnn_W_self", "L3_gnn_b_self", "L3_gnn_W_nb", "L3_gnn_b_nb", "L3_gnn_W_comb", "L3_gnn_b_comb"]


def kernel(**inputs):
    import numpy as np
    import concourse.bacc as bacc
    from concourse.bass_utils import run_bass_kernel_spmd

    nc = bacc.Bacc("TRN2", target_bir_lowering=False, num_devices=1)
    arrays, ap = {}, {}
    for name in INPUTS:
        a = np.ascontiguousarray(inputs[name])
        arrays[f"in_{name}_dram"] = a
        ap[name] = nc.dram_tensor(f"in_{name}_dram", a.shape, mybir.dt.from_np(a.dtype), kind="ExternalInput").ap()
    out = nc.dram_tensor("out_dram", (N, D), F32, kind="ExternalOutput").ap()
    build(nc, ap, out)
    r = run_bass_kernel_spmd(nc, [arrays], core_ids=[0])
    return r.results[0]["out_dram"]
```
